# Optimizing a Trainium2 kernel written in Bass

```python
import numpy as np
import jax
import jax.numpy as jnp

def _softmax(x, axis=-1):
    return jax.nn.softmax(x, axis=axis)

def _gelu(x):
    return jax.nn.gelu(x, approximate=True)

def _silu(x):
    return jax.nn.silu(x)

def _sigmoid(x):
    return jax.nn.sigmoid(x)

def _layernorm(x, axis=-1, eps=1e-05):
    m = jnp.mean(x, axis=axis, keepdims=True)
    v = jnp.var(x, axis=axis, keepdims=True)
    return (x - m) / jnp.sqrt(v + eps)

def _scatter_add(tgt, idx, src, axis=0):
    return tgt.at[idx].add(src)

def _segment_sum(src, seg, n):
    return jax.ops.segment_sum(src, seg, n)
kernel_name = 'mk_hybrid_d1_jaxref_r8_9c24ad'

def setup_inputs(seed: int=0):
    np.random.seed(seed)
    _w = jnp.asarray

    def _L0_attn_a_setup():
        import jax, jax.numpy as jnp
        import numpy as np
        D_MODEL = 128
        N_HEADS = 16
        D_K = D_MODEL // N_HEADS
        THETA = 10000.0
        MAX_SEQ = 256

        def _trunc_normal(key, shape, std):
            return jnp.clip(jax.random.normal(key, shape) * std, -3 * std, 3 * std).astype(jnp.float32)

        def _rope(x, positions):
            d = x.shape[-1]
            inv_freq = THETA ** (-2.0 * jnp.arange(0, d // 2, dtype=jnp.float32) / d)
            angles = positions.astype(jnp.float32)[:, None] * inv_freq[None, :]
            cos, sin = (jnp.cos(angles), jnp.sin(angles))
            xp = x.reshape(x.shape[:-1] + (d // 2, 2))
            x_even, x_odd = (xp[..., 0], xp[..., 1])
            out_even = x_even * cos - x_odd * sin
            out_odd = x_even * sin + x_odd * cos
            return jnp.stack((out_even, out_odd), axis=-1).reshape(x.shape)
        key = jax.random.key(seed)
        kx, kq, kk, kv, ko = jax.random.split(key, 5)
        std = np.sqrt(2.0 / (D_MODEL + D_MODEL))
        x = jax.random.normal(kx, (2, 256, D_MODEL), dtype=jnp.float32)
        W_q = _trunc_normal(kq, (D_MODEL, D_MODEL), std)
        W_k = _trunc_normal(kk, (D_MODEL, D_MODEL), std)
        W_v = _trunc_normal(kv, (D_MODEL, D_MODEL), std)
        W_o = _trunc_normal(ko, (D_MODEL, D_MODEL), std)
        return {'x': x, 'W_q': W_q, 'W_k': W_k, 'W_v': W_v, 'W_o': W_o}
    _L0_attn_a_in = _L0_attn_a_setup()

    def _L0_attn_b_setup():
        import math
        import jax, jax.numpy as jnp
        import numpy as np
        B, T, D, H = (2, 256, 128, 16)
        HD = D // H
        EPS = 1e-07

        def _coef(nc, fn):
            safe = jnp.where(nc > EPS, nc, 1.0)
            return jnp.where(nc > EPS, fn(safe) / safe, 1.0)

        def log_map0(x, c):
            n = jnp.sqrt(jnp.sum(x * x, axis=-1, keepdims=True))
            nc = jnp.sqrt(c) * n
            return _coef(nc, jnp.arcsinh) * x

        def exp_map0(v, c):
            n = jnp.sqrt(jnp.sum(v * v, axis=-1, keepdims=True))
            nc = jnp.sqrt(c) * n
            return _coef(nc, jnp.sinh) * v
        key = jax.random.key(seed)
        ks = jax.random.split(key, 9)
        s = 1.0 / math.sqrt(D)
        return {'h': jax.random.normal(ks[0], (B, T, D), jnp.float32) * 0.5, 'curv': jnp.ones((), jnp.float32), 'wq_w': jax.random.normal(ks[1], (D, D), jnp.float32) * s, 'wq_b': jnp.zeros((D,), jnp.float32), 'wk_w': jax.random.normal(ks[2], (D, D), jnp.float32) * s, 'wk_b': jnp.zeros((D,), jnp.float32), 'wv_w': jax.random.normal(ks[3], (D, D), jnp.float32) * s, 'wv_b': jnp.zeros((D,), jnp.float32), 'wo_w': jax.random.normal(ks[4], (D, D), jnp.float32) * s, 'wo_b': jnp.zeros((D,), jnp.float32)}
    _L0_attn_b_in = _L0_attn_b_setup()

    def _L0_ffn_setup():
        import jax, jax.numpy as jnp
        import numpy as np
        B, N, C, F, E, K = (2, 256, 128, 512, 8, 2)
        key = jax.random.key(seed)
        k = jax.random.split(key, 6)
        xavier1 = float(np.sqrt(6.0 / (C + F)))
        xavier2 = float(np.sqrt(6.0 / (F + C)))
        return {'x': jax.random.normal(k[0], (B, N, C), dtype=jnp.float32), 'router_w': jax.random.normal(k[1], (E, C), dtype=jnp.float32) * 0.01, 'w1': jax.random.uniform(k[2], (E, F, C), dtype=jnp.float32, minval=-xavier1, maxval=xavier1), 'b1': jnp.zeros((E, F), dtype=jnp.float32), 'w2': jax.random.uniform(k[3], (E, C, F), dtype=jnp.float32, minval=-xavier2, maxval=xavier2), 'b2': jnp.zeros((E, C), dtype=jnp.float32)}
    _L0_ffn_in = _L0_ffn_setup()
    _d = {'L0_attn_a_x': _L0_attn_a_in['x'], 'L0_attn_a_W_q': _L0_attn_a_in['W_q'], 'L0_attn_a_W_k': _L0_attn_a_in['W_k'], 'L0_attn_a_W_v': _L0_attn_a_in['W_v'], 'L0_attn_a_W_o': _L0_attn_a_in['W_o'], 'L0_attn_b_curv': _L0_attn_b_in['curv'], 'L0_attn_b_wq_w': _L0_attn_b_in['wq_w'], 'L0_attn_b_wq_b': _L0_attn_b_in['wq_b'], 'L0_attn_b_wk_w': _L0_attn_b_in['wk_w'], 'L0_attn_b_wk_b': _L0_attn_b_in['wk_b'], 'L0_attn_b_wv_w': _L0_attn_b_in['wv_w'], 'L0_attn_b_wv_b': _L0_attn_b_in['wv_b'], 'L0_attn_b_wo_w': _L0_attn_b_in['wo_w'], 'L0_attn_b_wo_b': _L0_attn_b_in['wo_b'], 'L0_ffn_router_w': _L0_ffn_in['router_w'], 'L0_ffn_w1': _L0_ffn_in['w1'], 'L0_ffn_b1': _L0_ffn_in['b1'], 'L0_ffn_w2': _L0_ffn_in['w2'], 'L0_ffn_b2': _L0_ffn_in['b2']}
    _x0 = _d['L0_attn_a_x']
    _d['L0_attn_a_x'] = jax.random.normal(jax.random.fold_in(jax.random.key(seed), 1), (8, 512, 128), dtype=_x0.dtype)
    del _x0
    return _d

def reference(L0_attn_a_x, L0_attn_a_W_q, L0_attn_a_W_k, L0_attn_a_W_v, L0_attn_a_W_o, L0_attn_b_curv, L0_attn_b_wq_w, L0_attn_b_wq_b, L0_attn_b_wk_w, L0_attn_b_wk_b, L0_attn_b_wv_w, L0_attn_b_wv_b, L0_attn_b_wo_w, L0_attn_b_wo_b, L0_ffn_router_w, L0_ffn_w1, L0_ffn_b1, L0_ffn_w2, L0_ffn_b2):

    def _L0_attn_a_ref(x, W_q, W_k, W_v, W_o):
        import jax, jax.numpy as jnp
        import numpy as np
        D_MODEL = 128
        N_HEADS = 16
        D_K = D_MODEL // N_HEADS
        THETA = 10000.0
        MAX_SEQ = 256

        def _trunc_normal(key, shape, std):
            return jnp.clip(jax.random.normal(key, shape) * std, -3 * std, 3 * std).astype(jnp.float32)

        def _rope(x, positions):
            d = x.shape[-1]
            inv_freq = THETA ** (-2.0 * jnp.arange(0, d // 2, dtype=jnp.float32) / d)
            angles = positions.astype(jnp.float32)[:, None] * inv_freq[None, :]
            cos, sin = (jnp.cos(angles), jnp.sin(angles))
            xp = x.reshape(x.shape[:-1] + (d // 2, 2))
            x_even, x_odd = (xp[..., 0], xp[..., 1])
            out_even = x_even * cos - x_odd * sin
            out_odd = x_even * sin + x_odd * cos
            return jnp.stack((out_even, out_odd), axis=-1).reshape(x.shape)
        b, s, _ = x.shape

        def split_heads(t):
            return t.reshape(b, s, N_HEADS, D_K).transpose(0, 2, 1, 3)
        Q = split_heads(x @ W_q.T)
        K = split_heads(x @ W_k.T)
        V = split_heads(x @ W_v.T)
        pos = jnp.arange(s)
        Q = _rope(Q, pos)
        K = _rope(K, pos)
        score = jnp.einsum('bnqd,bnkd->bnqk', Q, K) / jnp.sqrt(jnp.float32(D_K))
        causal = jnp.triu(jnp.ones((s, s), dtype=bool), k=1)
        score = jnp.where(causal[None, None], -jnp.inf, score)
        attn = jax.nn.softmax(score, axis=-1)
        out = jnp.einsum('bnqk,bnkd->bnqd', attn, V)
        out = out.transpose(0, 2, 1, 3).reshape(b, s, D_MODEL)
        return out @ W_o.T

    def _L0_attn_b_ref(h, curv, wq_w, wq_b, wk_w, wk_b, wv_w, wv_b, wo_w, wo_b):
        import math
        import jax, jax.numpy as jnp
        import numpy as np
        B, T, D, H = (2, 256, 128, 16)
        HD = D // H
        EPS = 1e-07

        def _coef(nc, fn):
            safe = jnp.where(nc > EPS, nc, 1.0)
            return jnp.where(nc > EPS, fn(safe) / safe, 1.0)

        def log_map0(x, c):
            n = jnp.sqrt(jnp.sum(x * x, axis=-1, keepdims=True))
            nc = jnp.sqrt(c) * n
            return _coef(nc, jnp.arcsinh) * x

        def exp_map0(v, c):
            n = jnp.sqrt(jnp.sum(v * v, axis=-1, keepdims=True))
            nc = jnp.sqrt(c) * n
            return _coef(nc, jnp.sinh) * v
        b, t, d = h.shape
        h_tan = log_map0(h, curv)

        def heads(x):
            return x.reshape(b, t, H, HD).transpose(0, 2, 1, 3)
        q_tan = heads(h_tan @ wq_w.T + wq_b)
        k_tan = heads(h_tan @ wk_w.T + wk_b)
        v_tan = heads(h_tan @ wv_w.T + wv_b)
        q_hyp = exp_map0(q_tan, curv)
        k_hyp = exp_map0(k_tan, curv)
        q_time = jnp.sqrt(1.0 / curv + jnp.sum(q_hyp * q_hyp, -1, keepdims=True))
        k_time = jnp.sqrt(1.0 / curv + jnp.sum(k_hyp * k_hyp, -1, keepdims=True))
        space_dot = jnp.einsum('bhqd,bhkd->bhqk', q_hyp, k_hyp)
        time_dot = q_time * jnp.swapaxes(k_time, -1, -2)
        attn_logits = -(space_dot - time_dot) / math.sqrt(HD)
        attn = jax.nn.softmax(attn_logits, axis=-1)
        out = jnp.einsum('bhqk,bhkd->bhqd', attn, v_tan)
        out = out.transpose(0, 2, 1, 3).reshape(b, t, d)
        return out @ wo_w.T + wo_b

    def _L0_ffn_ref(x, router_w, w1, b1, w2, b2):
        import jax, jax.numpy as jnp
        import numpy as np
        B, N, C, F, E, K = (2, 256, 128, 512, 8, 2)
        Bb, Nn, Cc = x.shape
        x_flat = x.reshape(-1, Cc)
        logits = jnp.einsum('tc,ec->te', x_flat, router_w)
        probs = jax.nn.softmax(logits, axis=-1)
        top_w, top_idx = jax.lax.top_k(probs, K)
        top_w = top_w / (jnp.sum(top_w, axis=-1, keepdims=True) + 1e-09)
        h = jnp.einsum('tc,efc->tef', x_flat, w1) + b1[None]
        h = jax.nn.relu(h)
        y = jnp.einsum('tef,ecf->tec', h, w2) + b2[None]
        sel = jnp.take_along_axis(y, top_idx[:, :, None], axis=1)
        out = jnp.einsum('tkc,tk->tc', sel, top_w)
        return out.reshape(Bb, Nn, Cc)
    x = L0_attn_a_x
    x = x + _L0_attn_a_ref(_layernorm(x, axis=-1), L0_attn_a_W_q, L0_attn_a_W_k, L0_attn_a_W_v, L0_attn_a_W_o)
    x = x + _L0_ffn_ref(_layernorm(x, axis=-1), L0_ffn_router_w, L0_ffn_w1, L0_ffn_b1, L0_ffn_w2, L0_ffn_b2)
    x = x + _L0_attn_b_ref(_layernorm(x, axis=-1), L0_attn_b_curv, L0_attn_b_wq_w, L0_attn_b_wq_b, L0_attn_b_wk_w, L0_attn_b_wk_b, L0_attn_b_wv_w, L0_attn_b_wv_b, L0_attn_b_wo_w, L0_attn_b_wo_b)
    x = x + _L0_ffn_ref(_layernorm(x, axis=-1), L0_ffn_router_w, L0_ffn_w1, L0_ffn_b1, L0_ffn_w2, L0_ffn_b2)
    return x

_drawn_inputs = setup_inputs


def setup_inputs(seed=0):
    import zlib

    import numpy as np

    out = dict(_drawn_inputs(seed))
    spreads = {'L0_attn_b_wq_b': (0.0, 0.549),
     'L0_attn_b_wk_b': (0.0, 0.435),
     'L0_attn_b_wv_b': (0.0, 0.1),
     'L0_attn_b_wo_b': (0.0, 0.1),
     'L0_ffn_b1': (0.0, 0.1),
     'L0_ffn_b2': (0.0, 0.1)}
    factors = {'L0_attn_b_wq_w': 3.223, 'L0_attn_b_wk_w': 2.694}
    for name, (base, spread) in spreads.items():
        noise = np.random.default_rng([zlib.crc32(name.encode()), seed]).standard_normal(out[name].shape)
        drawn = base * np.exp(spread * noise) if base else spread * noise
        out[name] = jnp.asarray(drawn.astype(out[name].dtype))
    for name, factor in factors.items():
        out[name] = (out[name] * factor).astype(out[name].dtype)
    return out
```

```python
from contextlib import ExitStack

import numpy as np
import concourse.bass as bass
from concourse import mybir
from concourse.bass import ds, IndirectOffsetOnAxis

B, S, D = 8, 512, 128
H, HD = 16, 8
P = 128
NT = S // P
E, FF, TOPK = 8, 512, 2
NF = FF // P
TOK = B * S
LIST = TOK
TILES = TOK * TOPK // P + E
ROUND = 8
ROUNDS = TILES // ROUND
NO_LIST = E * LIST
EPS = 1e-5
MASKED = -1e30
MAX_DELAY = 3
DVE_STEPS = {"a": 65, "b": 103}
FFN_STEPS = 24
SCALE = float(1.0 / np.sqrt(np.float32(HD)))
GROUPS = 4
JQ, JK = [0, 0, 0, 1, 1, 2], [0, 1, 2, 0, 1, 0]
MAXROW = 54
HEADROWS = 64

F32 = mybir.dt.float32
BF16 = mybir.dt.bfloat16
I32 = mybir.dt.int32
ALU = mybir.AluOpType
ACT = mybir.ActivationFunctionType
X_AXIS = mybir.AxisListType.X

UNITS_A = [(0, 0, 4), (1, 0, 2), (1, 2, 2)] + [(q, g, 1) for q in (2, 3) for g in range(4)]
UNITS_B = [(q, g, 1) for q in range(NT) for g in range(4)]

C_IDENT, C_COS, C_SIN, C_PICK, C_BASE, C_IDS = 0, 128, 640, 1152, 1184, 1216
C_END = 1232


def build_program(nc, a, out, stop=9):
    ctx = ExitStack()
    with ctx:
        def sb(name, shape, dt=F32):
            return ctx.enter_context(nc.sbuf_tensor(name, shape, dt))

        def sem(name):
            return ctx.enter_context(nc.semaphore(name))

        def sems(prefix, names):
            return {n: sem(prefix + n) for n in names.split()}

        xn_dram = nc.dram_tensor("xn_rows", [TOK + P, D], F32, kind="Internal").ap()
        list_dram = nc.dram_tensor("expert_lists", [E * LIST + P, 2], I32, kind="Internal").ap()
        y_dram = nc.dram_tensor("expert_rows", [TOPK * TOK, D], F32, kind="Internal").ap()

        x = sb("x", [P, B * NT, D])
        const = sb("const", [P, C_END])
        ident = const[:, C_IDENT:C_IDENT + P]
        cos_t, sin_t = const[:, C_COS:C_COS + S], const[:, C_SIN:C_SIN + S]
        pick = const[:, C_PICK:C_PICK + NT * E].rearrange("p (t e) -> p t e", e=E)
        listbase = const[:, C_BASE:C_BASE + NT * E].rearrange("p (t e) -> p t e", e=E)
        tilepos = sb("tilepos", [1, TILES, E])
        cbf = sb("cbf", [P, 5, P], BF16)
        ident_bf, mask_s, mask_t, before, ones_bf = (cbf[:, i, :] for i in range(5))
        half = sb("half", [P, NT * 2 * H])
        neghalf = sb("neghalf", [P, NT])
        wa = sb("wa", [P, 5, D])
        wao = sb("wao", [P, D])
        wb = sb("wb", [P, 3 * D])
        wbo = sb("wbo", [P, D])
        bias_qkv = sb("bias_qkv", [P, 3 * D])
        bias_o = sb("bias_o", [P, D])
        curv = sb("curv", [P, 1])
        inv_curv = sb("inv_curv", [P, 1])
        router = sb("router", [P, E])
        w1 = sb("w1", [P, E * FF])
        w2 = sb("w2", [P, E * FF])
        b1 = sb("b1", [P, E * FF])
        b2 = sb("b2", [P, E * D])

        stats = sb("stats", [P, NT, 6])
        moments = sb("moments", [P, NT, 2])
        var_eps = sb("var_eps", [P, NT])
        rstd = sb("rstd", [P, NT])
        xn = sb("xn", [P, NT, D])
        xnT = sb("xnT", [P, S])
        rest = sb("rest", [P, 4 * S])
        qk = rest[:, 0:2 * S].rearrange("p (t n) -> p t n", t=NT)
        qk_sq = rest[:, 2 * S:4 * S].rearrange("p (t n) -> p t n", t=NT)
        hyp = sb("hyp", [P, NT, 4, 9 * 8])
        ystage = hyp[:].rearrange("p a c n -> p (a c n)")[:, 0:TOPK * S].rearrange(
            "p (k t d) -> p k t d", k=TOPK, t=NT)
        work = sb("work", [P, 4, S])
        oT = work
        hypT = work[0:72, :, :]
        one_bf = work[0:3, :, :].rearrange("p c n -> p (c n)").bitcast(BF16)[:, 0:8 * S]
        qrot = work[:, 0:2, :]
        rope_c, rope_s = work[:, 2, :], work[:, 3, :]
        parts = sb("parts", [P, 3, 4 * S], BF16)
        qstack = sb("qstack", [P, 8, S], BF16)
        kstack = sb("kstack", [P, H, S], BF16)
        vones = sb("vones", [P, NT, H, 32])
        negmax = sb("negmax", [P, GROUPS, 4 * NT])
        maxrest = sb("maxrest", [16, P])
        maxparts = sb("maxparts", [16, GROUPS, 3, P], BF16)
        shared = sb("shared", [P, 2 * 4 * 2 * S])
        probs = shared[:].rearrange("p (a h n) -> p a h n", a=2, h=4)
        rsum = sb("rsum", [P, H])
        onorm = sb("onorm", [P, NT, D])
        onormT = sb("onormT", [P, S])
        xn2 = sb("xn2", [P, NT, D])
        xn2T = sb("xn2T", [P, S])
        rt = sb("rt", [P, 11, NT, E])
        rk = sb("rk", [P, 12, NT])
        lm = sb("lm", [P, 12, NT])
        lm_small = sb("lm_small", [P, NT], I32)
        em = sb("em", [P, 8, NT * 2 * H])
        em_small = sb("em_small", [P, NT * 2 * H], I32)
        tops_bf = sb("tops_bf", [P, NT, E], BF16)
        counts = sb("counts", [P, E])
        gates = sb("gates", [P, B * NT, TOPK])
        ids = sb("ids", [P, NT * TOPK * 2])
        entries = sb("entries", [P, NT, TOPK, 2], I32)
        slots = sb("slots", [P, TOPK, NT], I32)

        list_fill = sb("list_fill", [P, 2 * LIST * E // P], I32)
        lay = sb("lay", [P, 8, E])
        lay_i = sb("lay_i", [P, 2, E], I32)
        tile_f = sb("tile_f", [1, 2, TILES])
        tile_tab = sb("tile_tab", [1, 2, TILES], I32)
        entry = sb("entry", [P, ROUND, 2], I32)
        def view(at, *shape):
            names = "abc"[:len(shape)]
            n = int(np.prod(shape))
            return shared[:, at:at + n].rearrange(f"p ({' '.join(names)}) -> p {' '.join(names)}",
                                                  **dict(zip(names, shape)))

        xg = view(0, 4, D)
        xgT = view(512, 2, P)
        hid = view(768, 2, FF)
        hidT = view(1792, 2, NF, P)
        yrow = view(2816, 4, D)
        tl = view(3328, 4, TILES, E)[0:1]

        ps = ctx.enter_context(nc.psum_tensor("ps", [P, 8, 512], F32))
        misc = ps[:, 7, :]
        outT = ps[:, 6, :]

        def misc4(w):
            return misc[:, 0:4 * w].rearrange("p (t n) -> p t n", n=w)

        first = sems("init_", "x const weights tables ready clear emptied")
        ATT = ("dve pool norm_var norm_rstd norm_ready normT_ready normT_copied proj_ready proj_read "
               "part_ready stacked scores_ready max_done maxT_ready maxparts_ready "
               "exp_in exp_done pv_ready o_copied oT_ready onorm_ready onormT_ready onormT_copied "
               "oproj_ready norm2_var norm2_rstd norm2_ready norm2T_ready norm2T_copied logits_ready "
               "route_exp_in route_exp tops_ready rank_ready entries_ready entries_free scattered "
               "rows_stored rows_free ")
        att = {"a": sems("a_", ATT + "v_copied rot_ready"),
               "b": sems("b_", ATT + "nc_in nc_ready ln_in ln_ready norm_in norm_out exp_sh time_in "
                         "time_ready hyp_ready hypT_ready hypT_copied y_loaded combined square_done")}
        for ph in "ab":
            att[ph]["maxrows"] = [sem(f"{ph}_maxrows{half}") for half in range(2)]
        FFN = ("dve table xT_ready xT_copied h_ready h_copied hT_ready hT_copied "
               "y_ready y_copied")
        f = sems("f_", FFN)
        f["entry"] = [sem(f"f_entry{k}") for k in range(ROUND)]
        f["gathered"] = [sem(f"f_gathered{k}") for k in range(4)]
        f["scattered"] = [sem(f"f_scattered{k}") for k in range(4)]
        last = sems("end_", "y_loaded combined stored dve final_step")

        NSTACK = 2 * 2 * len(JQ) + 2
        units = {"a": UNITS_A, "b": UNITS_B}

        def first_tile(g):
            return 4 * (g // 2)

        def first_head(g):
            return 8 * (g % 2) + first_tile(g)

        def spans(ph, kp):
            if ph == "b":
                return [(2 * kp, 0, 0), (2 * kp + 1, 0, S)]
            k0, k1 = 2 * kp, 2 * kp + 1
            return [(k0, k0 * P, 0), (k1, k1 * P, S - k0 * P)]

        def width(ph, kp):
            kt, q0, c0 = spans(ph, kp)[-1]
            return c0 + S - q0

        def plain(eng):
            eng.sem_inc(carried[eng], 1)

        class Chain:
            def __init__(self, eng, semaphore, per_round):
                self.eng, self.sem, self.per_round = eng, semaphore, per_round

            def round(self, r):
                self.base, self.n = r * self.per_round, 0

            def link(self, ins):
                self.mark(ins)
                self.settle()

            def mark(self, ins):
                ins.then_inc(self.sem, 1)
                self.n += 1

            def settle(self):
                self.eng.wait_ge(self.sem, self.base + self.n)

            def end(self):
                assert self.n == self.per_round, (self.sem, self.n)

        TABLES = 9

        carried = {eng: sem("carried_" + name) for eng, name in ((nc.vector, "dve"), (nc.gpsimd, "pool"))}

        block = ctx.enter_context(nc.Block())

        @block.sync
        def _(sp):
            for ph in "ab":
                sp.sem_inc(att[ph]["rows_free"], 1)
            sp.dma_start(const[:], a["consts"]).then_inc(first["const"], 16)
            sp.dma_start(cbf[:], a["consts_bf"]).then_inc(first["const"], 16)
            sp.dma_start(x[:], a["x"].rearrange("(n p) d -> p n d", p=P)).then_inc(first["x"], 16)
            sp.dma_start(wa[:], a["wa"]).then_inc(first["weights"], 16)
            sp.dma_start(wao[:], a["wao"]).then_inc(first["weights"], 16)
            sp.dma_start(router[:], a["router"]).then_inc(first["weights"], 16)
            sp.dma_start(wb[:], a["wb"]).then_inc(first["weights"], 16)
            sp.dma_start(wbo[:], a["wbo"]).then_inc(first["weights"], 16)
            sp.dma_start(bias_qkv[:], a["bias_qkv"].partition_broadcast(P)).then_inc(first["weights"], 16)
            sp.dma_start(bias_o[:], a["bias_o"].partition_broadcast(P)).then_inc(first["weights"], 16)
            sp.dma_start(curv[:], a["curv"].partition_broadcast(P)).then_inc(first["weights"], 16)
            sp.dma_start(tilepos[:], a["tilepos"]).then_inc(first["weights"], 16)
            sp.dma_start(w1[:], a["w1"]).then_inc(first["weights"], 16)
            sp.dma_start(w2[:], a["w2"]).then_inc(first["weights"], 16)
            sp.dma_start(b1[:], a["b1"].partition_broadcast(P)).then_inc(first["weights"], 16)
            sp.dma_start(b2[:], a["b2"].partition_broadcast(P)).then_inc(first["weights"], 16)
            sp.wait_ge(first["tables"], TABLES)
            for par in range(2):
                r = HEADROWS * par + MAXROW
                sp.dma_start(kstack[r:r + 3, 8 * par:8 * par + 8, :],
                             one_bf).then_inc(first["ready"], 16)
            sp.dma_start(list_dram[0:NO_LIST, :].rearrange("(p n) c -> p (n c)", p=P),
                         list_fill[:]).then_inc(first["ready"], 16)
            sp.dma_start(list_dram[NO_LIST:NO_LIST + P, :],
                         list_fill[:, 0:2]).then_inc(first["ready"], 16)
            sp.dma_start(xn_dram[TOK:TOK + P, :].rearrange("(p n) d -> p (n d)", n=1),
                         onormT[:, 0:D]).then_inc(first["ready"], 16)

            def attention(ph, b):
                s = att[ph]
                if ph == "b":
                    sp.wait_ge(s["combined"], b + 1)
                    for k in range(TOPK):
                        sp.dma_start(ystage[:, k, :, :],
                                     y_dram[ds(b * S + k * TOK, S), :].rearrange(
                                         "(t p) d -> p t d", p=P)).then_inc(s["y_loaded"], 16)
                sp.wait_ge(s["part_ready"], 3 * b + 1)
                for par in range(2):
                    r = HEADROWS * par + MAXROW
                    sp.dma_start(qstack[r:r + 3, :, :], kstack[r + 3:r + 6, 8 * par:8 * par + 8, :]).then_inc(s["stacked"], 16)
                nd = HD + (ph == "b")
                for j in range(3):
                    sp.wait_ge(s["part_ready"], 3 * b + j + 1)
                    for par in range(2):
                        for i in range(len(JQ)):
                            r = HEADROWS * par + nd * i
                            if JQ[i] == j:
                                if ph == "a":
                                    src = parts[64 * par:64 * par + 64, j, 0:S]
                                else:
                                    src = parts[0:72, j, par * S:(par + 1) * S]
                                sp.dma_start(qstack[r:r + nd, :, :], src).then_inc(s["stacked"], 16)
                            if JK[i] == j:
                                if ph == "a":
                                    src = parts[64 * par:64 * par + 64, j, S:2 * S]
                                else:
                                    src = parts[0:72, j, (2 + par) * S:(3 + par) * S]
                                sp.dma_start(kstack[r:r + nd, 8 * par:8 * par + 8, :],
                                             src).then_inc(s["stacked"], 16)
                for g in range(GROUPS):
                    sp.wait_ge(s["maxparts_ready"], GROUPS * b + (g | 1) + 1)
                    t0 = first_tile(g)
                    for j in range(3):
                        r = HEADROWS * (g % 2) + MAXROW + j
                        sp.dma_start(qstack[r:r + 1, t0:t0 + 4, :].rearrange("j t (q n) -> j (t q) n", n=P),
                                     maxparts[:, g, j, :]).then_inc(s["maxrows"][g // 2], 16)
                sp.wait_ge(s["norm2_ready"], NT * b + NT)
                sp.dma_start(xn_dram[ds(b * S, S), :].rearrange("(t p) d -> p t d", p=P),
                             xn2[:]).then_inc(s["rows_stored"], 16)
                sp.wait_ge(s["rows_stored"], 16 * b + 16)
                sp.sem_inc(s["rows_free"], 1)

            def experts(n):
                r0 = n * ROUNDS
                sp.wait_ge(f["table"], n + 1)
                sp.wait_ge(att["ab"[n]]["scattered"], B * NT * TOPK * 16)

                def load_entries(i, k, first_round):
                    slot = sp.value_load(tile_tab[0:1, 1, ds(ROUND * i + k, 1)], min_val=0, max_val=NO_LIST)
                    if not first_round:
                        sp.wait_ge(f["scattered"][k % 4], 16 * (2 * (i + r0 - 1) + k // 4 + 1))
                    sp.dma_start(entry[:, k, :], list_dram[ds(slot, P), :]).then_inc(f["entry"][k], 16)

                for k in range(ROUND):
                    load_entries(0, k, True)
                with sp.Fori(1, ROUNDS) as i:
                    for k in range(ROUND):
                        load_entries(i, k, False)

            def rows_written(n):
                for k in range(4):
                    sp.wait_ge(f["scattered"][k], 16 * (n + 1) * TILES // 4)

            sp.wait_ge(first["ready"], 5 * 16)
            with sp.Fori(0, B) as b:
                attention("a", b)
            if stop >= 2:
                experts(0)
            if stop >= 3:
                rows_written(0)
                sp.dma_start(list_dram[0:NO_LIST, :].rearrange("(p n) c -> p (n c)", p=P),
                             list_fill[:]).then_inc(first["emptied"], 16)
                with sp.Fori(0, B) as b:
                    attention("b", b)
            if stop >= 4:
                experts(1)
            if stop in (1, 3):
                sp.wait_ge(last["combined"], B)
                sp.dma_start(out.rearrange("(n p) d -> p n d", p=P), x[:]).then_inc(last["stored"], 16)
                sp.wait_ge(last["stored"], 16)
            else:
                rows_written(1 if stop >= 4 else 0)
                with sp.Fori(0, B) as b:
                    sp.wait_ge(last["combined"], b + 1)
                    for k in range(TOPK):
                        sp.dma_start(ystage[:, k, :, :],
                                     y_dram[ds(b * S + k * TOK, S), :].rearrange(
                                         "(t p) d -> p t d", p=P)).then_inc(last["y_loaded"], 16)
                    sp.wait_ge(last["combined"], b + 2)
                    sp.dma_start(out[ds(b * S, S), :].rearrange("(t p) d -> p t d", p=P),
                                 x[:, ds(b * NT, NT), :]).then_inc(last["stored"], 16)
                sp.wait_ge(last["stored"], 16 * B)

        @block.gpsimd
        def _(pool):
            nc.gpsimd.memset(one_bf, 1.0).then_inc(first["tables"], 1)
            nc.gpsimd.iota(list_fill[:].rearrange("p (r n c) -> p r n c", n=P, c=2),
                           [[0, 2 * LIST * E // P // P // 2], [1, P], [TOK, 2]], base=TOK,
                           channel_multiplier=0).then_inc(first["tables"], 1)
            pool.sem_inc(att["a"]["entries_free"], 1)
            pool.sem_inc(att["b"]["entries_free"], 1)

            def attention(ph, b):
                s = att[ph]
                chain = pool_chain[ph]
                chain.round(b)
                pool.wait_ge(s["norm_var"], b + 1)
                nc.gpsimd.tensor_tensor(rstd[:], var_eps[:], neghalf[:], ALU.pow).then_inc(s["norm_rstd"], 1)
                if ph == "b":
                    pool.wait_ge(s["nc_in"], b + 1)
                    nc.gpsimd.tensor_tensor(lm[:, 2:4, :], lm[:, 0:2, :],
                                            half[:, 0:2 * NT].rearrange("p (a t) -> p a t", t=NT),
                                            ALU.pow).then_inc(s["nc_ready"], 1)
                    pool.wait_ge(s["norm_in"], b + 1)
                    nc.gpsimd.tensor_tensor(em[:, 1, :], em[:, 0, :], half[:], ALU.pow).then_inc(s["norm_out"], 1)
                    pool.wait_ge(s["time_in"], b + 1)
                    nc.gpsimd.tensor_tensor(hyp[:, :, :, 64:72].rearrange("p a c t -> p (a c) t"),
                                            em[:, 6, :].rearrange("p (c t) -> p c t", t=8),
                                            half[:].rearrange("p (c t) -> p c t", t=8),
                                            ALU.pow).then_inc(s["time_ready"], 1)
                    pool.wait_ge(s["hypT_copied"], 4 * b + 4)
                    src = hypT.rearrange("p c n -> p (c n)")
                    n, w = 72, 4 * S
                else:
                    pool.wait_ge(s["rot_ready"], 2 * b + 2)
                    src = qrot.rearrange("p c n -> p (c n)")
                    n, w = P, 2 * S
                plain(pool)
                nc.gpsimd.tensor_copy(parts[0:n, 0, 0:w], src).then_inc(s["part_ready"], 1)
                pool.wait_ge(s["part_ready"], 3 * b + 1)
                chain.link(nc.gpsimd.tensor_tensor(rest[0:n, 0:w], src, parts[0:n, 0, 0:w], ALU.subtract))
                plain(pool)
                nc.gpsimd.tensor_copy(parts[0:n, 1, 0:w], rest[0:n, 0:w]).then_inc(s["part_ready"], 1)
                pool.wait_ge(s["part_ready"], 3 * b + 2)
                nc.gpsimd.tensor_tensor(parts[0:n, 2, 0:w], rest[0:n, 0:w], parts[0:n, 1, 0:w],
                                        ALU.subtract).then_inc(s["part_ready"], 1)
                pool.wait_ge(s["norm2_var"], b + 1)
                nc.gpsimd.tensor_tensor(rstd[:], var_eps[:], neghalf[:], ALU.pow).then_inc(s["norm2_rstd"], 1)
                pool.wait_ge(s["entries_ready"], b + 1)
                plain(pool)
                for t in range(NT):
                    for k in range(TOPK):
                        nc.gpsimd.indirect_dma_start(
                            list_dram[:, :], IndirectOffsetOnAxis(slots[:, k, t:t + 1], 0),
                            entries[:, t, k, :], None).then_inc(s["scattered"], 16)
                pool.wait_ge(s["scattered"], (b + 1) * NT * TOPK * 16)
                pool.sem_inc(s["entries_free"], 1)
                chain.end()

            pool_chain = {"a": Chain(pool, att["a"]["pool"], 1), "b": Chain(pool, att["b"]["pool"], 1)}

            def experts(n):
                r0 = n * ROUNDS

                def gather(i, k, start):
                    pool.wait_ge(f["entry"][k], 16 * (i + r0) + 16)
                    if not start:
                        pool.wait_ge(f["xT_ready"], ROUND * (i + r0) + k - 3)
                        plain(pool)
                    nc.gpsimd.indirect_dma_start(
                        xg[:, k % 4, :], None, xn_dram[:, :],
                        IndirectOffsetOnAxis(entry[:, k, 0:1], 0)).then_inc(f["gathered"][k % 4], 16)

                def scatter(i, k):
                    pool.wait_ge(f["y_copied"], ROUND * (i + r0) + k + 1)
                    plain(pool)
                    nc.gpsimd.indirect_dma_start(
                        y_dram[:, :], IndirectOffsetOnAxis(entry[:, k, 1:2], 0), yrow[:, k % 4, :], None,
                        bounds_check=TOPK * TOK - 1, oob_is_err=False).then_inc(f["scattered"][k % 4], 16)

                for k in range(ROUND):
                    if k >= 4:
                        scatter(0, k - 4)
                    gather(0, k, k < 4)
                with pool.Fori(1, ROUNDS) as i:
                    for k in range(ROUND):
                        scatter(i - (k < 4), (k - 4) % ROUND)
                        gather(i, k, False)
                for k in range(ROUND - 4, ROUND):
                    scatter(ROUNDS - 1, k)

            pool.wait_ge(first["ready"], 5 * 16)
            pool.wait_ge(first["tables"], TABLES)
            with pool.Fori(0, B) as b:
                attention("a", b)
            if stop >= 2:
                experts(0)
            if stop >= 3:
                pool.wait_ge(first["emptied"], 16)
                with pool.Fori(0, B) as b:
                    attention("b", b)
            if stop >= 4:
                experts(1)

        @block.scalar
        def _(act):
            for ph in "ab":
                act.sem_inc(att[ph]["exp_done"], 2)
                act.sem_inc(att[ph]["o_copied"], 1)

            def attention(ph, b):
                s = att[ph]
                if ph == "b":
                    act.wait_ge(s["ln_in"], b + 1)
                    nc.scalar.activation(lm[:, 5, :], lm[:, 4, :], ACT.Ln).then_inc(s["ln_ready"], 1)
                act.wait_ge(s["normT_ready"], b + 1)
                nc.scalar.copy(xnT[:], misc).then_inc(s["normT_copied"], 1)
                if ph == "a":
                    act.wait_ge(s["proj_ready"], 5 * b + 5)
                    nc.scalar.copy(vones[:, :, :, 0:HD],
                                   misc.rearrange("p (t h d) -> p t h d", t=NT, h=H)).then_inc(s["v_copied"], 1)
                else:
                    act.wait_ge(s["proj_read"], NT * b + NT)
                    nc.scalar.activation(qk_sq, qk, ACT.Square).then_inc(s["square_done"], 1)
                    act.wait_ge(s["norm_out"], b + 1)
                    nc.scalar.activation(em[:, 2, :], em[:, 1, :], ACT.Exp).then_inc(s["exp_sh"], 1)
                    nc.scalar.activation(em[:, 3, :], em[:, 1, :], ACT.Exp, scale=-1.0).then_inc(s["exp_sh"], 1)
                    for c in range(4):
                        act.wait_ge(s["hypT_ready"], 4 * b + c + 1)
                        nc.scalar.copy(hypT[:, c, :], misc[0:72, :]).then_inc(s["hypT_copied"], 1)
                n = 0
                for g in range(GROUPS):
                    for kp in range(2):
                        quad = 2 * g + kp
                        act.wait_ge(s["pv_ready"], 8 * b + quad + 1)
                        for h in range(4):
                            act.wait_ge(s["exp_in"], 32 * b + n + 1)
                            w = width(ph, kp)
                            st = ps[:, 2 + 2 * (n % 2):4 + 2 * (n % 2), :].rearrange("p a n -> p (a n)")
                            nc.scalar.activation(probs[:, quad % 2, h, 0:w], st[:, 0:w], ACT.Exp,
                                                 scale=SCALE).then_inc(s["exp_done"], 1)
                            n += 1
                        if kp == 0 and g > 0:
                            copy_out(ph, b, g - 1)
                copy_out(ph, b, GROUPS - 1)
                act.wait_ge(s["onormT_ready"], b + 1)
                nc.scalar.copy(onormT[:], misc).then_inc(s["onormT_copied"], 1)
                act.wait_ge(s["norm2T_ready"], b + 1)
                nc.scalar.copy(xn2T[:], misc).then_inc(s["norm2T_copied"], 1)
                act.wait_ge(s["route_exp_in"], b + 1)
                nc.scalar.activation(rt[:, 9, :, :], rt[:, 8, :, :], ACT.Exp).then_inc(s["route_exp"], 1)

            def copy_out(ph, b, g):
                s = att[ph]
                act.wait_ge(s["pv_ready"], 8 * b + 2 * g + 2 + 2)
                nc.scalar.copy(oT[:, g, :], outT).then_inc(s["o_copied"], 1)

            def experts(n):
                r0 = n * ROUNDS

                def rows(i, k):
                    act.wait_ge(f["xT_ready"], ROUND * (i + r0) + k + 1)
                    nc.scalar.copy(xgT[:, k % 2, :], ps[:, 6, 0:P]).then_inc(f["xT_copied"], 1)

                def relu(i, k):
                    act.wait_ge(f["hT_ready"], ROUND * (i + r0) + k + 1)
                    nc.scalar.activation(hidT[:, k % 2, :, :], ps[:, 2 + k % 2, :].rearrange(
                        "p (f n) -> p f n", n=P), ACT.Relu).then_inc(f["hT_copied"], 1)

                for k in range(ROUND):
                    rows(0, k)
                    if k >= 1:
                        relu(0, k - 1)
                with act.Fori(1, ROUNDS) as i:
                    for k in range(ROUND):
                        rows(i, k)
                        relu(i - (k < 1), (k - 1) % ROUND)
                relu(ROUNDS - 1, ROUND - 1)

            act.wait_ge(first["tables"], TABLES)
            act.wait_ge(first["const"], 32)
            with act.Fori(0, B) as b:
                attention("a", b)
            if stop >= 2:
                experts(0)
            if stop >= 3:
                with act.Fori(0, B) as b:
                    attention("b", b)
            if stop >= 4:
                experts(1)

        @block.vector
        def _(dve):
            nc.vector.memset(vones[:], 0.0).then_inc(first["clear"], 1)
            nc.vector.memset(kstack[:], 0.0).then_inc(first["tables"], 1)
            nc.vector.memset(qstack[:], 0.0).then_inc(first["tables"], 1)
            nc.vector.memset(onormT[:], 0.0).then_inc(first["tables"], 1)
            nc.vector.memset(half[:], 0.5).then_inc(first["tables"], 1)
            nc.vector.memset(neghalf[:], -0.5).then_inc(first["tables"], 1)
            nc.vector.memset(counts[:], 0.0).then_inc(first["tables"], 1)
            dve.wait_ge(first["clear"], 1)
            nc.vector.memset(vones[:, :, :, HD:HD + 1], 1.0).then_inc(first["tables"], 1)
            dve.sem_inc(att["a"]["max_done"], 2)
            dve.sem_inc(att["b"]["max_done"], 2)
            dve.sem_inc(att["b"]["combined"], 1)
            dve.sem_inc(last["combined"], 1)

            chains = {"a": Chain(dve, att["a"]["dve"], DVE_STEPS["a"]), "b": Chain(dve, att["b"]["dve"], DVE_STEPS["b"])}

            def moments_of(b, chain):
                plain(dve)
                for t in range(NT):
                    chain.mark(nc.vector.bn_stats(stats[:, t, :], x[:, ds(b * NT + t, 1), :]))
                chain.settle()
                plain(dve)
                for t in range(NT):
                    chain.mark(nc.vector.bn_aggr(moments[:, t, :], stats[:, t, :]))
                chain.settle()
                return nc.vector.tensor_scalar(var_eps[:], moments[:, :, 1], EPS, None, ALU.add)

            def normalised(b, t, dst, factor):
                return nc.vector.tensor_scalar(dst[:, t, :], x[:, ds(b * NT + t, 1), :].rearrange("p a d -> p (a d)"),
                                               moments[:, t, 0:1], factor[:, t:t + 1],
                                               ALU.subtract, ALU.mult)

            def add_expert_rows(b, chain, done):
                xb = x[:, ds(b * NT, NT), :]
                for k in range(TOPK):
                    g = gates[:, ds(b * NT, NT), k:k + 1].to_broadcast([P, NT, D])
                    chain.mark(nc.vector.tensor_tensor(ystage[:, k, :, :], ystage[:, k, :, :], g, ALU.mult))
                chain.settle()
                chain.link(nc.vector.tensor_tensor(xb, xb, ystage[:, 0, :, :], ALU.add))
                nc.vector.tensor_tensor(xb, xb, ystage[:, 1, :, :], ALU.add).then_inc(done, 1)

            def rope(b):
                s = att["a"]
                for i in range(2):
                    dve.wait_ge(s["proj_ready"], 5 * b + 2 * i + 1)
                    nc.vector.tensor_tensor(rope_c, misc, cos_t, ALU.mult).then_inc(s["proj_read"], 1)
                    dve.wait_ge(s["proj_ready"], 5 * b + 2 * i + 2)
                    nc.vector.tensor_tensor(rope_s, misc, sin_t, ALU.mult).then_inc(s["proj_read"], 1)
                    dve.wait_ge(s["proj_read"], 4 * b + 2 * i + 2)
                    nc.vector.tensor_tensor(qrot[:, i, :], rope_c, rope_s, ALU.add).then_inc(s["rot_ready"], 1)
                    dve.wait_ge(s["rot_ready"], 2 * b + i + 1)

            def log_map(b, chain):
                s = att["b"]
                u, u1, root, root1, arg, ln, rec, ser, coef, rr, var, scale = (lm[:, i, :] for i in range(12))
                dve.wait_ge(s["norm_rstd"], b + 1)
                chain.link(nc.vector.tensor_tensor(rr, rstd[:], rstd[:], ALU.mult))
                chain.link(nc.vector.tensor_tensor(var, moments[:, :, 1], rr, ALU.mult))
                chain.link(nc.vector.tensor_scalar(u, var, float(D), curv[:, 0:1], ALU.mult, ALU.mult))
                nc.vector.tensor_scalar(u1, u, 1.0, None, ALU.add).then_inc(s["nc_in"], 1)
                dve.wait_ge(s["nc_ready"], b + 1)
                nc.vector.tensor_tensor(arg, root, root1, ALU.add).then_inc(s["ln_in"], 1)
                chain.link(nc.vector.tensor_scalar(rec, root, 1e-30, None, ALU.max))
                chain.link(nc.vector.reciprocal(rec, rec))
                chain.link(nc.vector.tensor_scalar(ser, u, 105.0 / 3456.0, None, ALU.mult))
                for c in (-15.0 / 336.0, 3.0 / 40.0, -1.0 / 6.0):
                    chain.link(nc.vector.scalar_tensor_tensor(ser, ser, c, u, ALU.add, ALU.mult))
                chain.link(nc.vector.tensor_scalar(ser, ser, 1.0, None, ALU.add))
                chain.link(nc.vector.tensor_scalar(lm_small[:], u, 0.06, None, ALU.is_lt))
                dve.wait_ge(s["ln_ready"], b + 1)
                chain.link(nc.vector.tensor_tensor(coef, ln, rec, ALU.mult))
                plain(dve)
                chain.link(nc.vector.copy_predicated(coef, lm_small[:], ser))
                chain.link(nc.vector.tensor_tensor(scale, coef, rstd[:], ALU.mult))
                return scale

            def exp_map(b, chain):
                s = att["b"]
                u, root, ep, en, n2, coef, t2, tmp = (em[:, i, :] for i in range(8))
                dve.wait_ge(s["square_done"], b + 1)
                chain.link(nc.vector.tensor_reduce(n2, qk_sq.rearrange("p a (h d) -> p (a h) d", d=HD),
                                                   axis=X_AXIS, op=ALU.add))
                nc.vector.tensor_scalar(u, n2, curv[:, 0:1], None, ALU.mult).then_inc(s["norm_in"], 1)
                dve.wait_ge(s["norm_out"], b + 1)
                chain.link(nc.vector.tensor_scalar(tmp, root, 1e-30, None, ALU.max))
                chain.link(nc.vector.reciprocal(tmp, tmp))
                dve.wait_ge(s["exp_sh"], 2 * b + 2)
                chain.link(nc.vector.tensor_tensor(ep, ep, en, ALU.subtract))
                chain.link(nc.vector.scalar_tensor_tensor(coef, ep, 0.5, tmp, ALU.mult, ALU.mult))
                chain.link(nc.vector.tensor_scalar(en, u, 1.0 / 39916800.0, None, ALU.mult))
                for c in (1.0 / 362880.0, 1.0 / 5040.0, 1.0 / 120.0, 1.0 / 6.0):
                    chain.link(nc.vector.scalar_tensor_tensor(en, en, c, u, ALU.add, ALU.mult))
                chain.link(nc.vector.tensor_scalar(en, en, 1.0, None, ALU.add))
                chain.link(nc.vector.tensor_scalar(em_small[:], u, 1.0, None, ALU.is_lt))
                plain(dve)
                chain.link(nc.vector.copy_predicated(coef, em_small[:], en))
                chain.link(nc.vector.tensor_tensor(tmp, coef, coef, ALU.mult))
                chain.link(nc.vector.tensor_tensor(tmp, tmp, n2, ALU.mult))
                nc.vector.tensor_scalar(t2, tmp, inv_curv[:, 0:1], None, ALU.add).then_inc(s["time_in"], 1)
                kc = coef.rearrange("p (a c h) -> p a c h", a=NT, c=2)[:, :, 1, :]
                chain.link(nc.vector.tensor_scalar(kc, kc, -1.0, None, ALU.mult))
                nc.vector.tensor_tensor(
                    hyp[:, :, :, 0:64].rearrange("p a c (d t) -> p (a c) t d", t=8),
                    qk.rearrange("p a (c t d) -> p (a c) t d", t=8, d=HD),
                    coef.rearrange("p (c t) -> p c t", t=8).unsqueeze(3).to_broadcast([P, 16, 8, HD]),
                    ALU.mult).then_inc(s["hyp_ready"], 1)

            def max_parts(ph, b, g, chain):
                s = att[ph]
                dve.wait_ge(s["maxT_ready"], GROUPS * b + g + 1)
                m = misc[0:16, g * P:(g + 1) * P]
                chain.link(nc.vector.tensor_copy(maxparts[:, g, 0, :], m))
                chain.link(nc.vector.tensor_tensor(maxrest[:], m, maxparts[:, g, 0, :], ALU.subtract))
                chain.link(nc.vector.tensor_copy(maxparts[:, g, 1, :], maxrest[:]))
                nc.vector.tensor_tensor(maxparts[:, g, 2, :], maxrest[:], maxparts[:, g, 1, :],
                                        ALU.subtract).then_inc(s["maxparts_ready"], 1)
                dve.wait_ge(s["maxparts_ready"], GROUPS * b + g + 1)

            def route(ph, b, chain):
                s = att[ph]
                logit, eq, sc, top1, logit2, top2, both, place, shifted, ex, tmp = (rt[:, i] for i in range(11))
                m1, w1_, m2, w2_, total, e2, p1, p2, den, rs, pl1, pl2 = (rk[:, i, :] for i in range(12))

                def over(v):
                    return v.unsqueeze(2).to_broadcast([P, NT, E])

                def best(of, m, w, top):
                    chain.link(nc.vector.tensor_reduce(m, of, axis=X_AXIS, op=ALU.max))
                    chain.link(nc.vector.tensor_tensor(eq, of, over(m), ALU.is_equal))
                    chain.link(nc.vector.tensor_tensor(sc, eq, pick, ALU.mult))
                    chain.link(nc.vector.tensor_reduce(w, sc, axis=X_AXIS, op=ALU.max))
                    chain.link(nc.vector.tensor_tensor(top, sc, over(w), ALU.is_equal))

                dve.wait_ge(s["logits_ready"], b + 1)
                chain.link(nc.vector.tensor_copy(logit, misc4(E)))
                best(logit, m1, w1_, top1)
                nc.vector.tensor_tensor(shifted, logit, over(m1), ALU.subtract).then_inc(s["route_exp_in"], 1)
                chain.link(nc.vector.scalar_tensor_tensor(logit2, top1, MASKED, logit, ALU.mult, ALU.add))
                best(logit2, m2, w2_, top2)
                nc.vector.tensor_tensor(tops_bf[:], top1, top2, ALU.add).then_inc(s["tops_ready"], 1)
                dve.wait_ge(s["route_exp"], b + 1)
                chain.link(nc.vector.tensor_reduce(total, ex, axis=X_AXIS, op=ALU.add))
                chain.link(nc.vector.reciprocal(p1, total))
                chain.link(nc.vector.tensor_tensor(tmp, ex, top2, ALU.mult))
                chain.link(nc.vector.tensor_reduce(e2, tmp, axis=X_AXIS, op=ALU.add))
                chain.link(nc.vector.tensor_tensor(p2, e2, p1, ALU.mult))
                chain.link(nc.vector.tensor_tensor(den, p1, p2, ALU.add))
                chain.link(nc.vector.tensor_scalar(den, den, 1e-9, None, ALU.add))
                chain.link(nc.vector.reciprocal(rs, den))
                for k, p in enumerate((p1, p2)):
                    chain.mark(nc.vector.tensor_tensor(gates[:, ds(b * NT, NT), k], p, rs, ALU.mult))
                dve.wait_ge(s["rank_ready"], b + 1)
                chain.link(nc.vector.tensor_tensor(
                    place, misc[:, 0:NT * E].rearrange("p (t e) -> p t e", e=E),
                    counts[:].unsqueeze(1).to_broadcast([P, NT, E]), ALU.add))
                chain.mark(nc.vector.tensor_tensor(counts[:], counts[:], misc[:, NT * E:NT * E + E], ALU.add))
                chain.link(nc.vector.tensor_tensor(place, place, listbase, ALU.add))
                dve.wait_ge(s["entries_free"], b + 1)
                for k, (top, pl) in enumerate(((top1, pl1), (top2, pl2))):
                    chain.link(nc.vector.tensor_tensor(tmp, place, top, ALU.mult))
                    chain.link(nc.vector.tensor_reduce(pl, tmp, axis=X_AXIS, op=ALU.add))
                    chain.mark(nc.vector.tensor_copy(slots[:, k, :], pl))
                nc.vector.tensor_copy(entries[:].rearrange("p t k c -> p (t k c)"), ids[:]).then_inc(s["entries_ready"], 1)
                dve.wait_ge(s["entries_ready"], b + 1)
                chain.link(nc.vector.tensor_scalar(ids[:], ids[:], float(S), None, ALU.add))

            def attention(ph, b):
                s = att[ph]
                chain = chains[ph]
                chain.round(b)
                if ph == "b":
                    dve.wait_ge(s["y_loaded"], TOPK * 16 * (b + 1))
                    add_expert_rows(b, chain, s["combined"])
                    dve.wait_ge(s["combined"], b + 2)
                moments_of(b, chain).then_inc(s["norm_var"], 1)
                if ph == "a":
                    dve.wait_ge(s["norm_rstd"], b + 1)
                    scale = rstd
                else:
                    scale = log_map(b, chain)
                for t in range(NT):
                    normalised(b, t, xn, scale).then_inc(s["norm_ready"], 1)
                if ph == "a":
                    rope(b)
                else:
                    for t in range(NT):
                        dve.wait_ge(s["proj_ready"], NT * b + t + 1)
                        chain.mark(nc.vector.tensor_tensor(qk[:, t, :], misc[:, 0:2 * D], bias_qkv[:, 0:2 * D], ALU.add))
                        nc.vector.tensor_tensor(vones[:, t, :, 0:HD],
                                                misc[:, 2 * D:3 * D].rearrange("p (h d) -> p h d", d=HD),
                                                bias_qkv[:, 2 * D:3 * D].rearrange("p (h d) -> p h d", d=HD),
                                                ALU.add).then_inc(s["proj_read"], 1)
                    exp_map(b, chain)
                n, per_group = 0, len(units[ph])
                for g in range(GROUPS):
                    for i, (q, h0, nh) in enumerate(units[ph]):
                        w = (q + 1) * P if ph == "a" else S
                        dve.wait_ge(s["scores_ready"], per_group * GROUPS * b + n + 1)
                        nc.vector.tensor_reduce(
                            negmax[:, g, :].rearrange("p (t q) -> p t q", q=NT)[:, h0:h0 + nh, q],
                            ps[:, n % 2, 0:nh * w].rearrange("p (h k) -> p h k", h=nh),
                            axis=X_AXIS, op=ALU.max, negate=True).then_inc(s["max_done"], 1)
                        n += 1
                        if i == MAX_DELAY and g > 0:
                            max_parts(ph, b, g - 1, chain)
                max_parts(ph, b, GROUPS - 1, chain)
                for t in range(NT):
                    dve.wait_ge(s["oT_ready"], NT * b + t + 1)
                    heads = misc.rearrange("p (h c) -> p h c", c=32)
                    chain.link(nc.vector.reciprocal(rsum[:], heads[:, :, HD]))
                    nc.vector.tensor_tensor(onorm[:, t, :].rearrange("p (h d) -> p h d", d=HD), heads[:, :, 0:HD],
                                            rsum[:].unsqueeze(2).to_broadcast([P, H, HD]),
                                            ALU.mult).then_inc(s["onorm_ready"], 1)
                xb = x[:, ds(b * NT, NT), :]
                dve.wait_ge(s["oproj_ready"], b + 1)
                chain.link(nc.vector.tensor_tensor(xb, xb, misc4(D), ALU.add))
                if ph == "b":
                    chain.link(nc.vector.tensor_tensor(xb, xb, bias_o[:].unsqueeze(1).to_broadcast([P, NT, D]), ALU.add))
                moments_of(b, chain).then_inc(s["norm2_var"], 1)
                dve.wait_ge(s["norm2_rstd"], b + 1)
                dve.wait_ge(s["rows_free"], b + 1)
                for t in range(NT):
                    normalised(b, t, xn2, rstd).then_inc(s["norm2_ready"], 1)
                route(ph, b, chain)
                chain.end()

            def experts(n):
                r0 = n * ROUNDS
                chain = Chain(dve, f["dve"], FFN_STEPS)
                chain.round(n)
                padded, ends, starts, offset = (lay[:, i, :] for i in range(4))
                chain.link(nc.vector.tensor_scalar(lay_i[:, 0, :], counts[:], float(P - 1), None, ALU.add))
                chain.link(nc.vector.tensor_scalar(lay_i[:, 1, :], lay_i[:, 0, :], 7, 7,
                                                   ALU.arith_shift_right, ALU.logical_shift_left))
                chain.link(nc.vector.tensor_copy(padded, lay_i[:, 1, :]))
                chain.link(nc.vector.tensor_copy(ends, padded))
                for e in range(1, E):
                    chain.link(nc.vector.tensor_tensor(ends[:, e:e + 1], ends[:, e:e + 1], ends[:, e - 1:e], ALU.add))
                chain.link(nc.vector.tensor_tensor(starts, ends, padded, ALU.subtract))
                chain.link(nc.vector.tensor_tensor(offset, listbase[:, 0, :], starts, ALU.subtract))
                chain.link(nc.vector.tensor_scalar(offset, offset, -float(NO_LIST), None, ALU.add))
                begun, ended, inside, entry_at = (tl[:, i] for i in range(4))

                def over(v):
                    return v[0:1, :].unsqueeze(1).to_broadcast([1, TILES, E])

                chain.link(nc.vector.tensor_tensor(begun, tilepos[:], over(starts), ALU.is_ge))
                chain.link(nc.vector.tensor_tensor(ended, tilepos[:], over(ends), ALU.is_ge))
                chain.link(nc.vector.tensor_tensor(inside, begun, ended, ALU.subtract))
                chain.link(nc.vector.tensor_tensor(entry_at, tilepos[:], over(offset), ALU.add))
                chain.link(nc.vector.tensor_tensor(entry_at, entry_at, inside, ALU.mult))
                chain.link(nc.vector.tensor_reduce(tile_f[:, 0, :], ended, axis=X_AXIS, op=ALU.add))
                chain.link(nc.vector.tensor_reduce(tile_f[:, 1, :], entry_at, axis=X_AXIS, op=ALU.add))
                chain.link(nc.vector.tensor_scalar(tile_tab[:, 0, :], tile_f[:, 0, :], float(E - 1), None, ALU.min))
                chain.link(nc.vector.memset(counts[:], 0.0))
                chain.link(nc.vector.tensor_scalar(ids[:], ids[:], -float(TOK), None, ALU.add))
                nc.vector.tensor_scalar(tile_tab[:, 1, :], tile_f[:, 1, :], float(NO_LIST), None,
                                        ALU.add).then_inc(f["table"], 1)
                chain.end()
                dve.wait_ge(f["table"], n + 1)

                def hidden(i, k, start):
                    e = dve.value_load(tile_tab[0:1, 0, ds(ROUND * i + k, 1)], min_val=0, max_val=E - 1)
                    dve.wait_ge(f["h_ready"], ROUND * (i + r0) + k + 1)
                    if not start:
                        dve.wait_ge(f["hT_ready"], ROUND * (i + r0) + k - 1)
                    nc.vector.tensor_tensor(hid[:, k % 2, :], ps[:, k % 2, :], b1[:, ds(e * FF, FF)],
                                            ALU.add).then_inc(f["h_copied"], 1)

                def result(i, k, start):
                    e = dve.value_load(tile_tab[0:1, 0, ds(ROUND * i + k, 1)], min_val=0, max_val=E - 1)
                    dve.wait_ge(f["y_ready"], ROUND * (i + r0) + k + 1)
                    if not start:
                        dve.wait_ge(f["scattered"][k % 4], 16 * (2 * (i + r0) + k // 4))
                    nc.vector.tensor_tensor(yrow[:, k % 4, :], ps[:, 4, 0:P], b2[:, ds(e * D, D)],
                                            ALU.add).then_inc(f["y_copied"], 1)

                for k in range(ROUND):
                    if k >= 1:
                        hidden(0, k - 1, k - 1 < 2)
                    if k >= 2:
                        result(0, k - 2, k - 2 < 4)
                with dve.Fori(1, ROUNDS) as i:
                    for k in range(ROUND):
                        hidden(i - (k < 1), (k - 1) % ROUND, False)
                        result(i - (k < 2), (k - 2) % ROUND, False)
                hidden(ROUNDS - 1, ROUND - 1, False)
                result(ROUNDS - 1, ROUND - 2, False)
                result(ROUNDS - 1, ROUND - 1, False)

            dve.wait_ge(first["const"], 32)
            dve.wait_ge(first["x"], 16)
            dve.wait_ge(first["weights"], 13 * 16)
            dve.wait_ge(first["tables"], TABLES)
            start = Chain(dve, last["dve"], 2)
            start.round(0)
            start.link(nc.vector.tensor_copy(ids[:], const[:, C_IDS:C_IDS + NT * TOPK * 2]))
            start.link(nc.vector.reciprocal(inv_curv[:], curv[:]))
            with dve.Fori(0, B) as b:
                attention("a", b)
            if stop >= 2:
                experts(0)
            if stop >= 3:
                with dve.Fori(0, B) as b:
                    attention("b", b)
            if stop >= 4:
                experts(1)
            if stop in (1, 3):
                dve.sem_inc(last["combined"], B)
            else:
                final = Chain(dve, last["final_step"], 3)
                with dve.Fori(0, B) as b:
                    final.round(b)
                    dve.wait_ge(last["y_loaded"], TOPK * 16 * (b + 1))
                    add_expert_rows(b, final, last["combined"])
                    dve.wait_ge(last["combined"], b + 2)
                    final.end()

        @block.tensor
        def _(pe):
            for ph in "ab":
                pe.sem_inc(att[ph]["pv_ready"], 2)

            def project_a(b):
                s = att["a"]
                for i in range(4):
                    if i:
                        pe.wait_ge(s["proj_read"], 4 * b + i)
                    nc.tensor.matmul(misc, wa[:, i, :], xnT[:], start=True, stop=True).then_inc(s["proj_ready"], 1)
                pe.wait_ge(s["proj_read"], 4 * b + 4)
                for t in range(NT):
                    mm = nc.tensor.matmul(misc[:, t * D:(t + 1) * D], xnT[:, t * P:(t + 1) * P], wa[:, 4, :],
                                          start=True, stop=True)
                mm.then_inc(s["proj_ready"], 1)
                pe.wait_ge(s["v_copied"], b + 1)

            def project_b(b):
                s = att["b"]
                for t in range(NT):
                    if t:
                        pe.wait_ge(s["proj_read"], NT * b + t)
                    nc.tensor.matmul(misc[:, 0:3 * D], xnT[:, t * P:(t + 1) * P], wb[:],
                                     start=True, stop=True).then_inc(s["proj_ready"], 1)
                pe.wait_ge(s["proj_read"], NT * b + NT)
                pe.wait_ge(s["hyp_ready"], b + 1)
                pe.wait_ge(s["time_ready"], b + 1)
                for c in range(4):
                    if c:
                        pe.wait_ge(s["hypT_copied"], 4 * b + c)
                    for t in range(NT):
                        mm = nc.tensor.transpose(misc[0:72, t * P:(t + 1) * P], hyp[:, t, c, :], ident)
                    mm.then_inc(s["hypT_ready"], 1)
                pe.wait_ge(s["hypT_copied"], 4 * b + 4)

            def score_unit(ph, b, g, unit, n):
                s = att[ph]
                q, h0, nh = unit
                w = (q + 1) * P if ph == "a" else S
                pe.wait_ge(s["max_done"], len(units[ph]) * GROUPS * b + n + 1)
                for h in range(h0, h0 + nh):
                    o = (h - h0) * w
                    mm = nc.tensor.matmul(ps[:, n % 2, o:o + w], qstack[:, first_tile(g) + h, q * P:(q + 1) * P],
                                          kstack[:, first_head(g) + h, 0:w], start=True, stop=ph == "b")
                    if ph == "a":
                        mm = nc.tensor.matmul(ps[:, n % 2, o + w - P:o + w], ident_bf, mask_s,
                                              start=False, stop=True)
                mm.then_inc(s["scores_ready"], 1)

            def transpose_max(ph, b, g):
                s = att[ph]
                pe.wait_ge(s["max_done"], len(units[ph]) * (GROUPS * b + g + 1) + 2)
                if g:
                    pe.wait_ge(s["maxparts_ready"], GROUPS * b + g)
                nc.tensor.transpose(misc[0:16, g * P:(g + 1) * P], negmax[:, g, :], ident).then_inc(s["maxT_ready"], 1)

            def prob_unit(ph, b, g, kp, h, n):
                s = att[ph]
                pe.wait_ge(s["exp_done"], 32 * b + n + 1)
                st = ps[:, 2 + 2 * (n % 2):4 + 2 * (n % 2), :].rearrange("p a n -> p (a n)")
                for kt, q0, c in spans(ph, kp):
                    mm = nc.tensor.matmul(st[:, c:c + S - q0], kstack[:, first_head(g) + h, kt * P:(kt + 1) * P],
                                          qstack[:, first_tile(g) + h, q0:S], start=True, stop=ph == "b")
                    if ph == "a":
                        mm = nc.tensor.matmul(st[:, c:c + P], ident_bf, mask_t, start=False, stop=True)
                mm.then_inc(s["exp_in"], 1)

            def weighted_sum(ph, b, quad):
                s = att[ph]
                g, kp = divmod(quad, 2)
                pe.wait_ge(s["exp_done"], 32 * b + 4 * quad + 4 + 2)
                if kp == 0:
                    pe.wait_ge(s["o_copied"], GROUPS * b + g + 1)
                for kt, q0, c in spans(ph, kp):
                    for h in range(4):
                        mm = nc.tensor.matmul(outT[32 * h:32 * h + 32, q0:S], vones[:, kt, first_head(g) + h, :],
                                              probs[:, quad % 2, h, c:c + S - q0],
                                              start=kt == 0, stop=kt == NT - 1)
                mm.then_inc(s["pv_ready"], 1)

            def attention(ph, b):
                s = att[ph]
                for t in range(NT):
                    pe.wait_ge(s["norm_ready"], NT * b + t + 1)
                    mm = nc.tensor.transpose(misc[:, t * P:(t + 1) * P], xn[:, t, :], ident)
                mm.then_inc(s["normT_ready"], 1)
                pe.wait_ge(s["normT_copied"], b + 1)
                if ph == "a":
                    project_a(b)
                else:
                    project_b(b)
                pe.wait_ge(s["stacked"], NSTACK * 16 * (b + 1))
                n = 0
                for g in range(GROUPS):
                    for i, unit in enumerate(units[ph]):
                        score_unit(ph, b, g, unit, n)
                        n += 1
                        if i == MAX_DELAY - 1 and g > 0:
                            transpose_max(ph, b, g - 1)
                transpose_max(ph, b, GROUPS - 1)
                n = 0
                for g in range(GROUPS):
                    pe.wait_ge(s["maxrows"][g // 2], 2 * 3 * 16 * (b + 1))
                    for kp in range(2):
                        for h in range(4):
                            prob_unit(ph, b, g, kp, h, n)
                            n += 1
                            if h == 1 and n > 4:
                                weighted_sum(ph, b, 2 * g + kp - 1)
                weighted_sum(ph, b, 2 * GROUPS - 1)
                pe.wait_ge(s["o_copied"], GROUPS * b + GROUPS + 1)
                for t in range(NT):
                    if t:
                        pe.wait_ge(s["onorm_ready"], NT * b + t)
                    for g in range(GROUPS):
                        mm = nc.tensor.transpose(misc[:, g * P:(g + 1) * P], oT[:, g, t * P:(t + 1) * P], ident)
                    mm.then_inc(s["oT_ready"], 1)
                pe.wait_ge(s["onorm_ready"], NT * b + NT)
                for t in range(NT):
                    mm = nc.tensor.transpose(misc[:, t * P:(t + 1) * P], onorm[:, t, :], ident)
                mm.then_inc(s["onormT_ready"], 1)
                pe.wait_ge(s["onormT_copied"], b + 1)
                for t in range(NT):
                    mm = nc.tensor.matmul(misc[:, t * D:(t + 1) * D], onormT[:, t * P:(t + 1) * P],
                                          (wao if ph == "a" else wbo)[:], start=True, stop=True)
                mm.then_inc(s["oproj_ready"], 1)
                for t in range(NT):
                    pe.wait_ge(s["norm2_ready"], NT * b + t + 1)
                    mm = nc.tensor.transpose(misc[:, t * P:(t + 1) * P], xn2[:, t, :], ident)
                mm.then_inc(s["norm2T_ready"], 1)
                pe.wait_ge(s["norm2T_copied"], b + 1)
                for t in range(NT):
                    mm = nc.tensor.matmul(misc[:, t * E:(t + 1) * E], xn2T[:, t * P:(t + 1) * P], router[:],
                                          start=True, stop=True)
                mm.then_inc(s["logits_ready"], 1)
                pe.wait_ge(s["tops_ready"], b + 1)
                for t in range(NT + 1):
                    for u in range(min(t + 1, NT)):
                        mm = nc.tensor.matmul(misc[:, t * E:(t + 1) * E], before if u == t else ones_bf,
                                              tops_bf[:, u, :], start=u == 0, stop=u == min(t, NT - 1))
                mm.then_inc(s["rank_ready"], 1)

            def experts(n):
                r0 = n * ROUNDS
                pe.wait_ge(f["table"], n + 1)

                def rows(i, k, start):
                    pe.wait_ge(f["gathered"][k % 4], 16 * (2 * (i + r0) + k // 4 + 1))
                    if not start:
                        pe.wait_ge(f["xT_copied"], ROUND * (i + r0) + k)
                    nc.tensor.transpose(ps[:, 6, 0:P], xg[:, k % 4, :], ident).then_inc(f["xT_ready"], 1)

                def up(i, k, start):
                    e = pe.value_load(tile_tab[0:1, 0, ds(ROUND * i + k, 1)], min_val=0, max_val=E - 1)
                    pe.wait_ge(f["xT_copied"], ROUND * (i + r0) + k + 1)
                    if not start:
                        pe.wait_ge(f["h_copied"], ROUND * (i + r0) + k - 1)
                    nc.tensor.matmul(ps[:, k % 2, :], xgT[:, k % 2, :], w1[:, ds(e * FF, FF)],
                                     start=True, stop=True).then_inc(f["h_ready"], 1)

                def turn(i, k):
                    pe.wait_ge(f["h_copied"], ROUND * (i + r0) + k + 1)
                    for j in range(NF):
                        mm = nc.tensor.transpose(ps[:, 2 + k % 2, j * P:(j + 1) * P],
                                                 hid[:, k % 2, j * P:(j + 1) * P], ident)
                    mm.then_inc(f["hT_ready"], 1)

                def down(i, k, start):
                    e = pe.value_load(tile_tab[0:1, 0, ds(ROUND * i + k, 1)], min_val=0, max_val=E - 1)
                    pe.wait_ge(f["hT_copied"], ROUND * (i + r0) + k + 1)
                    if not start:
                        pe.wait_ge(f["y_copied"], ROUND * (i + r0) + k)
                    for j in range(NF):
                        mm = nc.tensor.matmul(ps[:, 4, 0:P], hidT[:, k % 2, j, :], w2[:, ds(e * FF + j * P, P)],
                                              start=j == 0, stop=j == NF - 1)
                    mm.then_inc(f["y_ready"], 1)

                for k in range(ROUND):
                    rows(0, k, k == 0)
                    if k >= 1:
                        up(0, k - 1, k - 1 < 2)
                    if k >= 2:
                        down(0, k - 2, k == 2)
                    if k >= 1:
                        turn(0, k - 1)
                with pe.Fori(1, ROUNDS) as i:
                    for k in range(ROUND):
                        rows(i, k, False)
                        up(i - (k < 1), (k - 1) % ROUND, False)
                        down(i - (k < 2), (k - 2) % ROUND, False)
                        turn(i - (k < 1), (k - 1) % ROUND)
                end = ROUNDS - 1
                up(end, ROUND - 1, False)
                down(end, ROUND - 2, False)
                turn(end, ROUND - 1)
                down(end, ROUND - 1, False)

            pe.wait_ge(first["const"], 32)
            pe.wait_ge(first["weights"], 13 * 16)
            pe.wait_ge(first["tables"], TABLES)
            with pe.Fori(0, B) as b:
                attention("a", b)
            if stop >= 2:
                experts(0)
            if stop >= 3:
                with pe.Fori(0, B) as b:
                    attention("b", b)
            if stop >= 4:
                experts(1)


def constants():
    c = np.zeros((P, C_END), np.float32)
    c[:, C_IDENT:C_IDENT + P] = np.eye(P)
    freq = np.float32(10000.0) ** (-2.0 * np.arange(0, HD // 2, dtype=np.float32) / HD)
    angle = np.arange(S, dtype=np.float32)[None, :] * freq.astype(np.float32)[:, None]
    dim = (np.arange(P) % 64) // 8
    c[:, C_COS:C_COS + S] = np.cos(angle)[dim // 2]
    c[:, C_SIN:C_SIN + S] = np.sin(angle)[dim // 2] * np.where(dim % 2 == 0, -1, 1)[:, None]
    c[:, C_PICK:C_PICK + NT * E] = np.tile(E - np.arange(E), NT)
    c[:, C_BASE:C_BASE + NT * E] = np.tile(LIST * np.arange(E), NT)
    p, t, k, w = np.meshgrid(np.arange(P), np.arange(NT), np.arange(TOPK), np.arange(2), indexing="ij")
    c[:, C_IDS:] = (t * P + p + w * k * TOK).reshape(P, -1)
    r = np.arange(P)
    masked = np.where(r[None, :] > r[:, None], MASKED, 0)
    bf = np.stack([np.eye(P), masked, masked.T, r[:, None] < r[None, :], np.ones((P, P))], 1)
    tilepos = np.repeat(P * np.arange(TILES), E).reshape(1, TILES, E)
    return c, bf.astype(mybir.dt.np(BF16)), tilepos.astype(np.float32)


def kernel(**inputs):
    import concourse.bacc as bacc
    from concourse.bass_utils import run_bass_kernel_spmd

    v = {k: np.asarray(w) for k, w in inputs.items()}
    A, Bp, Fp = "L0_attn_a_", "L0_attn_b_", "L0_ffn_"
    par, dim, pair = np.meshgrid(np.arange(2), np.arange(HD), np.arange(H // 2), indexing="ij")
    order = (HD * (8 * par + pair) + dim).reshape(-1)
    swapped = (HD * (8 * par + pair) + (dim ^ 1)).reshape(-1)
    grouped = np.concatenate([HD * (8 * (g % 2) + 4 * (g // 2)) + np.arange(4 * HD) for g in range(GROUPS)])
    wq, wk, wv = (v[A + n].T for n in ("W_q", "W_k", "W_v"))
    consts, consts_bf, tilepos = constants()
    arrays = {
        "x": v[A + "x"].reshape(TOK, D),
        "consts": consts, "consts_bf": consts_bf, "tilepos": tilepos,
        "wa": np.stack([wq[:, order], wq[:, swapped], wk[:, order], wk[:, swapped], wv], 1),
        "wao": v[A + "W_o"].T[grouped],
        "wb": np.concatenate([v[Bp + n].T for n in ("wq_w", "wk_w", "wv_w")], 1),
        "wbo": v[Bp + "wo_w"].T[grouped],
        "bias_qkv": np.concatenate([v[Bp + n] for n in ("wq_b", "wk_b", "wv_b")]),
        "bias_o": v[Bp + "wo_b"],
        "curv": v[Bp + "curv"].reshape(1),
        "router": v[Fp + "router_w"].T,
        "w1": v[Fp + "w1"].transpose(2, 0, 1).reshape(D, E * FF),
        "b1": v[Fp + "b1"].reshape(-1),
        "w2": v[Fp + "w2"].transpose(2, 0, 1).reshape(NF, P, E, D).transpose(1, 2, 0, 3).reshape(P, E * FF),
        "b2": v[Fp + "b2"].reshape(-1),
    }
    arrays = {k: np.ascontiguousarray(w) for k, w in arrays.items()}
    nc = bacc.Bacc("TRN2", target_bir_lowering=False, num_devices=1)
    aps = {k: nc.dram_tensor("in_" + k, w.shape, mybir.dt.from_np(w.dtype), kind="ExternalInput").ap()
           for k, w in arrays.items()}
    out = nc.dram_tensor("out", (TOK, D), F32, kind="ExternalOutput").ap()
    build_program(nc, aps, out)
    r = run_bass_kernel_spmd(nc, [{"in_" + k: w for k, w in arrays.items()}], core_ids=[0])
    return r.results[0]["out"].reshape(B, S, D)
```

```python
from contextlib import ExitStack

import numpy as np
import concourse.bass as bass
from concourse import mybir
from concourse.bass import ds, IndirectOffsetOnAxis

B, S, D = 8, 512, 128
H, HD = 16, 8
P = 128
NT = S // P
E, FF, TOPK = 8, 512, 2
NF = FF // P
TOK = B * S
LIST = TOK
TILES = TOK * TOPK // P + E
ROUND = 8
ROUNDS = TILES // ROUND
BEHIND = 5
NO_LIST = E * LIST
LAYERS = 2
EPS = 1e-5
MASKED = -1e30
DVE_STEPS = {"a": (8, 42, 2), "b": (45, 43, 2)}
PIECES = {"a": 3, "b": 3}
FFN_STEPS = 24
SCALE = float(1.0 / np.sqrt(np.float32(HD)))
GROUPS = 4
JQ, JK = [0, 0, 0, 1, 1, 2], [0, 1, 2, 0, 1, 0]
MAXROW = 54
HEADROWS = 64

F32 = mybir.dt.float32
BF16 = mybir.dt.bfloat16
I32 = mybir.dt.int32
ALU = mybir.AluOpType
ACT = mybir.ActivationFunctionType
X_AXIS = mybir.AxisListType.X

UNITS = {"a": [(g, q, h, n) for g in range(2) for q, h, n in
               [(0, 0, 4), (1, 0, 2), (1, 2, 2)] + [(q, h, 1) for q in (2, 3) for h in range(4)]],
         "b": [(g, q, h, 1) for g in range(2) for q in range(NT) for h in range(4)]}
TIMES = {"a": (0.27, 0.8, 0.25, 1.2), "b": (0.27, 0.88, 0.27, 1.05)}
ROOM = {"oproj": 2, "logits": 3, "rank": 2}
QUADS = 4
EXPS = 4 * QUADS

POST = ["oT0", "oT1", "oT2", "oT3", "onormT", "oproj", "rstd2", "norm2T", "logits", "rexp"]
PREP = {"a": ["rstd", "normT", "proj0", "proj1", "proj2", "proj3"],
        "b": ["rows", "rstd", "nc", "ln", "normT", "proj0", "proj1", "square", "root", "sinh", "time",
              "hypT0", "hypT1", "hypT2", "hypT3"]}


def order(ph, e, s, early, side):
    n = len(UNITS[ph]) + 1
    start, end, side_start, side_end = TIMES[ph] if e else (0.0, 1.0, 0.0, 1.0)
    items = [((i + 0.5) / EXPS, ("e", i)) for i in range(EXPS if e else 0)]
    items += [(start + (end - start) * (i + 0.5) / n, ("s", i)) for i in range(n if s else 0)]
    items += [(0.16, ("side", name)) for name in early]
    room = [ROOM.get(name, 1) for name in side]
    items += [(side_start + (side_end - side_start) * (sum(room[:i]) + 0.5) / sum(room), ("side", name))
              for i, name in enumerate(side)]
    return [item for _, item in sorted(items, key=lambda it: it[0])]


def first_order(ph, prev, nxt):
    return order(ph, True, True, ["vcopy1"], (POST if prev else []) + (["vproj"] if nxt else []))


def second_order(ph, prev, nxt, nxt2, e=True):
    return order(ph, e, nxt, ["vcopy0"] if nxt else [], (["rank"] if prev else []) + (PREP[ph] if nxt2 else []))


C_IDENT, C_COS, C_SIN, C_PICK, C_BASE, C_IDS = 0, 128, 640, 1152, 1184, 1216
C_END = 1232


def build_program(nc, a, out, stop=9):
    ctx = ExitStack()
    with ctx:
        def sb(name, shape, dt=F32):
            return ctx.enter_context(nc.sbuf_tensor(name, shape, dt))

        def sem(name):
            return ctx.enter_context(nc.semaphore(name))

        def sems(prefix, names):
            return {n: sem(prefix + n) for n in names.split()}

        xn_dram = nc.dram_tensor("xn_rows", [TOK + P, D], F32, kind="Internal").ap()
        list_dram = nc.dram_tensor("expert_lists", [E * LIST + P, 2], I32, kind="Internal").ap()
        y_dram = nc.dram_tensor("expert_rows", [TOPK * TOK, D], F32, kind="Internal").ap()
        stack_dram = nc.dram_tensor("part_blocks", [2 * len(JQ) * 16 * (HD + 1), S], BF16, kind="Internal").ap()

        x = sb("x", [P, B * NT, D])
        const = sb("const", [P, C_END])
        ident = const[:, C_IDENT:C_IDENT + P]
        cos_t, sin_t = const[:, C_COS:C_COS + S], const[:, C_SIN:C_SIN + S]
        pick = const[:, C_PICK:C_PICK + NT * E].rearrange("p (t e) -> p t e", e=E)
        listbase = const[:, C_BASE:C_BASE + NT * E].rearrange("p (t e) -> p t e", e=E)
        tilepos = sb("tilepos", [1, TILES, E])
        cbf = sb("cbf", [P, 5, P], BF16)
        ident_bf, mask_s, mask_t, before, ones_bf = (cbf[:, i, :] for i in range(5))
        half = sb("half", [P, NT * 2 * H])
        neghalf = sb("neghalf", [P, NT])
        wa = sb("wa", [P, 5, D])
        wao = sb("wao", [P, D])
        wb = sb("wb", [P, 3 * D])
        wbo = sb("wbo", [P, D])
        bias_qkv = sb("bias_qkv", [P, 3 * D])
        bias_o = sb("bias_o", [P, D])
        curv = sb("curv", [P, 1])
        inv_curv = sb("inv_curv", [P, 1])
        router = sb("router", [P, E])
        w1 = sb("w1", [P, E * FF])
        w2 = sb("w2", [P, E * FF])
        b1 = sb("b1", [P, E * FF])
        b2 = sb("b2", [P, E * D])

        stats = sb("stats", [P, 2, NT, 6])
        moments = sb("moments", [P, 2, NT, 2])
        var_eps = sb("var_eps", [P, 2, NT])
        rstd = sb("rstd", [P, 2, NT])
        xn = sb("xn", [P, NT, D])
        xnT = sb("xnT", [P, S])
        qk = const[:, C_COS:C_COS + 2 * S]
        hyp = sb("hyp", [P, NT * 4 * 2, 9 * 4])
        hyp_flat = hyp[:].rearrange("p m r -> p (m r)")
        qk_sq = hyp_flat[:, 0:2 * S]
        ystage = hyp_flat[:, 0:TOPK * S].rearrange("p (k t d) -> p k t d", k=TOPK, t=NT)
        work = sb("work", [P, 4, S])
        hypT = work[0:72, :, :]
        qrot = work[:, 0:2, :]
        rope_c, rope_s = work[:, 2, :], work[:, 3, :]
        oT = sb("oT", [P, GROUPS, S])
        one_bf = oT[0:3, :, :].rearrange("p c n -> p (c n)").bitcast(BF16)[:, 0:8 * S]
        parts = sb("parts", [P, 3, 4 * S], BF16)
        qstack = sb("qstack", [P, 8, S], BF16)
        kstack = sb("kstack", [P, H, S], BF16)
        vstage = sb("vstage", [P, NT, D])
        vones = sb("vones", [P, NT, H, 16])
        negmax = sb("negmax", [P, 2, 2 * 4 * NT])
        maxrest = sb("maxrest", [32, P])
        maxparts = sb("maxparts", [32, 2, 3, P], BF16)
        shared = sb("shared", [P, 2 * 4 * 2 * S])
        probs = shared[:].rearrange("p (a h n) -> p a h n", a=2, h=4)
        rsum = sb("rsum", [P, H])
        onorm = sb("onorm", [P, NT, D])
        onormT = sb("onormT", [P, S])
        xn2 = sb("xn2", [P, NT, D])
        xn2T = sb("xn2T", [P, S])
        rt = sb("rt", [P, 11, NT, E])
        rk = sb("rk", [P, 12, NT])
        lm = sb("lm", [P, 12, NT])
        lm_small = sb("lm_small", [P, NT], I32)
        em = sb("em", [P, 8, NT * 2 * H])
        em_small = sb("em_small", [P, NT * 2 * H], I32)
        tops_bf = sb("tops_bf", [P, NT, E], BF16)
        counts = sb("counts", [P, E])
        gates = sb("gates", [P, B * NT, TOPK])
        ids = sb("ids", [P, NT * TOPK * 2])
        entries = sb("entries", [P, NT, TOPK, 2], I32)
        slots = sb("slots", [P, TOPK, NT], I32)

        list_fill = sb("list_fill", [P, 2 * LIST * E // P], I32)
        lay = sb("lay", [P, 8, E])
        lay_i = sb("lay_i", [P, 2, E], I32)
        tile_f = sb("tile_f", [1, 2, TILES])
        tile_tab = sb("tile_tab", [1, 2, TILES], I32)
        entry = sb("entry", [P, ROUND, 2], I32)
        def view(at, *shape):
            names = "abc"[:len(shape)]
            n = int(np.prod(shape))
            return shared[:, at:at + n].rearrange(f"p ({' '.join(names)}) -> p {' '.join(names)}",
                                                  **dict(zip(names, shape)))

        last_rows = shared[:].rearrange("p (b k t d) -> p b k t d", b=B, k=TOPK, t=NT)
        xg = view(0, 4, D)
        xgT = view(512, 2, P)
        hid = view(768, 2, FF)
        hidT = view(1792, 2, NF, P)
        yrow = view(2816, 4, D)
        tl = view(3328, 4, TILES, E)[0:1]

        ps = ctx.enter_context(nc.psum_tensor("ps", [P, 8, 512], F32))
        misc = ps[:, 7, :]
        outT = ps[:, 6, :]

        def misc4(w):
            return misc[:, 0:4 * w].rearrange("p (t n) -> p t n", n=w)

        first = sems("init_", "x const weights tables ready clear emptied")
        ATT = ("dve_prep dve_post dve_max pool norm_var norm_rstd norm_ready normT_ready normT_copied "
               "proj_ready proj_read v_ready v_staged v_spread part_ready parts_written scores_ready "
               "max_done maxparts_ready exp_in exp_done pv_ready o_copied oT_ready onorm_ready "
               "onormT_ready onormT_copied oproj_ready post_read norm2_var norm2_rstd norm2_ready "
               "norm2T_ready norm2T_copied logits_ready route_exp_in route_exp tops_ready "
               "rank_ready entries_ready entries_free scattered rows_stored rows_free ")
        att = {"a": sems("a_", ATT + "rot_ready"),
               "b": sems("b_", ATT + "nc_in nc_ready ln_in ln_ready norm_in norm_out exp_sh time_in "
                         "log_done root_ready time_out time_ready hyp_ready hypT_ready hypT_copied y_loaded combined square_done")}
        for ph in "ab":
            att[ph]["maxrows"] = [sem(f"{ph}_maxrows{half}") for half in range(2)]
            att[ph]["stacked"] = [sem(f"{ph}_stacked{half}") for half in range(2)]
        FFN = ("dve table xT_ready xT_copied h_ready h_copied hT_ready hT_copied "
               "y_ready y_copied")
        f = sems("f_", FFN)
        f["entry"] = [sem(f"f_entry{k}") for k in range(ROUND)]
        f["gathered"] = [sem(f"f_gathered{k}") for k in range(4)]
        f["scattered"] = [sem(f"f_scattered{k}") for k in range(4)]
        last = sems("end_", "combined stored dve final_step")
        last_loaded = f["entry"]

        STACKED = 6 * 16
        WRITTEN = 2 * len(JQ) * 16
        SCORES = {ph: len(UNITS[ph]) + 1 for ph in "ab"}

        def first_tile(g):
            return 4 * (g // 2)

        def first_head(g):
            return 8 * (g % 2) + first_tile(g)

        def spans(ph, kp):
            if ph == "b":
                return [(2 * kp, 0, 0), (2 * kp + 1, 0, S)]
            k0, k1 = 2 * kp, 2 * kp + 1
            return [(k0, k0 * P, 0), (k1, k1 * P, S - k0 * P)]

        def width(ph, kp):
            kt, q0, c0 = spans(ph, kp)[-1]
            return c0 + S - q0

        def plain(eng):
            eng.sem_inc(carried[eng], 1)

        class Chain:
            def __init__(self, eng, semaphore, per_round):
                self.eng, self.sem, self.per_round = eng, semaphore, per_round

            def round(self, r):
                self.base, self.n = r * self.per_round, 0

            def link(self, ins):
                self.mark(ins)
                self.settle()

            def mark(self, ins):
                ins.then_inc(self.sem, 1)
                self.n += 1

            def settle(self):
                self.eng.wait_ge(self.sem, self.base + self.n)

            def end(self):
                assert self.n == self.per_round, (self.sem, self.n)

        def last_parts(ph, c):
            return 3 * c + 3

        TABLES = 10

        carried = {eng: sem("carried_" + name) for eng, name in ((nc.vector, "dve"), (nc.gpsimd, "pool"))}

        block = ctx.enter_context(nc.Block())

        @block.sync
        def _(sp):
            for ph in "ab":
                sp.sem_inc(att[ph]["rows_free"], 1)
            sp.dma_start(x[:], a["x"].rearrange("(n p) d -> p n d", p=P)).then_inc(first["x"], 16)
            sp.dma_start(const[:], a["consts"]).then_inc(first["const"], 16)
            sp.dma_start(wa[:], a["wa"]).then_inc(first["const"], 16)
            sp.dma_start(cbf[:], a["consts_bf"]).then_inc(first["const"], 16)
            sp.wait_ge(first["tables"], TABLES)
            for par in range(2):
                r = HEADROWS * par + MAXROW
                sp.dma_start(kstack[r:r + 3, 8 * par:8 * par + 8, :],
                             one_bf).then_inc(first["ready"], 16)
            sp.dma_start(wao[:], a["wao"]).then_inc(first["ready"], 16)
            sp.dma_start(router[:], a["router"]).then_inc(first["ready"], 16)
            sp.dma_start(curv[:], a["curv"].partition_broadcast(P)).then_inc(first["ready"], 16)
            sp.dma_start(xn_dram[TOK:TOK + P, :].rearrange("(p n) d -> p (n d)", n=1),
                         onormT[:, 0:D]).then_inc(first["ready"], 16)

            def later_loads():
                sp.dma_start(list_dram[0:NO_LIST, :].rearrange("(p n) c -> p (n c)", p=P),
                             list_fill[:]).then_inc(first["emptied"], 16)
                sp.dma_start(list_dram[NO_LIST:NO_LIST + P, :],
                             list_fill[:, 0:2]).then_inc(first["emptied"], 16)
                sp.dma_start(wb[:], a["wb"]).then_inc(first["weights"], 16)
                sp.dma_start(wbo[:], a["wbo"]).then_inc(first["weights"], 16)
                sp.dma_start(bias_qkv[:], a["bias_qkv"].partition_broadcast(P)).then_inc(first["weights"], 16)
                sp.dma_start(bias_o[:], a["bias_o"].partition_broadcast(P)).then_inc(first["weights"], 16)
                sp.dma_start(tilepos[:], a["tilepos"]).then_inc(first["weights"], 16)
                sp.dma_start(w1[:], a["w1"]).then_inc(first["weights"], 16)
                sp.dma_start(w2[:], a["w2"]).then_inc(first["weights"], 16)
                sp.dma_start(b1[:], a["b1"].partition_broadcast(P)).then_inc(first["weights"], 16)
                sp.dma_start(b2[:], a["b2"].partition_broadcast(P)).then_inc(first["weights"], 16)

            def load_rows(c, start):
                s = att["b"]
                if not start:
                    sp.wait_ge(s["hypT_ready"], 4 * c)
                for k in range(TOPK):
                    sp.dma_start(ystage[:, k, :, :],
                                 y_dram[ds(c * S + k * TOK, S), :].rearrange(
                                     "(t p) d -> p t d", p=P)).then_inc(s["y_loaded"], 16)

            def write_parts(ph, c, start):
                s = att[ph]
                nd = HD + (ph == "b")
                if not start:
                    for half in range(2):
                        sp.wait_ge(s["stacked"][half], STACKED * c)
                for j in range(3):
                    sp.wait_ge(s["part_ready"], last_parts(ph, c) + j + 1)
                    for side, js in enumerate((JQ, JK)):
                        for i in range(len(JQ)):
                            if js[i] != j:
                                continue
                            at = (side * len(JQ) + i) * 16 * nd
                            dst = stack_dram[at:at + 16 * nd, :]
                            if ph == "a":
                                src = parts[:, j, side * S:(side + 1) * S]
                            else:
                                dst = dst.rearrange("(c r) n -> r c n", c=2)
                                src = parts[0:72, j, 2 * side * S:2 * (side + 1) * S].rearrange(
                                    "p (c n) -> p c n", c=2)
                            sp.dma_start(dst, src).then_inc(s["parts_written"], 16)

            def stack(ph, c, half, start):
                s = att[ph]
                nd = HD + (ph == "b")
                if not start:
                    sp.wait_ge(s["exp_in"], 2 * EXPS * (c - 1) + EXPS * (half + 1))
                for par in range(2):
                    r = HEADROWS * par + MAXROW
                    h0 = 8 * par + 4 * half
                    sp.dma_start(qstack[r:r + 3, 4 * half:4 * half + 4, :],
                                 kstack[r + 3:r + 6, h0:h0 + 4, :]).then_inc(s["stacked"][half], 16)
                sp.wait_ge(s["parts_written"], WRITTEN * (c + 1))
                for side in range(2):
                    n = len(JQ) * 16 * nd
                    blocks = stack_dram[side * n:(side + 1) * n, :].rearrange(
                        "(i q d t) n -> q i d t n", i=len(JQ), q=4, t=4)
                    for par in range(2):
                        r = HEADROWS * par
                        if side == 0:
                            dst = qstack[r:r + len(JQ) * nd, 4 * half:4 * half + 4, :]
                        else:
                            dst = kstack[r:r + len(JQ) * nd, 8 * par + 4 * half:8 * par + 4 * half + 4, :]
                        sp.dma_start(dst, blocks[2 * par + half]).then_inc(s["stacked"][half], 16)

            def max_rows(ph, c, half):
                s = att[ph]
                sp.wait_ge(s["maxparts_ready"], 2 * c + half + 1)
                for j in range(3):
                    r = MAXROW + j
                    sp.dma_start(qstack[r:r + HEADROWS + 1:HEADROWS, 4 * half:4 * half + 4, :].rearrange(
                        "j t (q n) -> j (t q) n", n=P), maxparts[:, half, j, :]).then_inc(s["maxrows"][half], 16)

            def store_rows(ph, c):
                s = att[ph]
                sp.wait_ge(s["norm2_ready"], NT * c + NT)
                sp.dma_start(xn_dram[ds(c * S, S), :].rearrange("(t p) d -> p t d", p=P),
                             xn2[:]).then_inc(s["rows_stored"], 16)

            def rows_are_stored(ph, c):
                s = att[ph]
                sp.wait_ge(s["rows_stored"], 16 * c + 16)
                sp.sem_inc(s["rows_free"], 1)

            def batch(ph, b, prev, nxt, nxt2):
                if nxt2 and ph == "b":
                    load_rows(b + 2, False)
                if nxt:
                    write_parts(ph, b + 1, False)
                if prev:
                    store_rows(ph, b - 1)
                max_rows(ph, b, 1)
                if nxt:
                    stack(ph, b + 1, 0, False)
                if prev:
                    rows_are_stored(ph, b - 1)
                if nxt:
                    max_rows(ph, b + 1, 0)
                    stack(ph, b + 1, 1, False)

            def before(ph):
                if ph == "b":
                    load_rows(0, True)
                write_parts(ph, 0, True)
                if ph == "b":
                    load_rows(1, False)
                stack(ph, 0, 0, True)
                stack(ph, 0, 1, True)
                max_rows(ph, 0, 0)
                if ph == "a":
                    later_loads()

            def attention(ph):
                before(ph)
                batch(ph, 0, False, True, True)
                with sp.Fori(1, B - 2) as b:
                    batch(ph, b, True, True, True)
                batch(ph, B - 2, True, True, False)
                batch(ph, B - 1, True, False, False)
                store_rows(ph, B - 1)
                rows_are_stored(ph, B - 1)

            def experts(n):
                r0 = n * ROUNDS
                sp.wait_ge(f["table"], n + 1)
                sp.wait_ge(att["ab"[n]]["scattered"], B * NT * TOPK * 16)

                def load_entries(i, k, first_round):
                    slot = sp.value_load(tile_tab[0:1, 1, ds(ROUND * i + k, 1)], min_val=0, max_val=NO_LIST)
                    if not first_round:
                        sp.wait_ge(f["scattered"][k % 4], 16 * (2 * (i + r0 - 1) + k // 4 + 1))
                    sp.dma_start(entry[:, k, :], list_dram[ds(slot, P), :]).then_inc(f["entry"][k], 16)

                for k in range(ROUND):
                    load_entries(0, k, True)
                with sp.Fori(1, ROUNDS) as i:
                    for k in range(ROUND):
                        load_entries(i, k, False)

            def rows_written(n):
                for k in range(4):
                    sp.wait_ge(f["scattered"][k], 16 * (n + 1) * TILES // 4)

            sp.wait_ge(first["ready"], 6 * 16)
            attention("a")
            if stop >= 2:
                experts(0)
            if stop >= 3:
                rows_written(0)
                sp.dma_start(list_dram[0:NO_LIST, :].rearrange("(p n) c -> p (n c)", p=P),
                             list_fill[:]).then_inc(first["emptied"], 16)
                attention("b")
            if stop >= 4:
                experts(1)
            if stop in (1, 3):
                sp.wait_ge(last["combined"], B)
                sp.dma_start(out.rearrange("(n p) d -> p n d", p=P), x[:]).then_inc(last["stored"], 16)
                sp.wait_ge(last["stored"], 16)
            else:
                rows_written(1 if stop >= 4 else 0)
                for b in range(B):
                    for k in range(TOPK):
                        sp.dma_start(last_rows[:, b, k, :, :],
                                     y_dram[b * S + k * TOK:(b + 1) * S + k * TOK, :].rearrange(
                                         "(t p) d -> p t d", p=P)).then_inc(last_loaded[b], 16)
                for b in range(B):
                    sp.wait_ge(last["combined"], b + 1)
                    sp.dma_start(out[b * S:(b + 1) * S, :].rearrange("(t p) d -> p t d", p=P),
                                 x[:, b * NT:(b + 1) * NT, :]).then_inc(last["stored"], 16)
                sp.wait_ge(last["stored"], 16 * B)

        @block.gpsimd
        def _(pool):
            nc.gpsimd.memset(one_bf, 1.0).then_inc(first["tables"], 1)
            nc.gpsimd.iota(list_fill[:].rearrange("p (r n c) -> p r n c", n=P, c=2),
                           [[0, 2 * LIST * E // P // P // 2], [1, P], [TOK, 2]], base=TOK,
                           channel_multiplier=0).then_inc(first["tables"], 1)
            pool.sem_inc(att["a"]["entries_free"], 1)
            pool.sem_inc(att["b"]["entries_free"], 1)
            for ph in "ab":
                pool.sem_inc(att[ph]["part_ready"], 3)

            def rstd_of(ph, which, c, have, done):
                s = att[ph]
                pool.wait_ge(s[have], c + 1)
                nc.gpsimd.tensor_tensor(rstd[:, which, :], var_eps[:, which, :], neghalf[:],
                                        ALU.pow).then_inc(s[done], 1)

            def log_roots(c):
                s = att["b"]
                pool.wait_ge(s["nc_in"], c + 1)
                nc.gpsimd.tensor_tensor(lm[:, 2:4, :], lm[:, 0:2, :],
                                        half[:, 0:2 * NT].rearrange("p (a t) -> p a t", t=NT),
                                        ALU.pow).then_inc(s["nc_ready"], 1)

            def split(ph, c, start):
                s = att[ph]
                chain = pool_chain[ph]
                chain.round(c)
                if ph == "b":
                    pool.wait_ge(s["hypT_copied"], 4 * c + 4)
                    pool.wait_ge(s["part_ready"], last_parts(ph, c) + 1)
                    src, n, w = hypT.rearrange("p c n -> p (c n)"), 72, 4 * S
                else:
                    pool.wait_ge(s["rot_ready"], 2 * c + 2)
                    src, n, w = qrot.rearrange("p c n -> p (c n)"), P, 2 * S
                if not start:
                    pool.wait_ge(s["parts_written"], WRITTEN * c)
                if ph == "a":
                    plain(pool)
                    nc.gpsimd.tensor_copy(parts[0:n, 0, 0:w], src).then_inc(s["part_ready"], 1)
                    pool.wait_ge(s["part_ready"], last_parts(ph, c) + 1)
                chain.link(nc.gpsimd.tensor_tensor(src, src, parts[0:n, 0, 0:w], ALU.subtract))
                plain(pool)
                nc.gpsimd.tensor_copy(parts[0:n, 1, 0:w], src).then_inc(s["part_ready"], 1)
                yield
                pool.wait_ge(s["part_ready"], last_parts(ph, c) + 2)
                nc.gpsimd.tensor_tensor(parts[0:n, 2, 0:w], src, parts[0:n, 1, 0:w],
                                        ALU.subtract).then_inc(s["part_ready"], 1)
                chain.end()

            def scatter_entries(ph, c):
                s = att[ph]
                pool.wait_ge(s["entries_ready"], c + 1)
                plain(pool)
                for t in range(NT):
                    for k in range(TOPK):
                        nc.gpsimd.indirect_dma_start(
                            list_dram[:, :], IndirectOffsetOnAxis(slots[:, k, t:t + 1], 0),
                            entries[:, t, k, :], None).then_inc(s["scattered"], 16)

            def entries_are_scattered(ph, c):
                s = att[ph]
                pool.wait_ge(s["scattered"], (c + 1) * NT * TOPK * 16)
                pool.sem_inc(s["entries_free"], 1)

            def batch(ph, b, prev, nxt, nxt2):
                if nxt:
                    parting = split(ph, b + 1, False)
                    next(parting)
                if prev:
                    rstd_of(ph, 1, b - 1, "norm2_var", "norm2_rstd")
                if nxt:
                    next(parting, None)
                if nxt2:
                    rstd_of(ph, 0, b + 2, "norm_var", "norm_rstd")
                    if ph == "b":
                        log_roots(b + 2)
                if prev:
                    scatter_entries(ph, b - 1)
                if prev:
                    entries_are_scattered(ph, b - 1)

            def attention(ph):
                for c in range(2):
                    rstd_of(ph, 0, c, "norm_var", "norm_rstd")
                    if ph == "b":
                        log_roots(c)
                    if c == 0:
                        for _ in split(ph, 0, True):
                            pass
                pool.wait_ge(first["emptied"], 2 * 16 if ph == "a" else 3 * 16)
                batch(ph, 0, False, True, True)
                with pool.Fori(1, B - 2) as b:
                    batch(ph, b, True, True, True)
                batch(ph, B - 2, True, True, False)
                batch(ph, B - 1, True, False, False)
                rstd_of(ph, 1, B - 1, "norm2_var", "norm2_rstd")
                scatter_entries(ph, B - 1)
                entries_are_scattered(ph, B - 1)

            pool_chain = {"a": Chain(pool, att["a"]["pool"], 1), "b": Chain(pool, att["b"]["pool"], 1)}

            def experts(n):
                r0 = n * ROUNDS

                def gather(i, k, start):
                    pool.wait_ge(f["entry"][k], 16 * (i + r0) + 16)
                    if not start:
                        pool.wait_ge(f["xT_ready"], ROUND * (i + r0) + k - 3)
                        plain(pool)
                    nc.gpsimd.indirect_dma_start(
                        xg[:, k % 4, :], None, xn_dram[:, :],
                        IndirectOffsetOnAxis(entry[:, k, 0:1], 0)).then_inc(f["gathered"][k % 4], 16)

                def scatter(i, k):
                    pool.wait_ge(f["y_copied"], ROUND * (i + r0) + k + 1)
                    plain(pool)
                    nc.gpsimd.indirect_dma_start(
                        y_dram[:, :], IndirectOffsetOnAxis(entry[:, k, 1:2], 0), yrow[:, k % 4, :], None,
                        bounds_check=TOPK * TOK - 1, oob_is_err=False).then_inc(f["scattered"][k % 4], 16)

                for k in range(ROUND):
                    gather(0, k, k < 4)
                    if k >= BEHIND:
                        scatter(0, k - BEHIND)
                with pool.Fori(1, ROUNDS) as i:
                    for k in range(ROUND):
                        gather(i, k, False)
                        scatter(i - (k < BEHIND), (k - BEHIND) % ROUND)
                for k in range(ROUND - BEHIND, ROUND):
                    scatter(ROUNDS - 1, k)

            pool.wait_ge(first["tables"], TABLES)
            attention("a")
            if stop >= 2:
                experts(0)
            if stop >= 3:
                attention("b")
            if stop >= 4:
                experts(1)

        @block.scalar
        def _(act):
            for ph in "ab":
                act.sem_inc(att[ph]["exp_done"], 2)
                act.sem_inc(att[ph]["o_copied"], 1)
                act.sem_inc(att[ph]["v_spread"], 2)

            def exponential(ph, b, half, i):
                s = att[ph]
                quad, h = divmod(i, 4)
                kp = quad % 2
                quad += QUADS * half
                n = 4 * quad + h
                if h == 0:
                    act.wait_ge(s["pv_ready"], 2 * QUADS * b + quad + 1)
                act.wait_ge(s["exp_in"], 2 * EXPS * b + n + 1)
                w = width(ph, kp)
                st = ps[:, 2 + 2 * (n % 2):4 + 2 * (n % 2), :].rearrange("p a n -> p (a n)")
                nc.scalar.activation(probs[:, quad % 2, h, 0:w], st[:, 0:w], ACT.Exp,
                                     scale=SCALE).then_inc(s["exp_done"], 1)

            def copy_out(ph, b, g, prev=False):
                s = att[ph]
                if g == 0 and prev:
                    act.wait_ge(s["oT_ready"], NT * b)
                act.wait_ge(s["pv_ready"], 2 * QUADS * b + 2 * g + 2 + 2)
                nc.scalar.copy(oT[:, g, :], outT).then_inc(s["o_copied"], 1)

            def spread_v(ph, c, half, start):
                s = att[ph]
                act.wait_ge(s["v_staged"], c + 1)
                if not start:
                    act.wait_ge(s["pv_ready"], 2 * QUADS * (c - 1) + QUADS * (half + 1) + 2)
                for par in range(2):
                    h0 = 8 * par + 4 * half
                    ins = nc.scalar.copy(vones[:, :, h0:h0 + 4, 0:HD],
                                         vstage[:, :, h0 * HD:(h0 + 4) * HD].rearrange("p t (h d) -> p t h d", d=HD))
                ins.then_inc(s["v_spread"], 1)

            def side(ph, name, b, start=False):
                s = att[ph]
                if name == "vcopy0":
                    spread_v(ph, b + 1, 0, start)
                if name == "vcopy1":
                    spread_v(ph, b, 1, start)
                if name == "onormT":
                    act.wait_ge(s["onormT_ready"], b)
                    nc.scalar.copy(onormT[:], misc).then_inc(s["onormT_copied"], 1)
                if name == "norm2T":
                    act.wait_ge(s["norm2T_ready"], b)
                    nc.scalar.copy(xn2T[:], misc).then_inc(s["norm2T_copied"], 1)
                if name == "rexp":
                    act.wait_ge(s["route_exp_in"], b)
                    nc.scalar.activation(rt[:, 9, :, :], rt[:, 8, :, :], ACT.Exp).then_inc(s["route_exp"], 1)
                if name == "vproj" and ph == "a":
                    act.wait_ge(s["v_ready"], b + 2)
                    act.wait_ge(s["v_spread"], 2 * (b + 2))
                    nc.scalar.copy(vstage[:], misc4(D)).then_inc(s["v_staged"], 1)
                if name == "ln":
                    act.wait_ge(s["ln_in"], b + 3)
                    nc.scalar.activation(lm[:, 5, :], lm[:, 4, :], ACT.Ln).then_inc(s["ln_ready"], 1)
                if name == "normT":
                    act.wait_ge(s["normT_ready"], b + 3)
                    nc.scalar.copy(xnT[:], misc).then_inc(s["normT_copied"], 1)
                if name == "square":
                    act.wait_ge(s["proj_read"], 2 * (b + 3))
                    nc.scalar.activation(qk_sq, qk, ACT.Square).then_inc(s["square_done"], 1)
                if name == "root":
                    act.wait_ge(s["norm_in"], b + 3)
                    nc.scalar.activation(em[:, 2, :], em[:, 0, :], ACT.Ln).then_inc(s["log_done"], 1)
                    act.wait_ge(s["log_done"], 2 * (b + 2) + 1)
                    nc.scalar.activation(em[:, 1, :], em[:, 2, :], ACT.Exp, scale=0.5).then_inc(s["norm_out"], 1)
                if name == "sinh":
                    act.wait_ge(s["root_ready"], b + 3)
                    nc.scalar.activation(em[:, 2, :], em[:, 1, :], ACT.Exp, scale=0.5).then_inc(s["exp_sh"], 1)
                    nc.scalar.activation(em[:, 3, :], em[:, 1, :], ACT.Exp, scale=-0.5).then_inc(s["exp_sh"], 1)
                if name == "time":
                    act.wait_ge(s["time_in"], b + 3)
                    nc.scalar.activation(em[:, 2, :], em[:, 6, :], ACT.Ln).then_inc(s["log_done"], 1)
                    act.wait_ge(s["log_done"], 2 * (b + 2) + 2)
                    nc.scalar.activation(em[:, 1, :], em[:, 2, :], ACT.Exp, scale=0.5).then_inc(s["time_out"], 1)
                if name[:4] == "hypT":
                    i = int(name[4])
                    act.wait_ge(s["hypT_ready"], 4 * (b + 2) + i + 1)
                    if i == 0:
                        act.wait_ge(s["part_ready"], last_parts(ph, b + 2))
                        if not start:
                            act.wait_ge(s["parts_written"], WRITTEN * (b + 2))
                    cast = nc.scalar.copy(parts[0:72, 0, i * S:(i + 1) * S], misc[0:72, :])
                    if i == 3:
                        cast.then_inc(s["part_ready"], 1)
                    nc.scalar.copy(hypT[:, i, :], misc[0:72, :]).then_inc(s["hypT_copied"], 1)

            def part(ph, b, half, prev, sequence):
                for kind, i in sequence:
                    if kind == "e":
                        exponential(ph, b, half, i)
                        if i == 3 and (half or prev):
                            copy_out(ph, b if half else b - 1, 1 if half else GROUPS - 1)
                        if i == EXPS // 2 + 3:
                            copy_out(ph, b, 2 * half, prev)
                    if kind == "side":
                        side(ph, i, b, start=not prev and i == "vcopy1")

            def batch(ph, b, prev, nxt, nxt2):
                part(ph, b, 0, prev, first_order(ph, prev, nxt))
                part(ph, b, 1, True, second_order(ph, prev, nxt, nxt2))

            def attention(ph):
                for name in PREP[ph]:
                    side(ph, name, -2, start=True)
                side(ph, "vproj", -1)
                for kind, name in second_order(ph, False, True, True, e=False):
                    if kind == "side":
                        side(ph, name, -1, start=name == "vcopy0")
                batch(ph, 0, False, True, True)
                with act.Fori(1, B - 2) as b:
                    batch(ph, b, True, True, True)
                batch(ph, B - 2, True, True, False)
                batch(ph, B - 1, True, False, False)
                copy_out(ph, B - 1, GROUPS - 1)
                for name in POST:
                    side(ph, name, B)

            def experts(n):
                r0 = n * ROUNDS

                def rows(i, k):
                    act.wait_ge(f["xT_ready"], ROUND * (i + r0) + k + 1)
                    nc.scalar.copy(xgT[:, k % 2, :], ps[:, 5, 0:P]).then_inc(f["xT_copied"], 1)

                def relu(i, k):
                    act.wait_ge(f["hT_ready"], ROUND * (i + r0) + k + 1)
                    nc.scalar.activation(hidT[:, k % 2, :, :], ps[:, 2 + k % 2, :].rearrange(
                        "p (f n) -> p f n", n=P), ACT.Relu).then_inc(f["hT_copied"], 1)

                for k in range(ROUND):
                    rows(0, k)
                    if k >= 1:
                        relu(0, k - 1)
                with act.Fori(1, ROUNDS) as i:
                    for k in range(ROUND):
                        rows(i, k)
                        relu(i - (k < 1), (k - 1) % ROUND)
                relu(ROUNDS - 1, ROUND - 1)

            act.wait_ge(first["tables"], TABLES)
            act.wait_ge(first["const"], 3 * 16)
            attention("a")
            if stop >= 2:
                experts(0)
            if stop >= 3:
                attention("b")
            if stop >= 4:
                experts(1)

        @block.vector
        def _(dve):
            nc.vector.memset(vones[:], 0.0).then_inc(first["clear"], 1)
            nc.vector.memset(kstack[:], 0.0).then_inc(first["tables"], 1)
            nc.vector.memset(qstack[:], 0.0).then_inc(first["tables"], 1)
            nc.vector.memset(outT, 0.0).then_inc(first["tables"], 1)
            nc.vector.memset(onormT[:], 0.0).then_inc(first["tables"], 1)
            nc.vector.memset(half[:], 0.5).then_inc(first["tables"], 1)
            nc.vector.memset(neghalf[:], -0.5).then_inc(first["tables"], 1)
            nc.vector.memset(counts[:], 0.0).then_inc(first["tables"], 1)
            dve.wait_ge(first["clear"], 1)
            nc.vector.memset(vones[:, :, :, HD:HD + 1], 1.0).then_inc(first["tables"], 1)
            dve.sem_inc(att["a"]["max_done"], 2)
            dve.sem_inc(att["b"]["max_done"], 2)

            chains = {ph: [Chain(dve, att[ph][name], n) for name, n in
                           zip(("dve_prep", "dve_post", "dve_max"), DVE_STEPS[ph])] for ph in "ab"}

            def moments_of(b, which, chain):
                plain(dve)
                for t in range(NT):
                    chain.mark(nc.vector.bn_stats(stats[:, which, t, :], x[:, ds(b * NT + t, 1), :]))
                yield None
                chain.settle()
                plain(dve)
                for t in range(NT):
                    chain.mark(nc.vector.bn_aggr(moments[:, which, t, :], stats[:, which, t, :]))
                yield None
                chain.settle()

            def add_eps(which):
                return nc.vector.tensor_scalar(var_eps[:, which, :], moments[:, which, :, 1], EPS, None, ALU.add)

            def normalised(b, t, which, dst, factor):
                return nc.vector.tensor_scalar(dst[:, t, :], x[:, ds(b * NT + t, 1), :].rearrange("p a d -> p (a d)"),
                                               moments[:, which, t, 0:1], factor[:, t:t + 1],
                                               ALU.subtract, ALU.mult)

            def add_rows(rows, b, chain, done):
                xb = x[:, ds(b * NT, NT), :]
                for k in range(TOPK):
                    g = gates[:, ds(b * NT, NT), k:k + 1].to_broadcast([P, NT, D])
                    chain.mark(nc.vector.tensor_tensor(rows[:, k, :, :], rows[:, k, :, :], g, ALU.mult))
                chain.settle()
                yield None
                chain.link(nc.vector.tensor_tensor(xb, xb, rows[:, 0, :, :], ALU.add))
                yield None
                nc.vector.tensor_tensor(xb, xb, rows[:, 1, :, :], ALU.add).then_inc(done, 1)

            def rope(c):
                s = att["a"]
                for i in range(2):
                    yield f"proj{2 * i}"
                    dve.wait_ge(s["proj_ready"], 4 * c + 2 * i + 1)
                    nc.vector.tensor_tensor(rope_c, misc, cos_t, ALU.mult).then_inc(s["proj_read"], 1)
                    yield f"proj{2 * i + 1}"
                    dve.wait_ge(s["proj_ready"], 4 * c + 2 * i + 2)
                    nc.vector.tensor_tensor(rope_s, misc, sin_t, ALU.mult).then_inc(s["proj_read"], 1)
                    yield None
                    dve.wait_ge(s["proj_read"], 4 * c + 2 * i + 2)
                    dve.wait_ge(s["part_ready"], last_parts("a", c))
                    nc.vector.tensor_tensor(qrot[:, i, :], rope_c, rope_s, ALU.add).then_inc(s["rot_ready"], 1)
                    dve.wait_ge(s["rot_ready"], 2 * c + i + 1)

            def log_map(c, chain):
                s = att["b"]
                u, u1, root, root1, arg, ln, rec, ser, coef, rr, var, scale = (lm[:, i, :] for i in range(12))
                chain.link(nc.vector.tensor_tensor(rr, rstd[:, 0, :], rstd[:, 0, :], ALU.mult))
                yield None
                chain.link(nc.vector.tensor_tensor(var, moments[:, 0, :, 1], rr, ALU.mult))
                yield None
                chain.link(nc.vector.tensor_scalar(u, var, float(D), curv[:, 0:1], ALU.mult, ALU.mult))
                nc.vector.tensor_scalar(u1, u, 1.0, None, ALU.add).then_inc(s["nc_in"], 1)
                chain.link(nc.vector.tensor_scalar(ser, u, 105.0 / 3456.0, None, ALU.mult))
                for k in (-15.0 / 336.0, 3.0 / 40.0, -1.0 / 6.0):
                    yield None
                    chain.link(nc.vector.scalar_tensor_tensor(ser, ser, k, u, ALU.add, ALU.mult))
                yield None
                chain.mark(nc.vector.tensor_scalar(ser, ser, 1.0, None, ALU.add))
                chain.mark(nc.vector.tensor_scalar(lm_small[:], u, 0.06, None, ALU.is_lt))
                yield "nc"
                dve.wait_ge(s["nc_ready"], c + 1)
                nc.vector.tensor_tensor(arg, root, root1, ALU.add).then_inc(s["ln_in"], 1)
                chain.link(nc.vector.tensor_scalar(rec, root, 1e-30, None, ALU.max))
                yield None
                chain.link(nc.vector.reciprocal(rec, rec))
                yield "ln"
                dve.wait_ge(s["ln_ready"], c + 1)
                chain.link(nc.vector.tensor_tensor(coef, ln, rec, ALU.mult))
                yield None
                plain(dve)
                chain.link(nc.vector.copy_predicated(coef, lm_small[:], ser))
                yield None
                chain.link(nc.vector.tensor_tensor(scale, coef, rstd[:, 0, :], ALU.mult))

            def exp_map(c, chain):
                s = att["b"]
                u, root, ep, en, n2, coef, t2, ser = (em[:, i, :] for i in range(8))
                yield "square"
                dve.wait_ge(s["square_done"], c + 1)
                chain.link(nc.vector.tensor_reduce(n2, qk_sq.rearrange("p (m d) -> p m d", d=HD),
                                                   axis=X_AXIS, op=ALU.add))
                yield None
                nc.vector.tensor_scalar(u, n2, curv[:, 0:1], 1e-30, ALU.mult, ALU.max).then_inc(s["norm_in"], 1)
                dve.wait_ge(s["norm_in"], c + 1)
                chain.link(nc.vector.tensor_scalar(ser, u, 1.0 / 39916800.0, None, ALU.mult))
                for k in (1.0 / 362880.0, 1.0 / 5040.0, 1.0 / 120.0, 1.0 / 6.0):
                    yield None
                    chain.link(nc.vector.scalar_tensor_tensor(ser, ser, k, u, ALU.add, ALU.mult))
                yield None
                chain.mark(nc.vector.tensor_scalar(ser, ser, 1.0, None, ALU.add))
                chain.mark(nc.vector.tensor_scalar(em_small[:], u, 1.0, None, ALU.is_lt))
                yield "root"
                dve.wait_ge(s["norm_out"], c + 1)
                chain.link(nc.vector.reciprocal(t2, root))
                yield None
                chain.link(nc.vector.tensor_tensor(t2, t2, u, ALU.mult))
                yield None
                nc.vector.tensor_tensor(root, root, t2, ALU.add).then_inc(s["root_ready"], 1)
                dve.wait_ge(s["root_ready"], c + 1)
                chain.link(nc.vector.reciprocal(t2, root))
                yield "sinh"
                dve.wait_ge(s["exp_sh"], 2 * c + 2)
                chain.link(nc.vector.tensor_tensor(ep, ep, en, ALU.subtract))
                yield None
                chain.link(nc.vector.tensor_tensor(coef, ep, t2, ALU.mult))
                yield None
                plain(dve)
                chain.link(nc.vector.copy_predicated(coef, em_small[:], ser))
                yield None
                chain.link(nc.vector.tensor_tensor(ser, coef, coef, ALU.mult))
                yield None
                chain.link(nc.vector.tensor_tensor(ser, ser, n2, ALU.mult))
                yield None
                nc.vector.tensor_scalar(t2, ser, inv_curv[:, 0:1], None, ALU.add).then_inc(s["time_in"], 1)
                kc = coef.rearrange("p (a c h) -> p a c h", a=NT, c=2)[:, :, 1, :]
                chain.link(nc.vector.tensor_scalar(kc, kc, -1.0, None, ALU.mult))
                yield None
                nc.vector.tensor_tensor(
                    hyp[:, :, 0:32].rearrange("p m (d t) -> p m t d", t=4),
                    qk.rearrange("p (m t d) -> p m t d", t=4, d=HD),
                    coef.rearrange("p (m t) -> p m t", t=4).unsqueeze(3).to_broadcast([P, NT * 8, 4, HD]),
                    ALU.mult).then_inc(s["hyp_ready"], 1)
                yield "time"
                dve.wait_ge(s["time_out"], c + 1)
                chain.link(nc.vector.reciprocal(ep, root))
                yield None
                chain.link(nc.vector.tensor_tensor(ep, ep, t2, ALU.mult))
                yield None
                chain.link(nc.vector.tensor_tensor(ep, ep, root, ALU.add))
                yield None
                nc.vector.tensor_scalar(hyp[:, :, 32:36], ep.rearrange("p (m t) -> p m t", t=4), 0.5, None,
                                        ALU.mult).then_inc(s["time_ready"], 1)

            def prep(ph, c):
                s = att[ph]
                chain = chains[ph][0]
                chain.round(c)
                if ph == "b":
                    yield "rows"
                    dve.wait_ge(s["y_loaded"], TOPK * 16 * (c + 1))
                    yield from add_rows(ystage, c, chain, s["combined"])
                    dve.wait_ge(s["combined"], c + 1)
                yield from moments_of(c, 0, chain)
                add_eps(0).then_inc(s["norm_var"], 1)
                yield "rstd"
                dve.wait_ge(s["norm_rstd"], c + 1)
                scale = rstd[:, 0, :]
                if ph == "b":
                    yield from log_map(c, chain)
                    scale = lm[:, 11, :]
                for t in range(NT):
                    normalised(c, t, 0, xn, scale).then_inc(s["norm_ready"], 1)
                if ph == "a":
                    yield from rope(c)
                else:
                    for i in range(2):
                        yield f"proj{i}"
                        dve.wait_ge(s["proj_ready"], 2 * c + i + 1)
                        nc.vector.tensor_tensor(
                            qk.rearrange("p (t n) -> p t n", t=NT)[:, 2 * i:2 * i + 2, :],
                            misc.rearrange("p (t n) -> p t n", t=2),
                            bias_qkv[:, 0:2 * D].unsqueeze(1).to_broadcast([P, 2, 2 * D]),
                            ALU.add).then_inc(s["proj_read"], 1)
                    yield from exp_map(c, chain)
                chain.end()

            def add_v_bias(c):
                s = att["b"]
                yield "vproj"
                dve.wait_ge(s["v_ready"], c + 1)
                dve.wait_ge(s["v_spread"], 2 * (c + 1))
                nc.vector.tensor_tensor(vstage[:], misc4(D),
                                        bias_qkv[:, 2 * D:3 * D].unsqueeze(1).to_broadcast([P, NT, D]),
                                        ALU.add).then_inc(s["v_staged"], 1)

            def post(ph, c):
                s = att[ph]
                chain = chains[ph][1]
                chain.round(c)
                heads = misc.rearrange("p (h c) -> p h c", c=32)
                for t in range(NT):
                    yield f"oT{t}"
                    dve.wait_ge(s["oT_ready"], NT * c + t + 1)
                    chain.link(nc.vector.reciprocal(rsum[:], heads[:, :, HD]))
                    yield None
                    nc.vector.tensor_tensor(onorm[:, t, :].rearrange("p (h d) -> p h d", d=HD), heads[:, :, 0:HD],
                                            rsum[:].unsqueeze(2).to_broadcast([P, H, HD]),
                                            ALU.mult).then_inc(s["onorm_ready"], 1)
                xb = x[:, ds(c * NT, NT), :]
                yield "oproj"
                dve.wait_ge(s["oproj_ready"], c + 1)
                nc.vector.tensor_tensor(xb, xb, misc4(D), ALU.add).then_inc(s["post_read"], 1)
                dve.wait_ge(s["post_read"], 3 * c + 1)
                yield None
                if ph == "b":
                    chain.link(nc.vector.tensor_tensor(xb, xb, bias_o[:].unsqueeze(1).to_broadcast([P, NT, D]), ALU.add))
                    yield None
                yield from moments_of(c, 1, chain)
                add_eps(1).then_inc(s["norm2_var"], 1)
                yield "rstd2"
                dve.wait_ge(s["norm2_rstd"], c + 1)
                dve.wait_ge(s["rows_free"], c + 1)
                for t in range(NT):
                    normalised(c, t, 1, xn2, rstd[:, 1, :]).then_inc(s["norm2_ready"], 1)

                logit, eq, sc, top1, logit2, top2, both, place, shifted, ex, tmp = (rt[:, i] for i in range(11))
                m1, w1_, m2, w2_, total, e2, p1, p2, den, rs, pl1, pl2 = (rk[:, i, :] for i in range(12))

                def over(v):
                    return v.unsqueeze(2).to_broadcast([P, NT, E])

                def best(of, m, w, top):
                    chain.link(nc.vector.tensor_reduce(m, of, axis=X_AXIS, op=ALU.max))
                    yield None
                    chain.link(nc.vector.tensor_tensor(eq, of, over(m), ALU.is_equal))
                    yield None
                    chain.link(nc.vector.tensor_tensor(sc, eq, pick, ALU.mult))
                    yield None
                    chain.link(nc.vector.tensor_reduce(w, sc, axis=X_AXIS, op=ALU.max))
                    yield None
                    chain.link(nc.vector.tensor_tensor(top, sc, over(w), ALU.is_equal))
                    yield None

                yield "logits"
                dve.wait_ge(s["logits_ready"], c + 1)
                nc.vector.tensor_copy(logit, misc4(E)).then_inc(s["post_read"], 1)
                yield None
                dve.wait_ge(s["post_read"], 3 * c + 2)
                yield from best(logit, m1, w1_, top1)
                nc.vector.tensor_tensor(shifted, logit, over(m1), ALU.subtract).then_inc(s["route_exp_in"], 1)
                chain.link(nc.vector.scalar_tensor_tensor(logit2, top1, MASKED, logit, ALU.mult, ALU.add))
                yield None
                yield from best(logit2, m2, w2_, top2)
                nc.vector.tensor_tensor(tops_bf[:], top1, top2, ALU.add).then_inc(s["tops_ready"], 1)
                yield "rexp"
                dve.wait_ge(s["route_exp"], c + 1)
                chain.mark(nc.vector.tensor_reduce(total, ex, axis=X_AXIS, op=ALU.add))
                chain.mark(nc.vector.tensor_tensor(tmp, ex, top2, ALU.mult))
                yield None
                chain.settle()
                chain.mark(nc.vector.reciprocal(p1, total))
                chain.mark(nc.vector.tensor_reduce(e2, tmp, axis=X_AXIS, op=ALU.add))
                yield None
                chain.settle()
                chain.link(nc.vector.tensor_tensor(p2, e2, p1, ALU.mult))
                yield None
                chain.link(nc.vector.tensor_tensor(den, p1, p2, ALU.add))
                yield None
                chain.link(nc.vector.tensor_scalar(den, den, 1e-9, None, ALU.add))
                yield None
                chain.link(nc.vector.reciprocal(rs, den))
                yield None
                for k, p in enumerate((p1, p2)):
                    chain.mark(nc.vector.tensor_tensor(gates[:, ds(c * NT, NT), k], p, rs, ALU.mult))

            def places(ph, c):
                s = att[ph]
                chain = chains[ph][1]
                top1, top2, place, tmp = (rt[:, i] for i in (3, 5, 7, 10))
                yield "rank"
                dve.wait_ge(s["rank_ready"], c + 1)
                chain.link(nc.vector.tensor_tensor(
                    place, misc[:, 0:NT * E].rearrange("p (t e) -> p t e", e=E),
                    counts[:].unsqueeze(1).to_broadcast([P, NT, E]), ALU.add))
                nc.vector.tensor_tensor(counts[:], counts[:], misc[:, NT * E:NT * E + E],
                                        ALU.add).then_inc(s["post_read"], 1)
                chain.link(nc.vector.tensor_tensor(place, place, listbase, ALU.add))
                yield None
                dve.wait_ge(s["entries_free"], c + 1)
                for k, (top, pl) in enumerate(((top1, rk[:, 10, :]), (top2, rk[:, 11, :]))):
                    chain.link(nc.vector.tensor_tensor(tmp, place, top, ALU.mult))
                    yield None
                    chain.link(nc.vector.tensor_reduce(pl, tmp, axis=X_AXIS, op=ALU.add))
                    yield None
                    chain.mark(nc.vector.tensor_copy(slots[:, k, :], pl))
                nc.vector.tensor_copy(entries[:].rearrange("p t k c -> p (t k c)"), ids[:]).then_inc(s["entries_ready"], 1)
                dve.wait_ge(s["entries_ready"], c + 1)
                chain.link(nc.vector.tensor_scalar(ids[:], ids[:], float(S), None, ALU.add))
                chain.end()

            class Pieces:
                def __init__(self, *flows):
                    self.flow = (piece for flow in flows for piece in flow)
                    self.needs = next(self.flow, "end")

                def some(self, n):
                    while self.needs is None and n > 0:
                        self.needs = next(self.flow, "end")
                        n -= 1

                def reach(self, name):
                    self.some(1000)
                    if self.needs == name:
                        self.needs = next(self.flow, "end")

                def finish(self):
                    self.some(1000)
                    assert self.needs == "end", self.needs

            def maximum(ph, b, half, i):
                s = att[ph]
                n = SCORES[ph] * half + i
                dve.wait_ge(s["scores_ready"], 2 * SCORES[ph] * b + n + 1)
                if i < len(UNITS[ph]):
                    g, q, h0, nh = UNITS[ph][i]
                    w = (q + 1) * P if ph == "a" else S
                    nc.vector.tensor_reduce(
                        negmax[:, half, :].rearrange("p (g t q) -> p g t q", g=2, q=NT)[:, g, h0:h0 + nh, q],
                        ps[:, n % 2, 0:nh * w].rearrange("p (h k) -> p h k", h=nh),
                        axis=X_AXIS, op=ALU.max, negate=True).then_inc(s["max_done"], 1)
                    return
                chain = chains[ph][2]
                chain.round(2 * b + half)
                m = ps[0:32, n % 2, 0:P]
                chain.link(nc.vector.tensor_copy(maxparts[:, half, 0, :], m))
                nc.vector.tensor_tensor(maxrest[:], m, maxparts[:, half, 0, :], ALU.subtract).then_inc(s["max_done"], 1)
                dve.wait_ge(s["max_done"], 2 * SCORES[ph] * b + n + 3)
                chain.link(nc.vector.tensor_copy(maxparts[:, half, 1, :], maxrest[:]))
                nc.vector.tensor_tensor(maxparts[:, half, 2, :], maxrest[:], maxparts[:, half, 1, :],
                                        ALU.subtract).then_inc(s["maxparts_ready"], 1)
                chain.end()

            def part(ph, b, half, sequence, side):
                for kind, i in sequence:
                    if kind == "s":
                        maximum(ph, b, half, i)
                        side.some(PIECES[ph])
                    if kind == "side":
                        side.reach(i)
                side.finish()

            def batch(ph, b, prev, nxt, nxt2):
                flows = [post(ph, b - 1)] if prev else []
                if nxt and ph == "b":
                    flows.append(add_v_bias(b + 1))
                part(ph, b, 1, first_order(ph, prev, nxt), Pieces(*flows))
                flows = [places(ph, b - 1)] if prev else []
                if nxt2:
                    flows.append(prep(ph, b + 2))
                part(ph, b + 1, 0, second_order(ph, prev, nxt, nxt2), Pieces(*flows))

            def all_steps(names, *flows):
                side = Pieces(*flows)
                for name in names:
                    side.reach(name)
                side.finish()

            def attention(ph):
                all_steps(PREP[ph], prep(ph, 0))
                if ph == "b":
                    all_steps(["vproj"], add_v_bias(0))
                part(ph, 0, 0, second_order(ph, False, True, True, e=False), Pieces(prep(ph, 1)))
                batch(ph, 0, False, True, True)
                with dve.Fori(1, B - 2) as b:
                    batch(ph, b, True, True, True)
                batch(ph, B - 2, True, True, False)
                batch(ph, B - 1, True, False, False)
                all_steps(POST + ["rank"], post(ph, B - 1), places(ph, B - 1))

            def experts(n):
                r0 = n * ROUNDS
                chain = Chain(dve, f["dve"], FFN_STEPS)
                chain.round(n)
                padded, ends, starts, offset = (lay[:, i, :] for i in range(4))
                chain.link(nc.vector.tensor_scalar(lay_i[:, 0, :], counts[:], float(P - 1), None, ALU.add))
                chain.link(nc.vector.tensor_scalar(lay_i[:, 1, :], lay_i[:, 0, :], 7, 7,
                                                   ALU.arith_shift_right, ALU.logical_shift_left))
                chain.link(nc.vector.tensor_copy(padded, lay_i[:, 1, :]))
                chain.link(nc.vector.tensor_copy(ends, padded))
                for e in range(1, E):
                    chain.link(nc.vector.tensor_tensor(ends[:, e:e + 1], ends[:, e:e + 1], ends[:, e - 1:e], ALU.add))
                chain.link(nc.vector.tensor_tensor(starts, ends, padded, ALU.subtract))
                chain.link(nc.vector.tensor_tensor(offset, listbase[:, 0, :], starts, ALU.subtract))
                chain.link(nc.vector.tensor_scalar(offset, offset, -float(NO_LIST), None, ALU.add))
                begun, ended, inside, entry_at = (tl[:, i] for i in range(4))

                def over(v):
                    return v[0:1, :].unsqueeze(1).to_broadcast([1, TILES, E])

                chain.link(nc.vector.tensor_tensor(begun, tilepos[:], over(starts), ALU.is_ge))
                chain.link(nc.vector.tensor_tensor(ended, tilepos[:], over(ends), ALU.is_ge))
                chain.link(nc.vector.tensor_tensor(inside, begun, ended, ALU.subtract))
                chain.link(nc.vector.tensor_tensor(entry_at, tilepos[:], over(offset), ALU.add))
                chain.link(nc.vector.tensor_tensor(entry_at, entry_at, inside, ALU.mult))
                chain.link(nc.vector.tensor_reduce(tile_f[:, 0, :], ended, axis=X_AXIS, op=ALU.add))
                chain.link(nc.vector.tensor_reduce(tile_f[:, 1, :], entry_at, axis=X_AXIS, op=ALU.add))
                chain.link(nc.vector.tensor_scalar(tile_tab[:, 0, :], tile_f[:, 0, :], float(E - 1), None, ALU.min))
                chain.link(nc.vector.memset(counts[:], 0.0))
                chain.link(nc.vector.tensor_scalar(ids[:], ids[:], -float(TOK), None, ALU.add))
                nc.vector.tensor_scalar(tile_tab[:, 1, :], tile_f[:, 1, :], float(NO_LIST), None,
                                        ALU.add).then_inc(f["table"], 1)
                chain.end()
                dve.wait_ge(f["table"], n + 1)

                def expert(i, k):
                    return dve.value_load(tile_tab[0:1, 0, ds(ROUND * i + k, 1)], min_val=0, max_val=E - 1)

                def hidden(i, k, start, e):
                    dve.wait_ge(f["h_ready"], ROUND * (i + r0) + k + 1)
                    if not start:
                        dve.wait_ge(f["hT_ready"], ROUND * (i + r0) + k - 1)
                    nc.vector.tensor_tensor(hid[:, k % 2, :], ps[:, k % 2, :], b1[:, ds(e * FF, FF)],
                                            ALU.add).then_inc(f["h_copied"], 1)

                def result(i, k, start, e):
                    dve.wait_ge(f["y_ready"], ROUND * (i + r0) + k + 1)
                    if not start:
                        dve.wait_ge(f["scattered"][k % 4], 16 * (2 * (i + r0) + k // 4))
                    nc.vector.tensor_tensor(yrow[:, k % 4, :], ps[:, 4, 0:P], b2[:, ds(e * D, D)],
                                            ALU.add).then_inc(f["y_copied"], 1)

                e = [None, expert(0, 0)]
                for k in range(1, ROUND):
                    hidden(0, k - 1, k - 1 < 2, e[-1])
                    if k >= 2:
                        result(0, k - 2, k - 2 < 4, e[-2])
                    e.append(expert(0, k))
                with dve.Fori(1, ROUNDS) as i:
                    e = [expert(i - 1, ROUND - 2), expert(i - 1, ROUND - 1)]
                    for k in range(ROUND):
                        hidden(i - (k < 1), (k - 1) % ROUND, False, e[-1])
                        result(i - (k < 2), (k - 2) % ROUND, False, e[-2])
                        if k < ROUND - 1:
                            e.append(expert(i, k))
                end = ROUNDS - 1
                e = [expert(end, ROUND - 2), expert(end, ROUND - 1)]
                hidden(end, ROUND - 1, False, e[1])
                result(end, ROUND - 2, False, e[0])
                result(end, ROUND - 1, False, e[1])

            dve.wait_ge(first["const"], 3 * 16)
            dve.wait_ge(first["x"], 16)
            dve.wait_ge(first["tables"], TABLES)
            start = Chain(dve, last["dve"], 2)
            start.round(0)
            start.link(nc.vector.tensor_copy(ids[:], const[:, C_IDS:C_IDS + NT * TOPK * 2]))
            attention("a")
            dve.wait_ge(first["ready"], 6 * 16)
            dve.wait_ge(first["weights"], 9 * 16)
            start.link(nc.vector.reciprocal(inv_curv[:], curv[:]))
            if stop >= 2:
                experts(0)
            if stop >= 3:
                attention("b")
            if stop >= 4:
                experts(1)
            if stop in (1, 3):
                dve.sem_inc(last["combined"], B)
            else:
                final = Chain(dve, last["final_step"], 3 * B)
                final.round(0)
                for b in range(B):
                    dve.wait_ge(last_loaded[b], LAYERS * ROUNDS * 16 + TOPK * 16)
                    for _ in add_rows(last_rows[:, b], b, final, last["combined"]):
                        pass
                final.end()

        @block.tensor
        def _(pe):
            for ph in "ab":
                pe.sem_inc(att[ph]["pv_ready"], 2)

            def score_unit(ph, b, half, i):
                s = att[ph]
                n = SCORES[ph] * half + i
                base = 2 * SCORES[ph] * b
                if i == 0:
                    pe.wait_ge(s["stacked"][half], STACKED * (b + 1))
                if i == len(UNITS[ph]):
                    pe.wait_ge(s["max_done"], base + n + 2)
                    nc.tensor.transpose(ps[0:32, n % 2, 0:P], negmax[:, half, :], ident).then_inc(s["scores_ready"], 1)
                    return
                g, q, h0, nh = UNITS[ph][i]
                g += 2 * half
                w = (q + 1) * P if ph == "a" else S
                pe.wait_ge(s["max_done"], base + n + 1)
                for h in range(h0, h0 + nh):
                    o = (h - h0) * w
                    mm = nc.tensor.matmul(ps[:, n % 2, o:o + w], qstack[:, first_tile(g) + h, q * P:(q + 1) * P],
                                          kstack[:, first_head(g) + h, 0:w], start=True, stop=ph == "b")
                    if ph == "a":
                        mm = nc.tensor.matmul(ps[:, n % 2, o + w - P:o + w], ident_bf, mask_s,
                                              start=False, stop=True)
                mm.then_inc(s["scores_ready"], 1)

            def prob_unit(ph, b, half, i):
                s = att[ph]
                quad, h = divmod(i, 4)
                g, kp = divmod(quad, 2)
                g += 2 * half
                n = EXPS * half + i
                if i == 0:
                    pe.wait_ge(s["maxrows"][half], 3 * 16 * (b + 1))
                pe.wait_ge(s["exp_done"], 2 * EXPS * b + n + 1)
                st = ps[:, 2 + 2 * (n % 2):4 + 2 * (n % 2), :].rearrange("p a n -> p (a n)")
                for kt, q0, c in spans(ph, kp):
                    mm = nc.tensor.matmul(st[:, c:c + S - q0], kstack[:, first_head(g) + h, kt * P:(kt + 1) * P],
                                          qstack[:, first_tile(g) + h, q0:S], start=True, stop=ph == "b")
                    if ph == "a":
                        mm = nc.tensor.matmul(st[:, c:c + P], ident_bf, mask_t, start=False, stop=True)
                mm.then_inc(s["exp_in"], 1)

            def weighted_sum(ph, b, quad):
                s = att[ph]
                g, kp = divmod(quad, 2)
                pe.wait_ge(s["exp_done"], 2 * EXPS * b + 4 * quad + 4 + 2)
                if kp == 0:
                    pe.wait_ge(s["o_copied"], GROUPS * b + g + 1)
                    pe.wait_ge(s["v_spread"], 2 * b + g // 2 + 1 + 2)
                for kt, q0, c in spans(ph, kp):
                    for h in range(4):
                        mm = nc.tensor.matmul(outT[32 * h:32 * h + 16, q0:S], vones[:, kt, first_head(g) + h, :],
                                              probs[:, quad % 2, h, c:c + S - q0],
                                              start=kt == 0, stop=kt == NT - 1)
                mm.then_inc(s["pv_ready"], 1)

            def side(ph, name, b):
                nonlocal misc_read
                s = att[ph]
                i = int(name[-1]) if name[-1] in "01234" else 0

                def misc_is_read():
                    if misc_read:
                        pe.wait_ge(*misc_read)

                c = b - 1
                if name[:2] == "oT":
                    if i == 0:
                        pe.wait_ge(s["o_copied"], GROUPS * c + GROUPS + 1)
                    misc_is_read()
                    for g in range(GROUPS):
                        mm = nc.tensor.transpose(misc[:, g * P:(g + 1) * P], oT[:, g, i * P:(i + 1) * P], ident)
                    mm.then_inc(s["oT_ready"], 1)
                    misc_read = s["onorm_ready"], NT * c + i + 1
                if name == "onormT":
                    misc_is_read()
                    for t in range(NT):
                        mm = nc.tensor.transpose(misc[:, t * P:(t + 1) * P], onorm[:, t, :], ident)
                    mm.then_inc(s["onormT_ready"], 1)
                    misc_read = s["onormT_copied"], c + 1
                if name == "oproj":
                    misc_is_read()
                    for t in range(NT):
                        mm = nc.tensor.matmul(misc[:, t * D:(t + 1) * D], onormT[:, t * P:(t + 1) * P],
                                              (wao if ph == "a" else wbo)[:], start=True, stop=True)
                    mm.then_inc(s["oproj_ready"], 1)
                    misc_read = s["post_read"], 3 * c + 1
                if name == "norm2T":
                    misc_is_read()
                    for t in range(NT):
                        pe.wait_ge(s["norm2_ready"], NT * c + t + 1)
                        mm = nc.tensor.transpose(misc[:, t * P:(t + 1) * P], xn2[:, t, :], ident)
                    mm.then_inc(s["norm2T_ready"], 1)
                    misc_read = s["norm2T_copied"], c + 1
                if name == "logits":
                    misc_is_read()
                    for t in range(NT):
                        mm = nc.tensor.matmul(misc[:, t * E:(t + 1) * E], xn2T[:, t * P:(t + 1) * P], router[:],
                                              start=True, stop=True)
                    mm.then_inc(s["logits_ready"], 1)
                    misc_read = s["post_read"], 3 * c + 2
                if name == "rank":
                    misc_is_read()
                    pe.wait_ge(s["tops_ready"], c + 1)
                    for t in range(NT + 1):
                        for u in range(min(t + 1, NT)):
                            mm = nc.tensor.matmul(misc[:, t * E:(t + 1) * E], before if u == t else ones_bf,
                                                  tops_bf[:, u, :], start=u == 0, stop=u == min(t, NT - 1))
                    mm.then_inc(s["rank_ready"], 1)
                    misc_read = s["post_read"], 3 * c + 3

                c = b + 1
                if name == "vproj":
                    misc_is_read()
                    for t in range(NT):
                        mm = nc.tensor.matmul(misc[:, t * D:(t + 1) * D], xnT[:, t * P:(t + 1) * P],
                                              wa[:, 4, :] if ph == "a" else wb[:, 2 * D:3 * D],
                                              start=True, stop=True)
                    mm.then_inc(s["v_ready"], 1)
                    misc_read = s["v_staged"], c + 1

                c = b + 2
                if name == "normT":
                    misc_is_read()
                    for t in range(NT):
                        pe.wait_ge(s["norm_ready"], NT * c + t + 1)
                        mm = nc.tensor.transpose(misc[:, t * P:(t + 1) * P], xn[:, t, :], ident)
                    mm.then_inc(s["normT_ready"], 1)
                    misc_read = s["normT_copied"], c + 1
                if name[:4] == "proj" and ph == "a":
                    misc_is_read()
                    nc.tensor.matmul(misc, wa[:, i, :], xnT[:], start=True, stop=True).then_inc(s["proj_ready"], 1)
                    misc_read = s["proj_read"], 4 * c + i + 1
                if name[:4] == "proj" and ph == "b":
                    misc_is_read()
                    for t in range(2):
                        mm = nc.tensor.matmul(misc[:, t * 2 * D:(t + 1) * 2 * D],
                                              xnT[:, (2 * i + t) * P:(2 * i + t + 1) * P], wb[:, 0:2 * D],
                                              start=True, stop=True)
                    mm.then_inc(s["proj_ready"], 1)
                    misc_read = s["proj_read"], 2 * c + i + 1
                if name[:4] == "hypT":
                    if i == 0:
                        pe.wait_ge(s["hyp_ready"], c + 1)
                        pe.wait_ge(s["time_ready"], c + 1)
                    misc_is_read()
                    for t in range(NT):
                        m = 8 * t + 2 * i
                        mm = nc.tensor.transpose(misc[0:72, t * P:(t + 1) * P],
                                                 hyp[:, m:m + 2, :].rearrange("p m r -> p (m r)"), ident)
                    mm.then_inc(s["hypT_ready"], 1)
                    misc_read = s["hypT_copied"], 4 * c + i + 1

            misc_read = None

            def part(ph, b, half, prev, sequence):
                for kind, i in sequence:
                    if kind == "e":
                        prob_unit(ph, b, half, i)
                        if i == 1 and (half or prev):
                            weighted_sum(ph, b if half else b - 1, QUADS - 1 if half else 2 * QUADS - 1)
                        elif i % 4 == 1 and i > 1:
                            weighted_sum(ph, b, QUADS * half + i // 4 - 1)
                    if kind == "s":
                        score_unit(ph, b + half, 1 - half, i)
                    if kind == "side":
                        side(ph, i, b)

            def batch(ph, b, prev, nxt, nxt2):
                nonlocal misc_read
                s = att[ph]
                if not nxt:
                    misc_read = s["post_read"], 3 * (b - 1)
                elif ph == "a":
                    misc_read = s["proj_read"], 4 * (b + 2)
                else:
                    misc_read = s["hypT_copied"], 4 * (b + 2)
                part(ph, b, 0, prev, first_order(ph, prev, nxt))
                part(ph, b, 1, True, second_order(ph, prev, nxt, nxt2))

            def attention(ph):
                for name in PREP[ph]:
                    side(ph, name, -2)
                side(ph, "vproj", -1)
                pe.wait_ge(first["ready"], 6 * 16)
                part(ph, -1, 1, False, second_order(ph, False, True, True, e=False))
                batch(ph, 0, False, True, True)
                with pe.Fori(1, B - 2) as b:
                    batch(ph, b, True, True, True)
                batch(ph, B - 2, True, True, False)
                batch(ph, B - 1, True, False, False)
                weighted_sum(ph, B - 1, 2 * QUADS - 1)
                for name in POST + ["rank"]:
                    side(ph, name, B)

            def experts(n):
                r0 = n * ROUNDS
                pe.wait_ge(f["table"], n + 1)

                def rows(i, k, start):
                    pe.wait_ge(f["gathered"][k % 4], 16 * (2 * (i + r0) + k // 4 + 1))
                    if not start:
                        pe.wait_ge(f["xT_copied"], ROUND * (i + r0) + k)
                    nc.tensor.transpose(ps[:, 5, 0:P], xg[:, k % 4, :], ident).then_inc(f["xT_ready"], 1)

                def expert(i, k):
                    return pe.value_load(tile_tab[0:1, 0, ds(ROUND * i + k, 1)], min_val=0, max_val=E - 1)

                def up(i, k, start, e):
                    pe.wait_ge(f["xT_copied"], ROUND * (i + r0) + k + 1)
                    if not start:
                        pe.wait_ge(f["h_copied"], ROUND * (i + r0) + k - 1)
                    nc.tensor.matmul(ps[:, k % 2, :], xgT[:, k % 2, :], w1[:, ds(e * FF, FF)],
                                     start=True, stop=True).then_inc(f["h_ready"], 1)

                def turn(i, k):
                    pe.wait_ge(f["h_copied"], ROUND * (i + r0) + k + 1)
                    for j in range(NF):
                        mm = nc.tensor.transpose(ps[:, 2 + k % 2, j * P:(j + 1) * P],
                                                 hid[:, k % 2, j * P:(j + 1) * P], ident)
                    mm.then_inc(f["hT_ready"], 1)

                def down(i, k, start, e):
                    pe.wait_ge(f["hT_copied"], ROUND * (i + r0) + k + 1)
                    if not start:
                        pe.wait_ge(f["y_copied"], ROUND * (i + r0) + k)
                    for j in range(NF):
                        mm = nc.tensor.matmul(ps[:, 4, 0:P], hidT[:, k % 2, j, :], w2[:, ds(e * FF + j * P, P)],
                                              start=j == 0, stop=j == NF - 1)
                    mm.then_inc(f["y_ready"], 1)

                rows(0, 0, True)
                e = [None, expert(0, 0)]
                for k in range(1, ROUND):
                    up(0, k - 1, k - 1 < 2, e[-1])
                    if k >= 2:
                        down(0, k - 2, k == 2, e[-2])
                    e.append(expert(0, k))
                    rows(0, k, False)
                    turn(0, k - 1)
                with pe.Fori(1, ROUNDS) as i:
                    e = [expert(i - 1, ROUND - 2), expert(i - 1, ROUND - 1)]
                    for k in range(ROUND):
                        up(i - (k < 1), (k - 1) % ROUND, False, e[-1])
                        down(i - (k < 2), (k - 2) % ROUND, False, e[-2])
                        if k < ROUND - 1:
                            e.append(expert(i, k))
                        rows(i, k, False)
                        turn(i - (k < 1), (k - 1) % ROUND)
                end = ROUNDS - 1
                e = [expert(end, ROUND - 2), expert(end, ROUND - 1)]
                up(end, ROUND - 1, False, e[1])
                down(end, ROUND - 2, False, e[0])
                turn(end, ROUND - 1)
                down(end, ROUND - 1, False, e[1])

            pe.wait_ge(first["const"], 3 * 16)
            pe.wait_ge(first["tables"], TABLES)
            attention("a")
            pe.wait_ge(first["weights"], 9 * 16)
            if stop >= 2:
                experts(0)
            if stop >= 3:
                attention("b")
            if stop >= 4:
                experts(1)


def constants():
    c = np.zeros((P, C_END), np.float32)
    c[:, C_IDENT:C_IDENT + P] = np.eye(P)
    freq = np.float32(10000.0) ** (-2.0 * np.arange(0, HD // 2, dtype=np.float32) / HD)
    angle = np.arange(S, dtype=np.float32)[None, :] * freq.astype(np.float32)[:, None]
    dim = (np.arange(P) % 32) // 4
    c[:, C_COS:C_COS + S] = np.cos(angle)[dim // 2]
    c[:, C_SIN:C_SIN + S] = np.sin(angle)[dim // 2] * np.where(dim % 2 == 0, -1, 1)[:, None]
    c[:, C_PICK:C_PICK + NT * E] = np.tile(E - np.arange(E), NT)
    c[:, C_BASE:C_BASE + NT * E] = np.tile(LIST * np.arange(E), NT)
    p, t, k, w = np.meshgrid(np.arange(P), np.arange(NT), np.arange(TOPK), np.arange(2), indexing="ij")
    c[:, C_IDS:] = (t * P + p + w * k * TOK).reshape(P, -1)
    r = np.arange(P)
    masked = np.where(r[None, :] > r[:, None], MASKED, 0)
    bf = np.stack([np.eye(P), masked, masked.T, r[:, None] < r[None, :], np.ones((P, P))], 1)
    tilepos = np.repeat(P * np.arange(TILES), E).reshape(1, TILES, E)
    return c, bf.astype(mybir.dt.np(BF16)), tilepos.astype(np.float32)


def kernel(**inputs):
    import concourse.bacc as bacc
    from concourse.bass_utils import run_bass_kernel_spmd

    v = {k: np.asarray(w) for k, w in inputs.items()}
    A, Bp, Fp = "L0_attn_a_", "L0_attn_b_", "L0_ffn_"
    par, half, dim, pair = np.meshgrid(np.arange(2), np.arange(2), np.arange(HD), np.arange(4), indexing="ij")
    rows = (HD * (8 * par + 4 * half + pair) + dim).reshape(-1)
    swapped = (HD * (8 * par + 4 * half + pair) + (dim ^ 1)).reshape(-1)
    grouped = np.concatenate([HD * (8 * (g % 2) + 4 * (g // 2)) + np.arange(4 * HD) for g in range(GROUPS)])
    wq, wk, wv = (v[A + n].T for n in ("W_q", "W_k", "W_v"))
    consts, consts_bf, tilepos = constants()
    arrays = {
        "x": v[A + "x"].reshape(TOK, D),
        "consts": consts, "consts_bf": consts_bf, "tilepos": tilepos,
        "wa": np.stack([wq[:, rows], wq[:, swapped], wk[:, rows], wk[:, swapped], wv], 1),
        "wao": v[A + "W_o"].T[grouped],
        "wb": np.concatenate([v[Bp + n].T for n in ("wq_w", "wk_w", "wv_w")], 1),
        "wbo": v[Bp + "wo_w"].T[grouped],
        "bias_qkv": np.concatenate([v[Bp + n] for n in ("wq_b", "wk_b", "wv_b")]),
        "bias_o": v[Bp + "wo_b"],
        "curv": v[Bp + "curv"].reshape(1),
        "router": v[Fp + "router_w"].T,
        "w1": v[Fp + "w1"].transpose(2, 0, 1).reshape(D, E * FF),
        "b1": v[Fp + "b1"].reshape(-1),
        "w2": v[Fp + "w2"].transpose(2, 0, 1).reshape(NF, P, E, D).transpose(1, 2, 0, 3).reshape(P, E * FF),
        "b2": v[Fp + "b2"].reshape(-1),
    }
    arrays = {k: np.ascontiguousarray(w) for k, w in arrays.items()}
    nc = bacc.Bacc("TRN2", target_bir_lowering=False, num_devices=1)
    aps = {k: nc.dram_tensor("in_" + k, w.shape, mybir.dt.from_np(w.dtype), kind="ExternalInput").ap()
           for k, w in arrays.items()}
    out = nc.dram_tensor("out", (TOK, D), F32, kind="ExternalOutput").ap()
    build_program(nc, aps, out)
    r = run_bass_kernel_spmd(nc, [{"in_" + k: w for k, w in arrays.items()}], core_ids=[0])
    return r.results[0]["out"].reshape(B, S, D)
```

```python
from contextlib import ExitStack

import numpy as np
import concourse.bass as bass
from concourse import mybir
from concourse.bass import ds, IndirectOffsetOnAxis

B, S, D = 8, 512, 128
H, HD = 16, 8
P = 128
NT = S // P
E, FF, TOPK = 8, 512, 2
NF = FF // P
TOK = B * S
LIST = TOK
TILES = TOK * TOPK // P + E
ROUND = 8
ROUNDS = TILES // ROUND
BEHIND = 5
NO_LIST = E * LIST
LAYERS = 2
EPS = 1e-5
MASKED = -1e30
DVE_STEPS = {"a": (8, 42, 2), "b": (35, 43, 2)}
PIECES = {"a": 3, "b": 3}
POOL_STEPS = 13
FFN_STEPS = 24
SCALE = float(1.0 / np.sqrt(np.float32(HD)))
GROUPS = 4
JQ, JK = [0, 0, 0, 1, 1, 2], [0, 1, 2, 0, 1, 0]
MAXROW = 54
HEADROWS = 64

F32 = mybir.dt.float32
BF16 = mybir.dt.bfloat16
I32 = mybir.dt.int32
ALU = mybir.AluOpType
ACT = mybir.ActivationFunctionType
X_AXIS = mybir.AxisListType.X

UNITS = {"a": [(g, q, h, n) for g in range(2) for q, h, n in
               [(0, 0, 4), (1, 0, 2), (1, 2, 2)] + [(q, h, 1) for q in (2, 3) for h in range(4)]],
         "b": [(g, q, h, 1) for g in range(2) for q in range(NT) for h in range(4)]}
TIMES = {"a": (0.0, 0.6, 0.2, 0.95), "b": (0.0, 0.65, 0.2, 1.0)}
ROOM = {"oproj": 2, "logits": 2, "rank": 2}
QUADS = 2 * NT
EXPS = 4 * QUADS
BANKS = 3

POST = ["oT0", "oT1", "oT2", "oT3", "onormT", "oproj", "rstd2", "norm2T", "logits", "rexp"]
PREP = {"a": ["rstd", "normT", "proj0", "proj1", "proj2", "proj3"],
        "b": ["rows", "rstd", "nc", "ln", "normT", "proj0", "proj1", "square", "root", "sinh", "time"]}
PREP_END = {"a": [], "b": ["hypT0", "hypT1", "hypT2", "hypT3"]}


def order(ph, e, s, early, side):
    n = len(UNITS[ph]) + 1
    start, end, side_start, side_end = TIMES[ph] if e else (0.0, 1.0, 0.0, 1.0)
    items = [((i + 0.5) / EXPS, ("e", i)) for i in range(EXPS if e else 0)]
    items += [(start + (end - start) * (i + 0.5) / n, ("s", i)) for i in range(n if s else 0)]
    items += [(0.16 * (i + 1) / len(early), ("side", name)) for i, name in enumerate(early)]
    room = [ROOM.get(name, 1) for name in side]
    items += [(side_start + (side_end - side_start) * (sum(room[:i]) + 0.5) / sum(room), ("side", name))
              for i, name in enumerate(side)]
    return [item for _, item in sorted(items, key=lambda it: it[0])]


def first_order(ph, prev, nxt):
    return order(ph, True, True, (PREP_END[ph] if nxt else []) + ["vcopy1"], (POST if prev else []) + (["vproj"] if nxt else []))


def second_order(ph, prev, nxt, nxt2, e=True):
    return order(ph, e, nxt, ["vcopy0"] if nxt else [], (["rank"] if prev else []) + (PREP[ph] if nxt2 else []))


C_IDENT, C_COS, C_SIN, C_PICK, C_BASE, C_IDS = 0, 128, 640, 1152, 1184, 1216
C_END = 1232


def build_program(nc, a, out):
    ctx = ExitStack()
    with ctx:
        def sb(name, shape, dt=F32):
            return ctx.enter_context(nc.sbuf_tensor(name, shape, dt))

        def sem(name):
            return ctx.enter_context(nc.semaphore(name))

        def sems(prefix, names):
            return {n: sem(prefix + n) for n in names.split()}

        xn_dram = nc.dram_tensor("xn_rows", [TOK + P, D], F32, kind="Internal").ap()
        list_dram = nc.dram_tensor("expert_lists", [E * LIST + P, 2], I32, kind="Internal").ap()
        y_dram = nc.dram_tensor("expert_rows", [TOPK * TOK, D], F32, kind="Internal").ap()
        stack_dram = nc.dram_tensor("part_blocks", [2 * len(JQ) * 16 * (HD + 1), S], BF16, kind="Internal").ap()

        x = sb("x", [P, B * NT, D])
        const = sb("const", [P, C_END])
        ident = const[:, C_IDENT:C_IDENT + P]
        cos_t, sin_t = const[:, C_COS:C_COS + S], const[:, C_SIN:C_SIN + S]
        pick = const[:, C_PICK:C_PICK + NT * E].rearrange("p (t e) -> p t e", e=E)
        listbase = const[:, C_BASE:C_BASE + NT * E].rearrange("p (t e) -> p t e", e=E)
        tilepos = sb("tilepos", [1, TILES, E])
        cbf = sb("cbf", [P, 5, P], BF16)
        ident_bf, mask_s, mask_t, before, ones_bf = (cbf[:, i, :] for i in range(5))
        half = sb("half", [P, NT * 2 * H])
        neghalf = sb("neghalf", [P, NT])
        wa = sb("wa", [P, 5, D])
        wao = sb("wao", [P, D])
        wb = sb("wb", [P, 3 * D])
        wbo = sb("wbo", [P, D])
        bias_qkv = sb("bias_qkv", [P, 3 * D])
        bias_o = sb("bias_o", [P, D])
        curv = sb("curv", [P, 1])
        inv_curv = sb("inv_curv", [P, 1])
        router = sb("router", [P, E])
        w1 = sb("w1", [P, E * FF])
        swap = sb("swap", [P, 2 * E * FF])
        w2, b1 = swap[:, 0:E * FF], swap[:, E * FF:]
        b2 = sb("b2", [P, E * D])

        stats = sb("stats", [P, 2, NT, 6])
        moments = sb("moments", [P, 2, NT, 2])
        var_eps = sb("var_eps", [P, 2, NT])
        rstd = sb("rstd", [P, 2, NT])
        xn = sb("xn", [P, NT, D])
        xnT = sb("xnT", [P, S])
        qk = const[:, C_COS:C_COS + 2 * S]
        hyp = sb("hyp", [P, NT * 4 * 2, 9 * 4])
        hyp_flat = hyp[:].rearrange("p m r -> p (m r)")
        qk_sq = hyp_flat[:, 0:2 * S]
        ystage = hyp_flat[:, 0:TOPK * S].rearrange("p (k t d) -> p k t d", k=TOPK, t=NT)
        work = sb("work", [P, 4, S])
        hypT = work[0:72, :, :]
        qrot = work[:, 0:2, :]
        rope_c, rope_s = work[:, 2, :], work[:, 3, :]
        oT = sb("oT", [P, GROUPS, S])
        one_bf = oT[0:3, :, :].rearrange("p c n -> p (c n)").bitcast(BF16)[:, 0:8 * S]
        parts = sb("parts", [P, 3, 4 * S], BF16)
        stacks_f32 = [swap[:, 0:12 * S], sb("stacks", [P, 12 * S])[:]]
        stacks = [st.bitcast(BF16) for st in stacks_f32]
        qstacks = [st[:, 0:8 * S].rearrange("p (t n) -> p t n", n=S) for st in stacks]
        kstacks = [st[:, 8 * S:24 * S].rearrange("p (t n) -> p t n", n=S) for st in stacks]
        vstage = sb("vstage", [P, NT, D])
        vones = sb("vones", [P, NT, H, 16])
        negmax = sb("negmax", [P, 2, 2 * 4 * NT])
        maxrest = sb("maxrest", [32, P])
        maxparts = sb("maxparts", [32, 2, 3, P], BF16)
        shared = sb("shared", [P, 2 * 4 * 2 * S])
        probs = shared[:].rearrange("p (a h n) -> p a h n", a=4, h=4)
        rsum = sb("rsum", [P, H])
        onorm = sb("onorm", [P, NT, D])
        onormT = sb("onormT", [P, S])
        xn2 = sb("xn2", [P, NT, D])
        xn2T = sb("xn2T", [P, S])
        rt = sb("rt", [P, 11, NT, E])
        rk = sb("rk", [P, 12, NT])
        lm = sb("lm", [P, 12, NT])
        lm_small = sb("lm_small", [P, NT], I32)
        em = sb("em", [P, 8, NT * 2 * H])
        em_small = sb("em_small", [P, NT * 2 * H], I32)
        tops_bf = sb("tops_bf", [P, NT, E], BF16)
        counts = sb("counts", [P, E])
        gates = sb("gates", [P, B * NT, TOPK])
        ids = sb("ids", [P, NT * TOPK * 2])
        entries = sb("entries", [P, NT, TOPK, 2], I32)
        slots = sb("slots", [P, TOPK, NT], I32)

        list_fill = sb("list_fill", [P, 2 * LIST * E // P], I32)
        lay = sb("lay", [P, 8, E])
        lay_i = sb("lay_i", [P, 2, E], I32)
        tile_f = sb("tile_f", [1, 2, TILES])
        tile_tab = sb("tile_tab", [1, 2, TILES], I32)
        entry = sb("entry", [P, ROUND, 2], I32)
        def view(at, *shape):
            names = "abc"[:len(shape)]
            n = int(np.prod(shape))
            return shared[:, at:at + n].rearrange(f"p ({' '.join(names)}) -> p {' '.join(names)}",
                                                  **dict(zip(names, shape)))

        last_rows = shared[:].rearrange("p (b k t d) -> p b k t d", b=B, k=TOPK, t=NT)
        xg = view(0, 4, D)
        xgT = view(512, 2, P)
        hid = view(768, 2, FF)
        hidT = view(1792, 2, NF, P)
        yrow = view(2816, 4, D)
        tl = view(3328, 4, TILES, E)[0:1]

        ps = ctx.enter_context(nc.psum_tensor("ps", [P, 8, 512], F32))
        misc = ps[:, 7, :]
        outT = ps[:, 6, :]

        def misc4(w):
            return misc[:, 0:4 * w].rearrange("p (t n) -> p t n", n=w)

        first = sems("init_", "x const weights tables ready clear emptied")
        ATT = ("dve_prep dve_post dve_max remainder norm_var norm_rstd norm_ready normT_ready normT_copied "
               "proj_ready proj_read v_ready v_staged v_spread part_ready parts_written scores_ready "
               "max_done maxparts_ready exp_in exp_done pv_ready o_copied oT_ready onorm_ready "
               "onormT_ready onormT_copied oproj_ready post_read norm2_var norm2_rstd norm2_ready "
               "norm2T_ready norm2T_copied logits_ready route_exp_in route_exp tops_ready "
               "rank_ready entries_ready entries_free scattered rows_stored rows_free ")
        att = {"a": sems("a_", ATT + "rot_ready"),
               "b": sems("b_", ATT + "nc_in nc_ready ln_in ln_ready norm_in norm_out exp_sh time_in "
                         "log_done root_ready time_out time_ready hyp_ready hypT_ready hypT_copied y_loaded combined pool_step square_done")}
        for ph in "ab":
            att[ph]["maxrows"] = [sem(f"{ph}_maxrows{half}") for half in range(2)]
            att[ph]["stacked"] = [sem(f"{ph}_stacked{half}") for half in range(2)]
        FFN = ("dve table xT_ready xT_copied h_ready h_copied hT_ready hT_copied "
               "y_ready y_copied")
        f = sems("f_", FFN)
        f["entry"] = [sem(f"f_entry{k}") for k in range(ROUND)]
        f["gathered"] = [sem(f"f_gathered{k}") for k in range(4)]
        f["scattered"] = [sem(f"f_scattered{k}") for k in range(4)]
        last = sems("end_", "combined stored dve final_step")
        swapped = sem("swapped")
        last_loaded = f["entry"]

        STACKED = 6 * 16
        WRITTEN = 2 * len(JQ) * 16
        SCORES = {ph: len(UNITS[ph]) + 1 for ph in "ab"}

        def first_tile(g):
            return 4 * (g // 2)

        def first_head(g):
            return 8 * (g % 2) + first_tile(g)

        def first_query(ph, kt):
            return kt * P if ph == "a" else 0

        def run_batches(eng, ph, batch):
            batch(ph, 0, 0, False, True, True)
            with eng.Fori(0, B // 2 - 2) as i:
                batch(ph, 2 * i + 1, 1, True, True, True)
                batch(ph, 2 * i + 2, 0, True, True, True)
            batch(ph, B - 3, 1, True, True, True)
            batch(ph, B - 2, 0, True, True, False)
            batch(ph, B - 1, 1, True, False, False)

        def plain(eng):
            eng.sem_inc(carried[eng], 1)

        class Chain:
            def __init__(self, eng, semaphore, per_round):
                self.eng, self.sem, self.per_round = eng, semaphore, per_round

            def round(self, r):
                self.base, self.n = r * self.per_round, 0

            def link(self, ins):
                self.mark(ins)
                self.settle()

            def mark(self, ins):
                ins.then_inc(self.sem, 1)
                self.n += 1

            def settle(self):
                self.eng.wait_ge(self.sem, self.base + self.n)

            def end(self):
                assert self.n == self.per_round, (self.sem, self.n)

        def last_parts(ph, c):
            return 3 * c + 3

        def split(eng, chain, ph, c, start):
            s = att[ph]
            chain.round(c)
            if ph == "b":
                eng.wait_ge(s["hypT_copied"], 4 * c + 4)
                eng.wait_ge(s["part_ready"], last_parts(ph, c) + 1)
                src, n, w = hypT.rearrange("p c n -> p (c n)"), 72, 4 * S
            else:
                eng.wait_ge(s["rot_ready"], 2 * c + 2)
                src, n, w = qrot.rearrange("p c n -> p (c n)"), P, 2 * S
            if not start:
                eng.wait_ge(s["parts_written"], WRITTEN * c)
            if ph == "a":
                plain(eng)
                eng.tensor_copy(parts[0:n, 0, 0:w], src).then_inc(s["part_ready"], 1)
                eng.wait_ge(s["part_ready"], last_parts(ph, c) + 1)
            chain.link(eng.tensor_tensor(src, src, parts[0:n, 0, 0:w], ALU.subtract))
            plain(eng)
            eng.tensor_copy(parts[0:n, 1, 0:w], src).then_inc(s["part_ready"], 1)
            eng.wait_ge(s["part_ready"], last_parts(ph, c) + 2)
            eng.tensor_tensor(parts[0:n, 2, 0:w], src, parts[0:n, 1, 0:w],
                                    ALU.subtract).then_inc(s["part_ready"], 1)
            chain.end()

        TABLES = 10

        carried = {eng: sem("carried_" + name) for eng, name in ((nc.vector, "dve"), (nc.gpsimd, "pool"))}

        block = ctx.enter_context(nc.Block())

        @block.sync
        def _(sp):
            for ph in "ab":
                sp.sem_inc(att[ph]["rows_free"], 1)
            n0 = 2 * NT
            sp.dma_start(x[:, 0:n0, :], a["x"][0:2 * S, :].rearrange("(n p) d -> p n d", p=P)).then_inc(first["const"], 16)
            sp.dma_start(const[:], a["consts"]).then_inc(first["const"], 16)
            sp.dma_start(wa[:], a["wa"]).then_inc(first["const"], 16)
            sp.dma_start(cbf[:], a["consts_bf"]).then_inc(first["const"], 16)
            sp.dma_start(x[:, n0:, :], a["x"][2 * S:, :].rearrange("(n p) d -> p n d", p=P)).then_inc(first["x"], 16)
            sp.wait_ge(first["tables"], TABLES)
            for kstack in kstacks:
                for par in range(2):
                    r = HEADROWS * par + MAXROW
                    sp.dma_start(kstack[r:r + 3, 8 * par:8 * par + 8, :],
                                 one_bf).then_inc(first["ready"], 16)
            sp.dma_start(wao[:], a["wao"]).then_inc(first["ready"], 16)
            sp.dma_start(router[:], a["router"]).then_inc(first["ready"], 16)
            sp.dma_start(curv[:], a["curv"].partition_broadcast(P)).then_inc(first["ready"], 16)
            sp.dma_start(xn_dram[TOK:TOK + P, :].rearrange("(p n) d -> p (n d)", n=1),
                         onormT[:, 0:D]).then_inc(first["ready"], 16)

            def later_loads():
                sp.dma_start(list_dram[0:NO_LIST, :].rearrange("(p n) c -> p (n c)", p=P),
                             list_fill[:]).then_inc(first["emptied"], 16)
                sp.dma_start(list_dram[NO_LIST:NO_LIST + P, :],
                             list_fill[:, 0:2]).then_inc(first["emptied"], 16)
                sp.dma_start(wb[:], a["wb"]).then_inc(first["weights"], 16)
                sp.dma_start(wbo[:], a["wbo"]).then_inc(first["weights"], 16)
                sp.dma_start(bias_qkv[:], a["bias_qkv"].partition_broadcast(P)).then_inc(first["weights"], 16)
                sp.dma_start(bias_o[:], a["bias_o"].partition_broadcast(P)).then_inc(first["weights"], 16)
                sp.dma_start(tilepos[:], a["tilepos"]).then_inc(first["weights"], 16)
                sp.dma_start(w1[:], a["w1"]).then_inc(first["weights"], 16)
                sp.dma_start(b2[:], a["b2"].partition_broadcast(P)).then_inc(first["weights"], 16)

            def swap_in(ph):
                sp.wait_ge(att[ph]["exp_in"], 2 * EXPS * (B - 1))
                sp.dma_start(w2, a["w2"]).then_inc(swapped, 16)
                sp.dma_start(b1, a["b1"].partition_broadcast(P)).then_inc(swapped, 16)

            def load_rows(c, start):
                s = att["b"]
                if not start:
                    sp.wait_ge(s["hypT_ready"], 4 * c)
                for k in range(TOPK):
                    sp.dma_start(ystage[:, k, :, :],
                                 y_dram[ds(c * S + k * TOK, S), :].rearrange(
                                     "(t p) d -> p t d", p=P)).then_inc(s["y_loaded"], 16)

            def write_parts(ph, c, start):
                s = att[ph]
                nd = HD + (ph == "b")
                if not start:
                    for half in range(2):
                        sp.wait_ge(s["stacked"][half], STACKED * c)
                for j in range(3):
                    sp.wait_ge(s["part_ready"], last_parts(ph, c) + j + 1)
                    for side, js in enumerate((JQ, JK)):
                        for i in range(len(JQ)):
                            if js[i] != j:
                                continue
                            at = (side * len(JQ) + i) * 16 * nd
                            dst = stack_dram[at:at + 16 * nd, :]
                            if ph == "a":
                                src = parts[:, j, side * S:(side + 1) * S]
                            else:
                                dst = dst.rearrange("(c r) n -> r c n", c=2)
                                src = parts[0:72, j, 2 * side * S:2 * (side + 1) * S].rearrange(
                                    "p (c n) -> p c n", c=2)
                            sp.dma_start(dst, src).then_inc(s["parts_written"], 16)

            def stack(ph, c, odd, half, start):
                s = att[ph]
                nd = HD + (ph == "b")
                qstack, kstack = qstacks[odd], kstacks[odd]
                if not start:
                    sp.wait_ge(s["exp_in"], 2 * EXPS * (c - 1))
                for par in range(2):
                    r = HEADROWS * par + MAXROW
                    h0 = 8 * par + 4 * half
                    sp.dma_start(qstack[r:r + 3, 4 * half:4 * half + 4, :],
                                 kstack[r + 3:r + 6, h0:h0 + 4, :]).then_inc(s["stacked"][half], 16)
                sp.wait_ge(s["parts_written"], WRITTEN * (c + 1))
                for side in range(2):
                    n = len(JQ) * 16 * nd
                    blocks = stack_dram[side * n:(side + 1) * n, :].rearrange(
                        "(i q d t) n -> q i d t n", i=len(JQ), q=4, t=4)
                    for par in range(2):
                        r = HEADROWS * par
                        if side == 0:
                            dst = qstack[r:r + len(JQ) * nd, 4 * half:4 * half + 4, :]
                        else:
                            dst = kstack[r:r + len(JQ) * nd, 8 * par + 4 * half:8 * par + 4 * half + 4, :]
                        sp.dma_start(dst, blocks[2 * par + half]).then_inc(s["stacked"][half], 16)

            def max_rows(ph, c, odd, half):
                s = att[ph]
                sp.wait_ge(s["maxparts_ready"], 2 * c + half + 1)
                for j in range(3):
                    r = MAXROW + j
                    sp.dma_start(qstacks[odd][r:r + HEADROWS + 1:HEADROWS, 4 * half:4 * half + 4, :].rearrange(
                        "j t (q n) -> j (t q) n", n=P), maxparts[:, half, j, :]).then_inc(s["maxrows"][half], 16)

            def store_rows(ph, c):
                s = att[ph]
                sp.wait_ge(s["norm2_ready"], NT * c + NT)
                sp.dma_start(xn_dram[ds(c * S, S), :].rearrange("(t p) d -> p t d", p=P),
                             xn2[:]).then_inc(s["rows_stored"], 16)

            def rows_are_stored(ph, c):
                s = att[ph]
                sp.wait_ge(s["rows_stored"], 16 * c + 16)
                sp.sem_inc(s["rows_free"], 1)

            def batch(ph, b, odd, prev, nxt, nxt2):
                if nxt2 and ph == "b":
                    load_rows(b + 2, False)
                if nxt:
                    write_parts(ph, b + 1, False)
                max_rows(ph, b, odd, 1)
                if nxt:
                    for half in range(2):
                        stack(ph, b + 1, 1 - odd, half, not prev)
                if prev:
                    store_rows(ph, b - 1)
                if nxt:
                    max_rows(ph, b + 1, 1 - odd, 0)
                if prev:
                    rows_are_stored(ph, b - 1)

            def attention(ph):
                if ph == "b":
                    load_rows(0, True)
                    sp.wait_ge(first["tables"], TABLES + 2)
                    for par in range(2):
                        r = HEADROWS * par + MAXROW
                        sp.dma_start(kstacks[0][r:r + 3, 8 * par:8 * par + 8, :],
                                     one_bf).then_inc(first["ready"], 16)
                    sp.wait_ge(first["ready"], 10 * 16)
                write_parts(ph, 0, True)
                if ph == "b":
                    load_rows(1, False)
                stack(ph, 0, 0, 0, True)
                stack(ph, 0, 0, 1, True)
                max_rows(ph, 0, 0, 0)
                if ph == "a":
                    later_loads()
                run_batches(sp, ph, batch)
                swap_in(ph)
                store_rows(ph, B - 1)
                rows_are_stored(ph, B - 1)

            def experts(n):
                r0 = n * ROUNDS
                sp.wait_ge(f["table"], n + 1)
                sp.wait_ge(att["ab"[n]]["scattered"], B * NT * TOPK * 16)

                def load_entries(i, k, first_round):
                    slot = sp.value_load(tile_tab[0:1, 1, ds(ROUND * i + k, 1)], min_val=0, max_val=NO_LIST)
                    if not first_round:
                        sp.wait_ge(f["scattered"][k % 4], 16 * (2 * (i + r0 - 1) + k // 4 + 1))
                    sp.dma_start(entry[:, k, :], list_dram[ds(slot, P), :]).then_inc(f["entry"][k], 16)

                for k in range(ROUND):
                    load_entries(0, k, True)
                with sp.Fori(1, ROUNDS) as i:
                    for k in range(ROUND):
                        load_entries(i, k, False)

            def rows_written(n):
                for k in range(4):
                    sp.wait_ge(f["scattered"][k], 16 * (n + 1) * TILES // 4)

            sp.wait_ge(first["ready"], 8 * 16)
            attention("a")
            experts(0)
            rows_written(0)
            sp.dma_start(list_dram[0:NO_LIST, :].rearrange("(p n) c -> p (n c)", p=P),
                         list_fill[:]).then_inc(first["emptied"], 16)
            attention("b")
            experts(1)
            rows_written(1)
            for b in range(B):
                for k in range(TOPK):
                    sp.dma_start(last_rows[:, b, k, :, :],
                                 y_dram[b * S + k * TOK:(b + 1) * S + k * TOK, :].rearrange(
                                     "(t p) d -> p t d", p=P)).then_inc(last_loaded[b], 16)
            for b in range(B):
                sp.wait_ge(last["combined"], b + 1)
                sp.dma_start(out[b * S:(b + 1) * S, :].rearrange("(t p) d -> p t d", p=P),
                             x[:, b * NT:(b + 1) * NT, :]).then_inc(last["stored"], 16)
            sp.wait_ge(last["stored"], 16 * B)

        @block.gpsimd
        def _(pool):
            nc.gpsimd.memset(one_bf, 1.0).then_inc(first["tables"], 1)
            nc.gpsimd.memset(stacks_f32[1], 0.0).then_inc(first["tables"], 1)
            nc.gpsimd.memset(stacks_f32[0], 0.0).then_inc(first["tables"], 1)
            nc.gpsimd.iota(list_fill[:].rearrange("p (r n c) -> p r n c", n=P, c=2),
                           [[0, 2 * LIST * E // P // P // 2], [1, P], [TOK, 2]], base=TOK,
                           channel_multiplier=0).then_inc(first["tables"], 1)
            pool.sem_inc(att["a"]["entries_free"], 1)
            pool.sem_inc(att["b"]["entries_free"], 1)
            for ph in "ab":
                pool.sem_inc(att[ph]["part_ready"], 3)

            def rstd_of(ph, which, c, have, done):
                s = att[ph]
                pool.wait_ge(s[have], c + 1)
                nc.gpsimd.tensor_tensor(rstd[:, which, :], var_eps[:, which, :], neghalf[:],
                                        ALU.pow).then_inc(s[done], 1)

            def add_expert_rows(c):
                s = att["b"]
                chain = rows_chain
                chain.round(c)
                pool.wait_ge(s["y_loaded"], TOPK * 16 * (c + 1))
                xb = x[:, ds(c * NT, NT), :]
                plain(pool)
                for k in range(TOPK):
                    g = gates[:, ds(c * NT, NT), k:k + 1].to_broadcast([P, NT, D])
                    chain.mark(nc.gpsimd.tensor_tensor(ystage[:, k, :, :], ystage[:, k, :, :], g, ALU.mult))
                chain.settle()
                plain(pool)
                chain.link(nc.gpsimd.tensor_tensor(xb, xb, ystage[:, 0, :, :], ALU.add))
                plain(pool)
                nc.gpsimd.tensor_tensor(xb, xb, ystage[:, 1, :, :], ALU.add).then_inc(s["combined"], 1)

            def sinh_series(c):
                s = att["b"]
                chain = rows_chain
                pool.wait_ge(s["norm_in"], c + 1)
                u, ser = em[:, 0, :], em[:, 7, :]
                plain(pool)
                chain.link(nc.gpsimd.tensor_scalar(ser, u, 1.0 / 39916800.0, 1.0 / 362880.0, ALU.mult, ALU.add))
                for k in (1.0 / 5040.0, 1.0 / 120.0, 1.0 / 6.0, 1.0):
                    chain.link(nc.gpsimd.tensor_tensor(ser, ser, u, ALU.mult))
                    plain(pool)
                    chain.link(nc.gpsimd.tensor_scalar(ser, ser, k, None, ALU.add))
                plain(pool)
                chain.mark(nc.gpsimd.tensor_scalar(em_small[:], u, 1.0, None, ALU.is_lt))
                chain.end()

            def log_roots(c):
                s = att["b"]
                pool.wait_ge(s["nc_in"], c + 1)
                nc.gpsimd.tensor_tensor(lm[:, 2:4, :], lm[:, 0:2, :],
                                        half[:, 0:2 * NT].rearrange("p (a t) -> p a t", t=NT),
                                        ALU.pow).then_inc(s["nc_ready"], 1)

            def scatter_entries(ph, c):
                s = att[ph]
                pool.wait_ge(s["entries_ready"], c + 1)
                plain(pool)
                for t in range(NT):
                    for k in range(TOPK):
                        nc.gpsimd.indirect_dma_start(
                            list_dram[:, :], IndirectOffsetOnAxis(slots[:, k, t:t + 1], 0),
                            entries[:, t, k, :], None).then_inc(s["scattered"], 16)

            def entries_are_scattered(ph, c):
                s = att[ph]
                pool.wait_ge(s["scattered"], (c + 1) * NT * TOPK * 16)
                pool.sem_inc(s["entries_free"], 1)

            def batch(ph, b, odd, prev, nxt, nxt2):
                if nxt:
                    split(pool, pool_chain[ph], ph, b + 1, False)
                if prev:
                    rstd_of(ph, 1, b - 1, "norm2_var", "norm2_rstd")
                if nxt2:
                    if ph == "b":
                        add_expert_rows(b + 2)
                    rstd_of(ph, 0, b + 2, "norm_var", "norm_rstd")
                    if ph == "b":
                        log_roots(b + 2)
                if prev:
                    scatter_entries(ph, b - 1)
                if nxt2 and ph == "b":
                    sinh_series(b + 2)
                if prev:
                    entries_are_scattered(ph, b - 1)

            def attention(ph):
                if ph == "b":
                    pool.wait_ge(f["y_copied"], TILES)
                    nc.gpsimd.memset(stacks_f32[0], 0.0).then_inc(first["tables"], 1)
                    nc.gpsimd.memset(one_bf, 1.0).then_inc(first["tables"], 1)
                for c in range(2):
                    if ph == "b":
                        add_expert_rows(c)
                    rstd_of(ph, 0, c, "norm_var", "norm_rstd")
                    if ph == "b":
                        log_roots(c)
                        sinh_series(c)
                pool.wait_ge(first["emptied"], 2 * 16 if ph == "a" else 3 * 16)
                run_batches(pool, ph, batch)
                rstd_of(ph, 1, B - 1, "norm2_var", "norm2_rstd")
                scatter_entries(ph, B - 1)
                entries_are_scattered(ph, B - 1)

            rows_chain = Chain(pool, att["b"]["pool_step"], POOL_STEPS)
            pool_chain = {ph: Chain(pool, att[ph]["remainder"], 1) for ph in "ab"}

            def experts(n):
                r0 = n * ROUNDS

                def gather(i, k, start):
                    pool.wait_ge(f["entry"][k], 16 * (i + r0) + 16)
                    if not start:
                        pool.wait_ge(f["xT_ready"], ROUND * (i + r0) + k - 3)
                        plain(pool)
                    nc.gpsimd.indirect_dma_start(
                        xg[:, k % 4, :], None, xn_dram[:, :],
                        IndirectOffsetOnAxis(entry[:, k, 0:1], 0)).then_inc(f["gathered"][k % 4], 16)

                def scatter(i, k):
                    pool.wait_ge(f["y_copied"], ROUND * (i + r0) + k + 1)
                    plain(pool)
                    nc.gpsimd.indirect_dma_start(
                        y_dram[:, :], IndirectOffsetOnAxis(entry[:, k, 1:2], 0), yrow[:, k % 4, :], None,
                        bounds_check=TOPK * TOK - 1, oob_is_err=False).then_inc(f["scattered"][k % 4], 16)

                for k in range(ROUND):
                    gather(0, k, k < 4)
                    if k >= BEHIND:
                        scatter(0, k - BEHIND)
                with pool.Fori(1, ROUNDS) as i:
                    for k in range(ROUND):
                        gather(i, k, False)
                        scatter(i - (k < BEHIND), (k - BEHIND) % ROUND)
                for k in range(ROUND - BEHIND, ROUND):
                    scatter(ROUNDS - 1, k)

            attention("a")
            experts(0)
            attention("b")
            experts(1)

        @block.scalar
        def _(act):
            for ph in "ab":
                act.sem_inc(att[ph]["exp_done"], 1)
                act.sem_inc(att[ph]["o_copied"], 1)
                act.sem_inc(att[ph]["v_spread"], 2)

            def exponential(ph, b, half, i):
                s = att[ph]
                quad, h = divmod(i, 4)
                w = S - first_query(ph, quad % NT)
                if h == 0:
                    act.wait_ge(s["pv_ready"], QUADS * (2 * b + half) + quad + 1)
                act.wait_ge(s["exp_in"], EXPS * (2 * b + half) + i + 1)
                nc.scalar.activation(probs[:, quad % 4, h, 0:w], ps[:, BANKS + i % BANKS, 0:w], ACT.Exp,
                                     scale=SCALE).then_inc(s["exp_done"], 1)

            def copy_out(ph, b, g, prev=False):
                s = att[ph]
                if g == 0 and prev:
                    act.wait_ge(s["oT_ready"], NT * b)
                act.wait_ge(s["pv_ready"], 2 * QUADS * b + NT * (g + 1) + 4)
                nc.scalar.copy(oT[:, g, :], outT).then_inc(s["o_copied"], 1)

            def spread_v(ph, c, half, start):
                s = att[ph]
                act.wait_ge(s["v_staged"], c + 1)
                if not start:
                    act.wait_ge(s["pv_ready"], 2 * QUADS * (c - 1) + QUADS * (half + 1) + 4)
                for par in range(2):
                    h0 = 8 * par + 4 * half
                    ins = nc.scalar.copy(vones[:, :, h0:h0 + 4, 0:HD],
                                         vstage[:, :, h0 * HD:(h0 + 4) * HD].rearrange("p t (h d) -> p t h d", d=HD))
                ins.then_inc(s["v_spread"], 1)

            def side(ph, name, b, start=False):
                s = att[ph]
                if name == "vcopy0":
                    spread_v(ph, b + 1, 0, start)
                if name == "vcopy1":
                    spread_v(ph, b, 1, start)
                if name == "onormT":
                    act.wait_ge(s["onormT_ready"], b)
                    nc.scalar.copy(onormT[:], misc).then_inc(s["onormT_copied"], 1)
                if name == "norm2T":
                    act.wait_ge(s["norm2T_ready"], b)
                    nc.scalar.copy(xn2T[:], misc).then_inc(s["norm2T_copied"], 1)
                if name == "rexp":
                    act.wait_ge(s["route_exp_in"], b)
                    nc.scalar.activation(rt[:, 9, :, :], rt[:, 8, :, :], ACT.Exp).then_inc(s["route_exp"], 1)
                if name == "vproj" and ph == "a":
                    act.wait_ge(s["v_ready"], b + 2)
                    act.wait_ge(s["v_spread"], 2 * (b + 2))
                    nc.scalar.copy(vstage[:], misc4(D)).then_inc(s["v_staged"], 1)
                if name == "ln":
                    act.wait_ge(s["ln_in"], b + 3)
                    nc.scalar.activation(lm[:, 5, :], lm[:, 4, :], ACT.Ln).then_inc(s["ln_ready"], 1)
                if name == "normT":
                    act.wait_ge(s["normT_ready"], b + 3)
                    nc.scalar.copy(xnT[:], misc).then_inc(s["normT_copied"], 1)
                if name == "square":
                    act.wait_ge(s["proj_read"], 2 * (b + 3))
                    nc.scalar.activation(qk_sq, qk, ACT.Square).then_inc(s["square_done"], 1)
                if name == "root":
                    act.wait_ge(s["norm_in"], b + 3)
                    nc.scalar.activation(em[:, 2, :], em[:, 0, :], ACT.Ln).then_inc(s["log_done"], 1)
                    act.wait_ge(s["log_done"], 2 * (b + 2) + 1)
                    nc.scalar.activation(em[:, 1, :], em[:, 2, :], ACT.Exp, scale=0.5).then_inc(s["norm_out"], 1)
                if name == "sinh":
                    act.wait_ge(s["root_ready"], b + 3)
                    nc.scalar.activation(em[:, 2, :], em[:, 1, :], ACT.Exp, scale=0.5).then_inc(s["exp_sh"], 1)
                    nc.scalar.activation(em[:, 3, :], em[:, 1, :], ACT.Exp, scale=-0.5).then_inc(s["exp_sh"], 1)
                if name == "time":
                    act.wait_ge(s["time_in"], b + 3)
                    nc.scalar.activation(em[:, 2, :], em[:, 6, :], ACT.Ln).then_inc(s["log_done"], 1)
                    act.wait_ge(s["log_done"], 2 * (b + 2) + 2)
                    nc.scalar.activation(em[:, 1, :], em[:, 2, :], ACT.Exp, scale=0.5).then_inc(s["time_out"], 1)
                if name[:4] == "hypT":
                    i = int(name[4])
                    act.wait_ge(s["hypT_ready"], 4 * (b + 1) + i + 1)
                    if i == 0:
                        act.wait_ge(s["part_ready"], last_parts(ph, b + 1))
                        if not start:
                            act.wait_ge(s["parts_written"], WRITTEN * (b + 1))
                    cast = nc.scalar.copy(parts[0:72, 0, i * S:(i + 1) * S], misc[0:72, :])
                    if i == 3:
                        cast.then_inc(s["part_ready"], 1)
                    nc.scalar.copy(hypT[:, i, :], misc[0:72, :]).then_inc(s["hypT_copied"], 1)

            def part(ph, b, half, prev, sequence):
                for kind, i in sequence:
                    if kind == "e":
                        exponential(ph, b, half, i)
                        if i == 4 and (half or prev):
                            copy_out(ph, b if half else b - 1, 1 if half else GROUPS - 1)
                        if i == EXPS // 2 + 4:
                            copy_out(ph, b, 2 * half, prev)
                    if kind == "side":
                        side(ph, i, b, start=not prev and i == "vcopy1")

            def batch(ph, b, odd, prev, nxt, nxt2):
                part(ph, b, 0, prev, first_order(ph, prev, nxt))
                part(ph, b, 1, True, second_order(ph, prev, nxt, nxt2))

            def attention(ph):
                for name in PREP[ph]:
                    side(ph, name, -2)
                for name in PREP_END[ph]:
                    side(ph, name, -1, start=True)
                side(ph, "vproj", -1)
                for kind, name in second_order(ph, False, True, True, e=False):
                    if kind == "side":
                        side(ph, name, -1, start=name == "vcopy0")
                run_batches(act, ph, batch)
                copy_out(ph, B - 1, GROUPS - 1)
                for name in POST:
                    side(ph, name, B)

            def experts(n):
                r0 = n * ROUNDS

                def rows(i, k):
                    act.wait_ge(f["xT_ready"], ROUND * (i + r0) + k + 1)
                    nc.scalar.copy(xgT[:, k % 2, :], misc[:, 0:P]).then_inc(f["xT_copied"], 1)

                def relu(i, k):
                    act.wait_ge(f["hT_ready"], ROUND * (i + r0) + k + 1)
                    nc.scalar.activation(hidT[:, k % 2, :, :], ps[:, 2 + k % 2, :].rearrange(
                        "p (f n) -> p f n", n=P), ACT.Relu).then_inc(f["hT_copied"], 1)

                for k in range(ROUND):
                    rows(0, k)
                    if k >= 1:
                        relu(0, k - 1)
                with act.Fori(1, ROUNDS) as i:
                    for k in range(ROUND):
                        rows(i, k)
                        relu(i - (k < 1), (k - 1) % ROUND)
                relu(ROUNDS - 1, ROUND - 1)

            act.wait_ge(first["const"], 4 * 16)
            attention("a")
            experts(0)
            attention("b")
            experts(1)

        @block.vector
        def _(dve):
            nc.vector.memset(vones[:], 0.0).then_inc(first["clear"], 1)
            nc.vector.memset(outT, 0.0).then_inc(first["tables"], 1)
            nc.vector.memset(onormT[:], 0.0).then_inc(first["tables"], 1)
            nc.vector.memset(half[:], 0.5).then_inc(first["tables"], 1)
            nc.vector.memset(neghalf[:], -0.5).then_inc(first["tables"], 1)
            nc.vector.memset(counts[:], 0.0).then_inc(first["tables"], 1)
            dve.wait_ge(first["clear"], 1)
            nc.vector.memset(vones[:, :, :, HD:HD + 1], 1.0).then_inc(first["tables"], 1)
            dve.sem_inc(att["a"]["max_done"], 1)
            dve.sem_inc(att["b"]["max_done"], 1)

            chains = {ph: [Chain(dve, att[ph][name], n) for name, n in
                           zip(("dve_prep", "dve_post", "dve_max"), DVE_STEPS[ph])] for ph in "ab"}

            def moments_of(b, which, chain):
                plain(dve)
                for t in range(NT):
                    chain.mark(nc.vector.bn_stats(stats[:, which, t, :], x[:, ds(b * NT + t, 1), :]))
                yield None
                chain.settle()
                plain(dve)
                for t in range(NT):
                    chain.mark(nc.vector.bn_aggr(moments[:, which, t, :], stats[:, which, t, :]))
                yield None
                chain.settle()

            def add_eps(which):
                return nc.vector.tensor_scalar(var_eps[:, which, :], moments[:, which, :, 1], EPS, None, ALU.add)

            def normalised(b, t, which, dst, factor):
                return nc.vector.tensor_scalar(dst[:, t, :], x[:, ds(b * NT + t, 1), :].rearrange("p a d -> p (a d)"),
                                               moments[:, which, t, 0:1], factor[:, t:t + 1],
                                               ALU.subtract, ALU.mult)

            def add_rows(rows, b, chain, done):
                xb = x[:, ds(b * NT, NT), :]
                for k in range(TOPK):
                    g = gates[:, ds(b * NT, NT), k:k + 1].to_broadcast([P, NT, D])
                    chain.mark(nc.vector.tensor_tensor(rows[:, k, :, :], rows[:, k, :, :], g, ALU.mult))
                yield None
                chain.settle()
                chain.mark(nc.vector.tensor_tensor(xb, xb, rows[:, 0, :, :], ALU.add))
                yield None
                chain.settle()
                nc.vector.tensor_tensor(xb, xb, rows[:, 1, :, :], ALU.add).then_inc(done, 1)

            def rope(c):
                s = att["a"]
                for i in range(2):
                    yield f"proj{2 * i}"
                    dve.wait_ge(s["proj_ready"], 4 * c + 2 * i + 1)
                    nc.vector.tensor_tensor(rope_c, misc, cos_t, ALU.mult).then_inc(s["proj_read"], 1)
                    yield f"proj{2 * i + 1}"
                    dve.wait_ge(s["proj_ready"], 4 * c + 2 * i + 2)
                    nc.vector.tensor_tensor(rope_s, misc, sin_t, ALU.mult).then_inc(s["proj_read"], 1)
                    yield None
                    dve.wait_ge(s["proj_read"], 4 * c + 2 * i + 2)
                    dve.wait_ge(s["part_ready"], last_parts("a", c))
                    nc.vector.tensor_tensor(qrot[:, i, :], rope_c, rope_s, ALU.add).then_inc(s["rot_ready"], 1)
                    dve.wait_ge(s["rot_ready"], 2 * c + i + 1)

            def log_map(c, chain):
                s = att["b"]
                u, u1, root, root1, arg, ln, rec, ser, coef, rr, var, scale = (lm[:, i, :] for i in range(12))
                chain.mark(nc.vector.tensor_tensor(rr, rstd[:, 0, :], rstd[:, 0, :], ALU.mult))
                yield None
                chain.settle()
                chain.mark(nc.vector.tensor_tensor(var, moments[:, 0, :, 1], rr, ALU.mult))
                yield None
                chain.settle()
                chain.link(nc.vector.tensor_scalar(u, var, float(D), curv[:, 0:1], ALU.mult, ALU.mult))
                nc.vector.tensor_scalar(u1, u, 1.0, None, ALU.add).then_inc(s["nc_in"], 1)
                chain.mark(nc.vector.tensor_scalar(ser, u, 105.0 / 3456.0, None, ALU.mult))
                for k in (-15.0 / 336.0, 3.0 / 40.0, -1.0 / 6.0):
                    yield None
                    chain.settle()
                    chain.mark(nc.vector.scalar_tensor_tensor(ser, ser, k, u, ALU.add, ALU.mult))
                yield None
                chain.settle()
                chain.mark(nc.vector.tensor_scalar(ser, ser, 1.0, None, ALU.add))
                chain.mark(nc.vector.tensor_scalar(lm_small[:], u, 0.06, None, ALU.is_lt))
                yield "nc"
                dve.wait_ge(s["nc_ready"], c + 1)
                nc.vector.tensor_tensor(arg, root, root1, ALU.add).then_inc(s["ln_in"], 1)
                chain.mark(nc.vector.tensor_scalar(rec, root, 1e-30, None, ALU.max))
                yield None
                chain.settle()
                chain.mark(nc.vector.reciprocal(rec, rec))
                yield "ln"
                chain.settle()
                dve.wait_ge(s["ln_ready"], c + 1)
                chain.mark(nc.vector.tensor_tensor(coef, ln, rec, ALU.mult))
                yield None
                chain.settle()
                plain(dve)
                chain.mark(nc.vector.copy_predicated(coef, lm_small[:], ser))
                yield None
                chain.settle()
                chain.link(nc.vector.tensor_tensor(scale, coef, rstd[:, 0, :], ALU.mult))

            def exp_map(c, chain):
                s = att["b"]
                u, root, ep, en, n2, coef, t2, ser = (em[:, i, :] for i in range(8))
                yield "square"
                dve.wait_ge(s["square_done"], c + 1)
                chain.mark(nc.vector.tensor_reduce(n2, qk_sq.rearrange("p (m d) -> p m d", d=HD),
                                                   axis=X_AXIS, op=ALU.add))
                yield None
                chain.settle()
                nc.vector.tensor_scalar(u, n2, curv[:, 0:1], 1e-30, ALU.mult, ALU.max).then_inc(s["norm_in"], 1)
                yield "root"
                dve.wait_ge(s["norm_out"], c + 1)
                chain.mark(nc.vector.reciprocal(t2, root))
                yield None
                chain.settle()
                chain.mark(nc.vector.tensor_tensor(t2, t2, u, ALU.mult))
                yield None
                chain.settle()
                nc.vector.tensor_tensor(root, root, t2, ALU.add).then_inc(s["root_ready"], 1)
                dve.wait_ge(s["root_ready"], c + 1)
                chain.mark(nc.vector.reciprocal(t2, root))
                yield "sinh"
                chain.settle()
                dve.wait_ge(s["exp_sh"], 2 * c + 2)
                chain.mark(nc.vector.tensor_tensor(ep, ep, en, ALU.subtract))
                yield None
                chain.settle()
                chain.mark(nc.vector.tensor_tensor(coef, ep, t2, ALU.mult))
                yield None
                chain.settle()
                dve.wait_ge(s["pool_step"], POOL_STEPS * (c + 1))
                plain(dve)
                chain.mark(nc.vector.copy_predicated(coef, em_small[:], ser))
                yield None
                chain.settle()
                chain.mark(nc.vector.tensor_tensor(ser, coef, coef, ALU.mult))
                yield None
                chain.settle()
                chain.mark(nc.vector.tensor_tensor(ser, ser, n2, ALU.mult))
                yield None
                chain.settle()
                nc.vector.tensor_scalar(t2, ser, inv_curv[:, 0:1], None, ALU.add).then_inc(s["time_in"], 1)
                kc = coef.rearrange("p (a c h) -> p a c h", a=NT, c=2)[:, :, 1, :]
                chain.mark(nc.vector.tensor_scalar(kc, kc, -1.0, None, ALU.mult))
                yield None
                chain.settle()
                nc.vector.tensor_tensor(
                    hyp[:, :, 0:32].rearrange("p m (d t) -> p m t d", t=4),
                    qk.rearrange("p (m t d) -> p m t d", t=4, d=HD),
                    coef.rearrange("p (m t) -> p m t", t=4).unsqueeze(3).to_broadcast([P, NT * 8, 4, HD]),
                    ALU.mult).then_inc(s["hyp_ready"], 1)
                yield "time"
                dve.wait_ge(s["time_out"], c + 1)
                chain.mark(nc.vector.reciprocal(ep, root))
                yield None
                chain.settle()
                chain.mark(nc.vector.tensor_tensor(ep, ep, t2, ALU.mult))
                yield None
                chain.settle()
                chain.mark(nc.vector.tensor_tensor(ep, ep, root, ALU.add))
                yield None
                chain.settle()
                nc.vector.tensor_scalar(hyp[:, :, 32:36], ep.rearrange("p (m t) -> p m t", t=4), 0.5, None,
                                        ALU.mult).then_inc(s["time_ready"], 1)

            def prep(ph, c):
                s = att[ph]
                chain = chains[ph][0]
                chain.round(c)
                if ph == "b":
                    yield "rows"
                    dve.wait_ge(s["combined"], c + 1)
                yield from moments_of(c, 0, chain)
                add_eps(0).then_inc(s["norm_var"], 1)
                yield "rstd"
                dve.wait_ge(s["norm_rstd"], c + 1)
                scale = rstd[:, 0, :]
                if ph == "b":
                    yield from log_map(c, chain)
                    scale = lm[:, 11, :]
                for t in range(NT):
                    normalised(c, t, 0, xn, scale).then_inc(s["norm_ready"], 1)
                if ph == "a":
                    yield from rope(c)
                else:
                    for i in range(2):
                        yield f"proj{i}"
                        dve.wait_ge(s["proj_ready"], 2 * c + i + 1)
                        nc.vector.tensor_tensor(
                            qk.rearrange("p (t n) -> p t n", t=NT)[:, 2 * i:2 * i + 2, :],
                            misc.rearrange("p (t n) -> p t n", t=2),
                            bias_qkv[:, 0:2 * D].unsqueeze(1).to_broadcast([P, 2, 2 * D]),
                            ALU.add).then_inc(s["proj_read"], 1)
                    yield from exp_map(c, chain)
                chain.end()

            def add_v_bias(c):
                s = att["b"]
                yield "vproj"
                dve.wait_ge(s["v_ready"], c + 1)
                dve.wait_ge(s["v_spread"], 2 * (c + 1))
                nc.vector.tensor_tensor(vstage[:], misc4(D),
                                        bias_qkv[:, 2 * D:3 * D].unsqueeze(1).to_broadcast([P, NT, D]),
                                        ALU.add).then_inc(s["v_staged"], 1)

            def post(ph, c):
                s = att[ph]
                chain = chains[ph][1]
                chain.round(c)
                heads = misc.rearrange("p (h c) -> p h c", c=32)
                for t in range(NT):
                    yield f"oT{t}"
                    dve.wait_ge(s["oT_ready"], NT * c + t + 1)
                    chain.mark(nc.vector.reciprocal(rsum[:], heads[:, :, HD]))
                    yield None
                    chain.settle()
                    nc.vector.tensor_tensor(onorm[:, t, :].rearrange("p (h d) -> p h d", d=HD), heads[:, :, 0:HD],
                                            rsum[:].unsqueeze(2).to_broadcast([P, H, HD]),
                                            ALU.mult).then_inc(s["onorm_ready"], 1)
                xb = x[:, ds(c * NT, NT), :]
                yield "oproj"
                dve.wait_ge(s["oproj_ready"], c + 1)
                nc.vector.tensor_tensor(xb, xb, misc4(D), ALU.add).then_inc(s["post_read"], 1)
                yield None
                dve.wait_ge(s["post_read"], 3 * c + 1)
                if ph == "b":
                    chain.mark(nc.vector.tensor_tensor(xb, xb, bias_o[:].unsqueeze(1).to_broadcast([P, NT, D]), ALU.add))
                    yield None
                    chain.settle()
                yield from moments_of(c, 1, chain)
                add_eps(1).then_inc(s["norm2_var"], 1)
                yield "rstd2"
                dve.wait_ge(s["norm2_rstd"], c + 1)
                dve.wait_ge(s["rows_free"], c + 1)
                for t in range(NT):
                    normalised(c, t, 1, xn2, rstd[:, 1, :]).then_inc(s["norm2_ready"], 1)

                logit, eq, sc, top1, logit2, top2, both, place, shifted, ex, tmp = (rt[:, i] for i in range(11))
                m1, w1_, m2, w2_, total, e2, p1, p2, den, rs, pl1, pl2 = (rk[:, i, :] for i in range(12))

                def over(v):
                    return v.unsqueeze(2).to_broadcast([P, NT, E])

                def best(of, m, w, top):
                    chain.mark(nc.vector.tensor_reduce(m, of, axis=X_AXIS, op=ALU.max))
                    yield None
                    chain.settle()
                    chain.mark(nc.vector.tensor_tensor(eq, of, over(m), ALU.is_equal))
                    yield None
                    chain.settle()
                    chain.mark(nc.vector.tensor_tensor(sc, eq, pick, ALU.mult))
                    yield None
                    chain.settle()
                    chain.mark(nc.vector.tensor_reduce(w, sc, axis=X_AXIS, op=ALU.max))
                    yield None
                    chain.settle()
                    chain.mark(nc.vector.tensor_tensor(top, sc, over(w), ALU.is_equal))
                    yield None
                    chain.settle()

                yield "logits"
                dve.wait_ge(s["logits_ready"], c + 1)
                nc.vector.tensor_copy(logit, misc4(E)).then_inc(s["post_read"], 1)
                yield None
                dve.wait_ge(s["post_read"], 3 * c + 2)
                yield from best(logit, m1, w1_, top1)
                nc.vector.tensor_tensor(shifted, logit, over(m1), ALU.subtract).then_inc(s["route_exp_in"], 1)
                chain.mark(nc.vector.scalar_tensor_tensor(logit2, top1, MASKED, logit, ALU.mult, ALU.add))
                yield None
                chain.settle()
                yield from best(logit2, m2, w2_, top2)
                nc.vector.tensor_tensor(tops_bf[:], top1, top2, ALU.add).then_inc(s["tops_ready"], 1)
                yield "rexp"
                dve.wait_ge(s["route_exp"], c + 1)
                chain.mark(nc.vector.tensor_reduce(total, ex, axis=X_AXIS, op=ALU.add))
                chain.mark(nc.vector.tensor_tensor(tmp, ex, top2, ALU.mult))
                yield None
                chain.settle()
                chain.mark(nc.vector.reciprocal(p1, total))
                chain.mark(nc.vector.tensor_reduce(e2, tmp, axis=X_AXIS, op=ALU.add))
                yield None
                chain.settle()
                chain.mark(nc.vector.tensor_tensor(p2, e2, p1, ALU.mult))
                yield None
                chain.settle()
                chain.mark(nc.vector.tensor_tensor(den, p1, p2, ALU.add))
                yield None
                chain.settle()
                chain.mark(nc.vector.tensor_scalar(den, den, 1e-9, None, ALU.add))
                yield None
                chain.settle()
                chain.mark(nc.vector.reciprocal(rs, den))
                yield None
                chain.settle()
                for k, p in enumerate((p1, p2)):
                    chain.mark(nc.vector.tensor_tensor(gates[:, ds(c * NT, NT), k], p, rs, ALU.mult))

            def places(ph, c):
                s = att[ph]
                chain = chains[ph][1]
                top1, top2, place, tmp = (rt[:, i] for i in (3, 5, 7, 10))
                yield "rank"
                dve.wait_ge(s["rank_ready"], c + 1)
                chain.link(nc.vector.tensor_tensor(
                    place, misc[:, 0:NT * E].rearrange("p (t e) -> p t e", e=E),
                    counts[:].unsqueeze(1).to_broadcast([P, NT, E]), ALU.add))
                nc.vector.tensor_tensor(counts[:], counts[:], misc[:, NT * E:NT * E + E],
                                        ALU.add).then_inc(s["post_read"], 1)
                chain.mark(nc.vector.tensor_tensor(place, place, listbase, ALU.add))
                yield None
                chain.settle()
                dve.wait_ge(s["entries_free"], c + 1)
                for k, (top, pl) in enumerate(((top1, rk[:, 10, :]), (top2, rk[:, 11, :]))):
                    chain.mark(nc.vector.tensor_tensor(tmp, place, top, ALU.mult))
                    yield None
                    chain.settle()
                    chain.mark(nc.vector.tensor_reduce(pl, tmp, axis=X_AXIS, op=ALU.add))
                    yield None
                    chain.settle()
                    chain.mark(nc.vector.tensor_copy(slots[:, k, :], pl))
                nc.vector.tensor_copy(entries[:].rearrange("p t k c -> p (t k c)"), ids[:]).then_inc(s["entries_ready"], 1)
                dve.wait_ge(s["entries_ready"], c + 1)
                chain.link(nc.vector.tensor_scalar(ids[:], ids[:], float(S), None, ALU.add))
                chain.end()

            class Pieces:
                def __init__(self, *flows):
                    self.flow = (piece for flow in flows for piece in flow)
                    self.needs = next(self.flow, "end")

                def some(self, n):
                    while self.needs is None and n > 0:
                        self.needs = next(self.flow, "end")
                        n -= 1

                def reach(self, name):
                    self.some(1000)
                    if self.needs == name:
                        self.needs = next(self.flow, "end")

                def finish(self):
                    self.some(1000)
                    assert self.needs == "end", self.needs

            def maximum(ph, b, half, i):
                s = att[ph]
                base = SCORES[ph] * (2 * b + half)
                dve.wait_ge(s["scores_ready"], base + i + 1)
                if i < len(UNITS[ph]):
                    g, q, h0, nh = UNITS[ph][i]
                    w = (q + 1) * P if ph == "a" else S
                    nc.vector.tensor_reduce(
                        negmax[:, half, :].rearrange("p (g t q) -> p g t q", g=2, q=NT)[:, g, h0:h0 + nh, q],
                        ps[:, i % BANKS, 0:nh * w].rearrange("p (h k) -> p h k", h=nh),
                        axis=X_AXIS, op=ALU.max, negate=True).then_inc(s["max_done"], 1)
                    return
                chain = chains[ph][2]
                chain.round(2 * b + half)
                m = ps[0:32, i % BANKS, 0:P]
                chain.link(nc.vector.tensor_copy(maxparts[:, half, 0, :], m))
                nc.vector.tensor_tensor(maxrest[:], m, maxparts[:, half, 0, :], ALU.subtract).then_inc(s["max_done"], 1)
                dve.wait_ge(s["max_done"], base + i + 2)
                chain.link(nc.vector.tensor_copy(maxparts[:, half, 1, :], maxrest[:]))
                nc.vector.tensor_tensor(maxparts[:, half, 2, :], maxrest[:], maxparts[:, half, 1, :],
                                        ALU.subtract).then_inc(s["maxparts_ready"], 1)
                chain.end()

            def part(ph, b, half, sequence, side):
                for kind, i in sequence:
                    if kind == "s":
                        maximum(ph, b, half, i)
                        side.some(PIECES[ph])
                    if kind == "side":
                        side.reach(i)
                side.finish()

            def batch(ph, b, odd, prev, nxt, nxt2):
                flows = [post(ph, b - 1)] if prev else []
                if nxt and ph == "b":
                    flows.append(add_v_bias(b + 1))
                part(ph, b, 1, first_order(ph, prev, nxt), Pieces(*flows))
                flows = [places(ph, b - 1)] if prev else []
                if nxt2:
                    flows.append(prep(ph, b + 2))
                part(ph, b + 1, 0, second_order(ph, prev, nxt, nxt2), Pieces(*flows))

            def all_steps(names, *flows):
                side = Pieces(*flows)
                for name in names:
                    side.reach(name)
                side.finish()

            def attention(ph):
                all_steps(PREP[ph], prep(ph, 0))
                split(dve, Chain(dve, att[ph]["remainder"], 1), ph, 0, True)
                if ph == "b":
                    all_steps(["vproj"], add_v_bias(0))
                part(ph, 0, 0, second_order(ph, False, True, True, e=False), Pieces(prep(ph, 1)))
                dve.wait_ge(first["x"], 16)
                run_batches(dve, ph, batch)
                all_steps(POST + ["rank"], post(ph, B - 1), places(ph, B - 1))

            def experts(n):
                r0 = n * ROUNDS
                chain = Chain(dve, f["dve"], FFN_STEPS)
                chain.round(n)
                padded, ends, starts, offset = (lay[:, i, :] for i in range(4))
                chain.link(nc.vector.tensor_scalar(lay_i[:, 0, :], counts[:], float(P - 1), None, ALU.add))
                chain.link(nc.vector.tensor_scalar(lay_i[:, 1, :], lay_i[:, 0, :], 7, 7,
                                                   ALU.arith_shift_right, ALU.logical_shift_left))
                chain.link(nc.vector.tensor_copy(padded, lay_i[:, 1, :]))
                chain.link(nc.vector.tensor_copy(ends, padded))
                for e in range(1, E):
                    chain.link(nc.vector.tensor_tensor(ends[:, e:e + 1], ends[:, e:e + 1], ends[:, e - 1:e], ALU.add))
                chain.link(nc.vector.tensor_tensor(starts, ends, padded, ALU.subtract))
                chain.link(nc.vector.tensor_tensor(offset, listbase[:, 0, :], starts, ALU.subtract))
                chain.link(nc.vector.tensor_scalar(offset, offset, -float(NO_LIST), None, ALU.add))
                begun, ended, inside, entry_at = (tl[:, i] for i in range(4))

                def over(v):
                    return v[0:1, :].unsqueeze(1).to_broadcast([1, TILES, E])

                chain.link(nc.vector.tensor_tensor(begun, tilepos[:], over(starts), ALU.is_ge))
                chain.link(nc.vector.tensor_tensor(ended, tilepos[:], over(ends), ALU.is_ge))
                chain.link(nc.vector.tensor_tensor(inside, begun, ended, ALU.subtract))
                chain.link(nc.vector.tensor_tensor(entry_at, tilepos[:], over(offset), ALU.add))
                chain.link(nc.vector.tensor_tensor(entry_at, entry_at, inside, ALU.mult))
                chain.link(nc.vector.tensor_reduce(tile_f[:, 0, :], ended, axis=X_AXIS, op=ALU.add))
                chain.link(nc.vector.tensor_reduce(tile_f[:, 1, :], entry_at, axis=X_AXIS, op=ALU.add))
                chain.link(nc.vector.tensor_scalar(tile_tab[:, 0, :], tile_f[:, 0, :], float(E - 1), None, ALU.min))
                chain.link(nc.vector.memset(counts[:], 0.0))
                chain.link(nc.vector.tensor_scalar(ids[:], ids[:], -float(TOK), None, ALU.add))
                nc.vector.tensor_scalar(tile_tab[:, 1, :], tile_f[:, 1, :], float(NO_LIST), None,
                                        ALU.add).then_inc(f["table"], 1)
                chain.end()
                dve.wait_ge(f["table"], n + 1)
                dve.wait_ge(swapped, 2 * 16 * (n + 1))

                def expert(i, k):
                    return dve.value_load(tile_tab[0:1, 0, ds(ROUND * i + k, 1)], min_val=0, max_val=E - 1)

                def hidden(i, k, start, e):
                    dve.wait_ge(f["h_ready"], ROUND * (i + r0) + k + 1)
                    if not start:
                        dve.wait_ge(f["hT_ready"], ROUND * (i + r0) + k - 1)
                    nc.vector.tensor_tensor(hid[:, k % 2, :], ps[:, k % 2, :], b1[:, ds(e * FF, FF)],
                                            ALU.add).then_inc(f["h_copied"], 1)

                def result(i, k, start, e):
                    dve.wait_ge(f["y_ready"], ROUND * (i + r0) + k + 1)
                    if not start:
                        dve.wait_ge(f["scattered"][k % 4], 16 * (2 * (i + r0) + k // 4))
                    nc.vector.tensor_tensor(yrow[:, k % 4, :], ps[:, 4 + k % 2, 0:P], b2[:, ds(e * D, D)],
                                            ALU.add).then_inc(f["y_copied"], 1)

                e = [None, expert(0, 0)]
                for k in range(1, ROUND):
                    hidden(0, k - 1, k - 1 < 2, e[-1])
                    if k >= 2:
                        result(0, k - 2, k - 2 < 4, e[-2])
                    e.append(expert(0, k))
                with dve.Fori(0, (ROUNDS - 1) // 2) as pair:
                    e = [expert(2 * pair, ROUND - 2), expert(2 * pair, ROUND - 1)]
                    for i in (2 * pair + 1, 2 * pair + 2):
                        for k in range(ROUND):
                            hidden(i - (k < 1), (k - 1) % ROUND, False, e[-1])
                            result(i - (k < 2), (k - 2) % ROUND, False, e[-2])
                            if len(e) < 2 * ROUND + 1:
                                e.append(expert(i, k))
                end = ROUNDS - 1
                e = [expert(end, ROUND - 2), expert(end, ROUND - 1)]
                hidden(end, ROUND - 1, False, e[1])
                result(end, ROUND - 2, False, e[0])
                result(end, ROUND - 1, False, e[1])

            dve.wait_ge(first["const"], 4 * 16)
            start = Chain(dve, last["dve"], 2)
            start.round(0)
            start.link(nc.vector.tensor_copy(ids[:], const[:, C_IDS:C_IDS + NT * TOPK * 2]))
            attention("a")
            dve.wait_ge(first["ready"], 8 * 16)
            dve.wait_ge(first["weights"], 7 * 16)
            start.link(nc.vector.reciprocal(inv_curv[:], curv[:]))
            experts(0)
            attention("b")
            experts(1)
            final = Chain(dve, last["final_step"], 3 * B)
            final.round(0)
            for b in range(B):
                dve.wait_ge(last_loaded[b], LAYERS * ROUNDS * 16 + TOPK * 16)
                for _ in add_rows(last_rows[:, b], b, final, last["combined"]):
                    pass
            final.end()

        @block.tensor
        def _(pe):
            for ph in "ab":
                pe.sem_inc(att[ph]["pv_ready"], 4)

            def score_unit(ph, b, odd, half, i):
                s = att[ph]
                base = SCORES[ph] * (2 * b + half)
                if i == 0:
                    pe.wait_ge(s["stacked"][half], STACKED * (b + 1))
                if i == len(UNITS[ph]):
                    pe.wait_ge(s["max_done"], base + i + 1)
                    nc.tensor.transpose(ps[0:32, i % BANKS, 0:P], negmax[:, half, :], ident).then_inc(s["scores_ready"], 1)
                    return
                g, q, h0, nh = UNITS[ph][i]
                g += 2 * half
                w = (q + 1) * P if ph == "a" else S
                pe.wait_ge(s["max_done"], base + max(i - BANKS + 1, 0) + 1)
                for h in range(h0, h0 + nh):
                    o = (h - h0) * w
                    mm = nc.tensor.matmul(ps[:, i % BANKS, o:o + w], qstacks[odd][:, first_tile(g) + h, q * P:(q + 1) * P],
                                          kstacks[odd][:, first_head(g) + h, 0:w], start=True, stop=ph == "b")
                    if ph == "a":
                        mm = nc.tensor.matmul(ps[:, i % BANKS, o + w - P:o + w], ident_bf, mask_s,
                                              start=False, stop=True)
                mm.then_inc(s["scores_ready"], 1)

            def prob_unit(ph, b, odd, half, i):
                s = att[ph]
                quad, h = divmod(i, 4)
                g, kt = divmod(quad, NT)
                g += 2 * half
                q0 = first_query(ph, kt)
                if i == 0:
                    pe.wait_ge(s["maxrows"][half], 3 * 16 * (b + 1))
                pe.wait_ge(s["exp_done"], EXPS * (2 * b + half) + max(i - BANKS + 1, 0) + 1)
                st = ps[:, BANKS + i % BANKS, :]
                mm = nc.tensor.matmul(st[:, 0:S - q0], kstacks[odd][:, first_head(g) + h, kt * P:(kt + 1) * P],
                                      qstacks[odd][:, first_tile(g) + h, q0:S], start=True, stop=ph == "b")
                if ph == "a":
                    mm = nc.tensor.matmul(st[:, 0:P], ident_bf, mask_t, start=False, stop=True)
                mm.then_inc(s["exp_in"], 1)

            def weighted_sum(ph, b, quad):
                s = att[ph]
                g, kt = divmod(quad, NT)
                q0 = first_query(ph, kt)
                pe.wait_ge(s["exp_done"], 2 * EXPS * b + 4 * quad + 4 + 1)
                if kt == 0:
                    pe.wait_ge(s["o_copied"], GROUPS * b + g + 1)
                    pe.wait_ge(s["v_spread"], 2 * b + g // 2 + 1 + 2)
                for h in range(4):
                    mm = nc.tensor.matmul(outT[32 * h:32 * h + 16, q0:S], vones[:, kt, first_head(g) + h, :],
                                          probs[:, quad % 4, h, 0:S - q0],
                                          start=kt == 0, stop=kt == NT - 1)
                mm.then_inc(s["pv_ready"], 1)

            def side(ph, name, b):
                nonlocal misc_read
                s = att[ph]
                i = int(name[-1]) if name[-1] in "01234" else 0

                def misc_is_read():
                    if misc_read:
                        pe.wait_ge(*misc_read)

                c = b - 1
                if name[:2] == "oT":
                    if i == 0:
                        pe.wait_ge(s["o_copied"], GROUPS * c + GROUPS + 1)
                    misc_is_read()
                    for g in range(GROUPS):
                        mm = nc.tensor.transpose(misc[:, g * P:(g + 1) * P], oT[:, g, i * P:(i + 1) * P], ident)
                    mm.then_inc(s["oT_ready"], 1)
                    misc_read = s["onorm_ready"], NT * c + i + 1
                if name == "onormT":
                    misc_is_read()
                    for t in range(NT):
                        mm = nc.tensor.transpose(misc[:, t * P:(t + 1) * P], onorm[:, t, :], ident)
                    mm.then_inc(s["onormT_ready"], 1)
                    misc_read = s["onormT_copied"], c + 1
                if name == "oproj":
                    misc_is_read()
                    for t in range(NT):
                        mm = nc.tensor.matmul(misc[:, t * D:(t + 1) * D], onormT[:, t * P:(t + 1) * P],
                                              (wao if ph == "a" else wbo)[:], start=True, stop=True)
                    mm.then_inc(s["oproj_ready"], 1)
                    misc_read = s["post_read"], 3 * c + 1
                if name == "norm2T":
                    misc_is_read()
                    for t in range(NT):
                        pe.wait_ge(s["norm2_ready"], NT * c + t + 1)
                        mm = nc.tensor.transpose(misc[:, t * P:(t + 1) * P], xn2[:, t, :], ident)
                    mm.then_inc(s["norm2T_ready"], 1)
                    misc_read = s["norm2T_copied"], c + 1
                if name == "logits":
                    misc_is_read()
                    for t in range(NT):
                        mm = nc.tensor.matmul(misc[:, t * E:(t + 1) * E], xn2T[:, t * P:(t + 1) * P], router[:],
                                              start=True, stop=True)
                    mm.then_inc(s["logits_ready"], 1)
                    misc_read = s["post_read"], 3 * c + 2
                if name == "rank":
                    misc_is_read()
                    pe.wait_ge(s["tops_ready"], c + 1)
                    for t in range(NT + 1):
                        for u in range(min(t + 1, NT)):
                            mm = nc.tensor.matmul(misc[:, t * E:(t + 1) * E], before if u == t else ones_bf,
                                                  tops_bf[:, u, :], start=u == 0, stop=u == min(t, NT - 1))
                    mm.then_inc(s["rank_ready"], 1)
                    misc_read = s["post_read"], 3 * c + 3

                c = b + 1
                if name == "vproj":
                    misc_is_read()
                    for t in range(NT):
                        mm = nc.tensor.matmul(misc[:, t * D:(t + 1) * D], xnT[:, t * P:(t + 1) * P],
                                              wa[:, 4, :] if ph == "a" else wb[:, 2 * D:3 * D],
                                              start=True, stop=True)
                    mm.then_inc(s["v_ready"], 1)
                    misc_read = s["v_staged"], c + 1

                c = b + 2
                if name == "normT":
                    misc_is_read()
                    for t in range(NT):
                        pe.wait_ge(s["norm_ready"], NT * c + t + 1)
                        mm = nc.tensor.transpose(misc[:, t * P:(t + 1) * P], xn[:, t, :], ident)
                    mm.then_inc(s["normT_ready"], 1)
                    misc_read = s["normT_copied"], c + 1
                if name[:4] == "proj" and ph == "a":
                    misc_is_read()
                    nc.tensor.matmul(misc, wa[:, i, :], xnT[:], start=True, stop=True).then_inc(s["proj_ready"], 1)
                    misc_read = s["proj_read"], 4 * c + i + 1
                if name[:4] == "proj" and ph == "b":
                    misc_is_read()
                    for t in range(2):
                        mm = nc.tensor.matmul(misc[:, t * 2 * D:(t + 1) * 2 * D],
                                              xnT[:, (2 * i + t) * P:(2 * i + t + 1) * P], wb[:, 0:2 * D],
                                              start=True, stop=True)
                    mm.then_inc(s["proj_ready"], 1)
                    misc_read = s["proj_read"], 2 * c + i + 1
                c = b + 1
                if name[:4] == "hypT":
                    if i == 0:
                        pe.wait_ge(s["hyp_ready"], c + 1)
                        pe.wait_ge(s["time_ready"], c + 1)
                    misc_is_read()
                    for t in range(NT):
                        m = 8 * t + 2 * i
                        mm = nc.tensor.transpose(misc[0:72, t * P:(t + 1) * P],
                                                 hyp[:, m:m + 2, :].rearrange("p m r -> p (m r)"), ident)
                    mm.then_inc(s["hypT_ready"], 1)
                    misc_read = s["hypT_copied"], 4 * c + i + 1

            misc_read = None

            def part(ph, b, odd, half, prev, sequence):
                for kind, i in sequence:
                    if kind == "e":
                        prob_unit(ph, b, odd, half, i)
                        if i == 2 and (half or prev):
                            weighted_sum(ph, b if half else b - 1, QUADS - 1 if half else 2 * QUADS - 1)
                        elif i % 4 == 2 and i > 2:
                            weighted_sum(ph, b, QUADS * half + i // 4 - 1)
                    if kind == "s":
                        score_unit(ph, b + half, odd ^ half, 1 - half, i)
                    if kind == "side":
                        side(ph, i, b)

            def batch(ph, b, odd, prev, nxt, nxt2):
                nonlocal misc_read
                s = att[ph]
                if not nxt:
                    misc_read = s["post_read"], 3 * (b - 1)
                elif ph == "a":
                    misc_read = s["proj_read"], 4 * (b + 2)
                else:
                    misc_read = s["proj_read"], 2 * (b + 2)
                part(ph, b, odd, 0, prev, first_order(ph, prev, nxt))
                part(ph, b, odd, 1, True, second_order(ph, prev, nxt, nxt2))

            def attention(ph):
                for name in PREP[ph]:
                    side(ph, name, -2)
                for name in PREP_END[ph]:
                    side(ph, name, -1)
                side(ph, "vproj", -1)
                pe.wait_ge(first["ready"], 8 * 16)
                part(ph, -1, 1, 1, False, second_order(ph, False, True, True, e=False))
                run_batches(pe, ph, batch)
                weighted_sum(ph, B - 1, 2 * QUADS - 1)
                for name in POST + ["rank"]:
                    side(ph, name, B)

            def experts(n):
                r0 = n * ROUNDS
                pe.wait_ge(f["table"], n + 1)
                pe.wait_ge(swapped, 2 * 16 * (n + 1))

                def rows(i, k):
                    pe.wait_ge(f["gathered"][k % 4], 16 * (2 * (i + r0) + k // 4 + 1))
                    nc.tensor.transpose(misc[:, 0:P], xg[:, k % 4, :], ident).then_inc(f["xT_ready"], 1)

                def expert(i, k):
                    return pe.value_load(tile_tab[0:1, 0, ds(ROUND * i + k, 1)], min_val=0, max_val=E - 1)

                def up(i, k, e):
                    pe.wait_ge(f["xT_copied"], ROUND * (i + r0) + k + 1)
                    nc.tensor.matmul(ps[:, k % 2, :], xgT[:, k % 2, :], w1[:, ds(e * FF, FF)],
                                     start=True, stop=True).then_inc(f["h_ready"], 1)

                def turn(i, k):
                    pe.wait_ge(f["h_copied"], ROUND * (i + r0) + k + 1)
                    for j in range(NF):
                        mm = nc.tensor.transpose(ps[:, 2 + k % 2, j * P:(j + 1) * P],
                                                 hid[:, k % 2, j * P:(j + 1) * P], ident)
                    mm.then_inc(f["hT_ready"], 1)

                def down(i, k, start, e):
                    pe.wait_ge(f["hT_copied"], ROUND * (i + r0) + k + 1)
                    if not start:
                        pe.wait_ge(f["y_copied"], ROUND * (i + r0) + k - 1)
                    for j in range(NF):
                        mm = nc.tensor.matmul(ps[:, 4 + k % 2, 0:P], hidT[:, k % 2, j, :], w2[:, ds(e * FF + j * P, P)],
                                              start=j == 0, stop=j == NF - 1)
                    mm.then_inc(f["y_ready"], 1)

                rows(0, 0)
                e = [None, expert(0, 0)]
                for k in range(1, ROUND):
                    up(0, k - 1, e[-1])
                    if k >= 2:
                        down(0, k - 2, k - 2 < 2, e[-2])
                    e.append(expert(0, k))
                    rows(0, k)
                    turn(0, k - 1)
                with pe.Fori(0, (ROUNDS - 1) // 2) as pair:
                    e = [expert(2 * pair, ROUND - 2), expert(2 * pair, ROUND - 1)]
                    for i in (2 * pair + 1, 2 * pair + 2):
                        for k in range(ROUND):
                            up(i - (k < 1), (k - 1) % ROUND, e[-1])
                            down(i - (k < 2), (k - 2) % ROUND, False, e[-2])
                            if len(e) < 2 * ROUND + 1:
                                e.append(expert(i, k))
                            rows(i, k)
                            turn(i - (k < 1), (k - 1) % ROUND)
                end = ROUNDS - 1
                e = [expert(end, ROUND - 2), expert(end, ROUND - 1)]
                up(end, ROUND - 1, e[1])
                down(end, ROUND - 2, False, e[0])
                turn(end, ROUND - 1)
                down(end, ROUND - 1, False, e[1])

            pe.wait_ge(first["const"], 4 * 16)
            attention("a")
            pe.wait_ge(first["weights"], 7 * 16)
            experts(0)
            attention("b")
            experts(1)


def constants():
    c = np.zeros((P, C_END), np.float32)
    c[:, C_IDENT:C_IDENT + P] = np.eye(P)
    freq = np.float32(10000.0) ** (-2.0 * np.arange(0, HD // 2, dtype=np.float32) / HD)
    angle = np.arange(S, dtype=np.float32)[None, :] * freq.astype(np.float32)[:, None]
    dim = (np.arange(P) % 32) // 4
    c[:, C_COS:C_COS + S] = np.cos(angle)[dim // 2]
    c[:, C_SIN:C_SIN + S] = np.sin(angle)[dim // 2] * np.where(dim % 2 == 0, -1, 1)[:, None]
    c[:, C_PICK:C_PICK + NT * E] = np.tile(E - np.arange(E), NT)
    c[:, C_BASE:C_BASE + NT * E] = np.tile(LIST * np.arange(E), NT)
    p, t, k, w = np.meshgrid(np.arange(P), np.arange(NT), np.arange(TOPK), np.arange(2), indexing="ij")
    c[:, C_IDS:] = (t * P + p + w * k * TOK).reshape(P, -1)
    r = np.arange(P)
    masked = np.where(r[None, :] > r[:, None], MASKED, 0)
    bf = np.stack([np.eye(P), masked, masked.T, r[:, None] < r[None, :], np.ones((P, P))], 1)
    tilepos = np.repeat(P * np.arange(TILES), E).reshape(1, TILES, E)
    return c, bf.astype(mybir.dt.np(BF16)), tilepos.astype(np.float32)


def kernel(**inputs):
    import concourse.bacc as bacc
    from concourse.bass_utils import run_bass_kernel_spmd

    v = {k: np.asarray(w) for k, w in inputs.items()}
    A, Bp, Fp = "L0_attn_a_", "L0_attn_b_", "L0_ffn_"
    par, half, dim, pair = np.meshgrid(np.arange(2), np.arange(2), np.arange(HD), np.arange(4), indexing="ij")
    rows = (HD * (8 * par + 4 * half + pair) + dim).reshape(-1)
    swapped = (HD * (8 * par + 4 * half + pair) + (dim ^ 1)).reshape(-1)
    grouped = np.concatenate([HD * (8 * (g % 2) + 4 * (g // 2)) + np.arange(4 * HD) for g in range(GROUPS)])
    wq, wk, wv = (v[A + n].T for n in ("W_q", "W_k", "W_v"))
    consts, consts_bf, tilepos = constants()
    arrays = {
        "x": v[A + "x"].reshape(TOK, D),
        "consts": consts, "consts_bf": consts_bf, "tilepos": tilepos,
        "wa": np.stack([wq[:, rows], wq[:, swapped], wk[:, rows], wk[:, swapped], wv], 1),
        "wao": v[A + "W_o"].T[grouped],
        "wb": np.concatenate([v[Bp + n].T for n in ("wq_w", "wk_w", "wv_w")], 1),
        "wbo": v[Bp + "wo_w"].T[grouped],
        "bias_qkv": np.concatenate([v[Bp + n] for n in ("wq_b", "wk_b", "wv_b")]),
        "bias_o": v[Bp + "wo_b"],
        "curv": v[Bp + "curv"].reshape(1),
        "router": v[Fp + "router_w"].T,
        "w1": v[Fp + "w1"].transpose(2, 0, 1).reshape(D, E * FF),
        "b1": v[Fp + "b1"].reshape(-1),
        "w2": v[Fp + "w2"].transpose(2, 0, 1).reshape(NF, P, E, D).transpose(1, 2, 0, 3).reshape(P, E * FF),
        "b2": v[Fp + "b2"].reshape(-1),
    }
    arrays = {k: np.ascontiguousarray(w) for k, w in arrays.items()}
    nc = bacc.Bacc("TRN2", target_bir_lowering=False, num_devices=1)
    aps = {k: nc.dram_tensor("in_" + k, w.shape, mybir.dt.from_np(w.dtype), kind="ExternalInput").ap()
           for k, w in arrays.items()}
    out = nc.dram_tensor("out", (TOK, D), F32, kind="ExternalOutput").ap()
    build_program(nc, aps, out)
    r = run_bass_kernel_spmd(nc, [{"in_" + k: w for k, w in arrays.items()}], core_ids=[0])
    return r.results[0]["out"].reshape(B, S, D)
```
